# Optimizing a Trainium2 kernel written in Bass

```python
import numpy as np
import jax
import jax.numpy as jnp

def _softmax(x, axis=-1):
    return jax.nn.softmax(x, axis=axis)

def _gelu(x):
    return jax.nn.gelu(x, approximate=True)

def _silu(x):
    return jax.nn.silu(x)

def _sigmoid(x):
    return jax.nn.sigmoid(x)

def _layernorm(x, axis=-1, eps=1e-05):
    m = jnp.mean(x, axis=axis, keepdims=True)
    v = jnp.var(x, axis=axis, keepdims=True)
    return (x - m) / jnp.sqrt(v + eps)

def _scatter_add(tgt, idx, src, axis=0):
    return tgt.at[idx].add(src)

def _segment_sum(src, seg, n):
    return jax.ops.segment_sum(src, seg, n)
kernel_name = 'mk_early_fusion_d1_tok_img768_r4_143f18'

def setup_inputs(seed: int=0):
    np.random.seed(seed)
    _w = jnp.asarray

    def _rec_inputs():
        import jax
        import jax.numpy as jnp
        _rk = jax.random.key(seed)
        x = -0.00016672 + 0.999947 * jax.random.normal(jax.random.fold_in(_rk, 1), (64, 96, 96, 3), jnp.float32)
        txt = 0.000359596 + 1.00025 * jax.random.normal(jax.random.fold_in(_rk, 2), (64, 128, 192), jnp.float32)
        return (x, txt)
    x, txt = _rec_inputs()

    def _L0_tok_setup():
        import jax, jax.numpy as jnp
        import numpy as np
        PATCH = 16
        HIDDEN = 192

        def extract_patches(x, p):
            B, H, W, C = x.shape
            Hp, Wp = (H // p, W // p)
            x = x.reshape(B, Hp, p, Wp, p, C)
            x = x.transpose(0, 1, 3, 2, 4, 5)
            return x.reshape(B, Hp * Wp, p * p * C)
        key = jax.random.key(seed)
        k1, k2, k3, k4, k5 = jax.random.split(key, 5)
        B, H, W, C = (64, 96, 96, 3)
        num_patches = (H // PATCH) ** 2
        patch_dim = PATCH * PATCH * C
        contactMap = jax.random.normal(k1, (B, H, W, C), dtype=jnp.float32)
        W_proj = jax.random.normal(k2, (patch_dim, HIDDEN), dtype=jnp.float32) * (1.0 / np.sqrt(patch_dim))
        b_proj = jnp.zeros((HIDDEN,), dtype=jnp.float32)
        cls_token = jax.random.normal(k3, (1, 1, HIDDEN), dtype=jnp.float32) * 0.05
        pos_embedding = jax.random.normal(k4, (num_patches + 1, HIDDEN), dtype=jnp.float32) * 0.05
        return {'contactMap': contactMap, 'W_proj': W_proj, 'b_proj': b_proj, 'cls_token': cls_token, 'pos_embedding': pos_embedding}
    _L0_tok_all = _L0_tok_setup()
    _L0_tok_in = {k: v for k, v in _L0_tok_all.items() if k in ('W_proj', 'b_proj', 'cls_token', 'pos_embedding')}
    del _L0_tok_all

    def _L0_attn_setup():
        import jax, jax.numpy as jnp
        import numpy as np
        NB_HEADS = 12
        key = jax.random.key(seed)
        ks = jax.random.split(key, 6)
        B, S, D, H = (4, 256, 192, NB_HEADS)
        x = jax.random.normal(ks[0], (B, S, D), dtype=jnp.float32)
        Wqkv = jax.random.normal(ks[1], (D, 3 * D), dtype=jnp.float32) * 0.02
        bqkv = jnp.zeros((3 * D,), dtype=jnp.float32)
        Wl = jax.random.normal(ks[2], (H, H), dtype=jnp.float32) * 0.3
        bl = jnp.zeros((H,), dtype=jnp.float32)
        Ww = jax.random.normal(ks[3], (H, H), dtype=jnp.float32) * 0.3
        bw = jnp.zeros((H,), dtype=jnp.float32)
        Wproj = jax.random.normal(ks[4], (D, D), dtype=jnp.float32) * 0.02
        bproj = jnp.zeros((D,), dtype=jnp.float32)
        return {'x': x, 'Wqkv': Wqkv, 'bqkv': bqkv, 'Wl': Wl, 'bl': bl, 'Ww': Ww, 'bw': bw, 'Wproj': Wproj, 'bproj': bproj}
    _L0_attn_all = _L0_attn_setup()
    _L0_attn_in = {k: v for k, v in _L0_attn_all.items() if k in ('Wqkv', 'bqkv', 'Wl', 'bl', 'Ww', 'bw', 'Wproj', 'bproj')}
    del _L0_attn_all

    def _L0_ffn_setup():
        import jax, jax.numpy as jnp
        import numpy as np
        B, S, H, I = (4, 512, 192, 384)
        E, K = (3, 2)
        INIT = 0.02

        def _expert(x, gw, uw, dw):
            return jax.nn.silu(x @ gw) * (x @ uw) @ dw
        key = jax.random.key(seed)
        ks = jax.random.split(key, 8)
        f32 = jnp.float32
        return {'x': jax.random.normal(ks[0], (B, S, H), f32), 'shared_gate': jax.random.normal(ks[1], (H, I), f32) * INIT, 'shared_up': jax.random.normal(ks[2], (H, I), f32) * INIT, 'shared_down': jax.random.normal(ks[3], (I, H), f32) * INIT, 'routed_gate': jax.random.normal(ks[4], (E, H, I), f32) * INIT, 'routed_up': jax.random.normal(ks[5], (E, H, I), f32) * INIT, 'routed_down': jax.random.normal(ks[6], (E, I, H), f32) * INIT, 'router_w': jax.random.normal(ks[7], (H, E), f32) * INIT, 'routing_bias': jnp.zeros((E,), f32)}
    _L0_ffn_all = _L0_ffn_setup()
    _L0_ffn_in = {k: v for k, v in _L0_ffn_all.items() if k in ('shared_gate', 'shared_up', 'shared_down', 'routed_gate', 'routed_up', 'routed_down', 'router_w', 'routing_bias')}
    del _L0_ffn_all
    return {'x': x, 'txt': txt, 'L0_tok_W_proj': _L0_tok_in['W_proj'], 'L0_tok_b_proj': _L0_tok_in['b_proj'], 'L0_tok_cls_token': _L0_tok_in['cls_token'], 'L0_tok_pos_embedding': _L0_tok_in['pos_embedding'], 'L0_attn_Wqkv': _L0_attn_in['Wqkv'], 'L0_attn_bqkv': _L0_attn_in['bqkv'], 'L0_attn_Wl': _L0_attn_in['Wl'], 'L0_attn_bl': _L0_attn_in['bl'], 'L0_attn_Ww': _L0_attn_in['Ww'], 'L0_attn_bw': _L0_attn_in['bw'], 'L0_attn_Wproj': _L0_attn_in['Wproj'], 'L0_attn_bproj': _L0_attn_in['bproj'], 'L0_ffn_shared_gate': _L0_ffn_in['shared_gate'], 'L0_ffn_shared_up': _L0_ffn_in['shared_up'], 'L0_ffn_shared_down': _L0_ffn_in['shared_down'], 'L0_ffn_routed_gate': _L0_ffn_in['routed_gate'], 'L0_ffn_routed_up': _L0_ffn_in['routed_up'], 'L0_ffn_routed_down': _L0_ffn_in['routed_down'], 'L0_ffn_router_w': _L0_ffn_in['router_w'], 'L0_ffn_routing_bias': _L0_ffn_in['routing_bias']}

def reference(x, txt, L0_tok_W_proj, L0_tok_b_proj, L0_tok_cls_token, L0_tok_pos_embedding, L0_attn_Wqkv, L0_attn_bqkv, L0_attn_Wl, L0_attn_bl, L0_attn_Ww, L0_attn_bw, L0_attn_Wproj, L0_attn_bproj, L0_ffn_shared_gate, L0_ffn_shared_up, L0_ffn_shared_down, L0_ffn_routed_gate, L0_ffn_routed_up, L0_ffn_routed_down, L0_ffn_router_w, L0_ffn_routing_bias):
    import jax
    import jax.numpy as jnp

    def _L0_tok_ref(contactMap, W_proj, b_proj, cls_token, pos_embedding):
        import jax, jax.numpy as jnp
        import numpy as np
        PATCH = 16
        HIDDEN = 192

        def extract_patches(x, p):
            B, H, W, C = x.shape
            Hp, Wp = (H // p, W // p)
            x = x.reshape(B, Hp, p, Wp, p, C)
            x = x.transpose(0, 1, 3, 2, 4, 5)
            return x.reshape(B, Hp * Wp, p * p * C)
        B = contactMap.shape[0]
        patches = extract_patches(contactMap, PATCH)
        enc = jnp.einsum('bnd,dh->bnh', patches, W_proj) + b_proj
        cls = jnp.broadcast_to(cls_token.astype(contactMap.dtype), (B, 1, enc.shape[-1]))
        enc = jnp.concatenate([cls, enc], axis=1)
        return enc + pos_embedding

    def _L0_attn_ref(x, Wqkv, bqkv, Wl, bl, Ww, bw, Wproj, bproj):
        import jax, jax.numpy as jnp
        import numpy as np
        NB_HEADS = 12
        B, S, D = x.shape
        H = NB_HEADS
        dh = D // H
        scale = dh ** (-0.5)
        qkv = (x @ Wqkv + bqkv).reshape(B, S, 3, H, dh).transpose(2, 0, 3, 1, 4)
        q, k, v = (qkv[0] * scale, qkv[1], qkv[2])
        attn = jnp.einsum('bhqd,bhkd->bhqk', q, k)
        attn = jnp.einsum('bhqk,hg->bgqk', attn, Wl) + bl[None, :, None, None]
        attn = jax.nn.softmax(attn, axis=-1)
        attn = jnp.einsum('bhqk,hg->bgqk', attn, Ww) + bw[None, :, None, None]
        out = jnp.einsum('bhqk,bhkd->bqhd', attn, v).reshape(B, S, D)
        return out @ Wproj + bproj

    def _L0_ffn_ref(x, shared_gate, shared_up, shared_down, routed_gate, routed_up, routed_down, router_w, routing_bias):
        import jax, jax.numpy as jnp
        import numpy as np
        B, S, H, I = (4, 512, 192, 384)
        E, K = (3, 2)
        INIT = 0.02

        def _expert(x, gw, uw, dw):
            return jax.nn.silu(x @ gw) * (x @ uw) @ dw
        shared_out = _expert(x, shared_gate, shared_up, shared_down)
        routing_probs = jax.nn.sigmoid(x @ router_w + routing_bias)
        scores, indices = jax.lax.top_k(routing_probs, K)
        scores = scores / scores.sum(axis=-1, keepdims=True)
        combine_w = (jax.nn.one_hot(indices, E, dtype=x.dtype) * scores[..., None]).sum(axis=-2)
        g = jnp.einsum('bsh,ehi->ebsi', x, routed_gate)
        u = jnp.einsum('bsh,ehi->ebsi', x, routed_up)
        h = jax.nn.silu(g) * u
        out_e = jnp.einsum('ebsi,eih->ebsh', h, routed_down)
        combined = jnp.einsum('ebsh,bse->bsh', out_e, combine_w)
        return shared_out + combined
    h = _L0_tok_ref(x, L0_tok_W_proj, L0_tok_b_proj, L0_tok_cls_token, L0_tok_pos_embedding)
    h = jnp.concatenate([h, txt], axis=1)
    h = h + _L0_attn_ref(_layernorm(h, axis=-1), L0_attn_Wqkv, L0_attn_bqkv, L0_attn_Wl, L0_attn_bl, L0_attn_Ww, L0_attn_bw, L0_attn_Wproj, L0_attn_bproj)
    h = h + _L0_ffn_ref(_layernorm(h, axis=-1), L0_ffn_shared_gate, L0_ffn_shared_up, L0_ffn_shared_down, L0_ffn_routed_gate, L0_ffn_routed_up, L0_ffn_routed_down, L0_ffn_router_w, L0_ffn_routing_bias)
    return h

_drawn_inputs = setup_inputs


def setup_inputs(seed=0):
    import zlib

    import numpy as np

    out = dict(_drawn_inputs(seed))
    spreads = {'L0_tok_b_proj': (0.0, 0.1),
     'L0_attn_bqkv': (0.0, 0.1),
     'L0_attn_bl': (0.0, 0.8),
     'L0_attn_bw': (0.0, 0.1),
     'L0_attn_bproj': (0.0, 0.1),
     'L0_ffn_routing_bias': (0.0, 0.8)}
    factors = {'L0_tok_cls_token': 8.0,
     'L0_tok_pos_embedding': 2.682,
     'L0_attn_Wl': 8.0,
     'L0_ffn_shared_gate': 4.305,
     'L0_ffn_shared_up': 4.216,
     'L0_ffn_shared_down': 4.172,
     'L0_ffn_routed_gate': 6.093,
     'L0_ffn_routed_up': 6.071,
     'L0_ffn_routed_down': 6.089,
     'L0_ffn_router_w': 8.0}
    for name, (base, spread) in spreads.items():
        noise = np.random.default_rng([zlib.crc32(name.encode()), seed]).standard_normal(out[name].shape)
        drawn = base * np.exp(spread * noise) if base else spread * noise
        out[name] = jnp.asarray(drawn.astype(out[name].dtype))
    for name, factor in factors.items():
        out[name] = (out[name] * factor).astype(out[name].dtype)
    return out
```

```python
import concourse.bass as bass
from concourse import mybir
from contextlib import ExitStack

F32 = mybir.dt.float32
F32R = mybir.dt.float32r
ACT = mybir.ActivationFunctionType
ALU = mybir.AluOpType
AX_X = mybir.AxisListType.X

B = 64
D = 192
NT = 128
NP = 36
NC = NP + 1
S = NT + NC
SE = S + 1
H = 12
DH = D // H
DM = 128
DR = D - DM
QS = 10
HQ = H * QS
TILES = -(-S // QS)
SQ = TILES * QS
GROUP = 3
GROUPS = -(-TILES // GROUP)
EPS = 1e-5
KD = 768 // 128
EMB = 2 * NP
NW = 16
VW = 128
VZ = H * VW + VW - DH

FT = 384
E = 3
NF = 4 * FT // 128
TP = 120
TT = 4
CH = TP * TT
CHUNKS = B * S // CH


def group_tiles(j):
    return range(j * GROUP, min(TILES, (j + 1) * GROUP))


def wait(eng, sem, value):
    if isinstance(value, int) and value <= 0:
        return
    eng.wait_ge(sem, value)


def f(ap):
    return ap.bitcast(F32)


class Split:

    def __init__(self, sb, name, n):
        self.hi = sb(name + "_hi", [DM, n], F32R)
        self.lo = sb(name + "_lo", [DM, n], F32R)
        self.rest2 = sb(name + "_rest2", [2 * DR, n], F32R)
        self.rest_lo = sb(name + "_rest_lo", [DR, n], F32R)


def product(pe, out, a, b, a_cols, b_cols, moving_weights):
    xh, xl, xr, w = a[0], a[1], a[2], b
    pairs = [(xh[:, a_cols], w.hi[:, b_cols]), (xl[:, a_cols], w.hi[:, b_cols]), (xh[:, a_cols], w.lo[:, b_cols]),
             (xr[:, a_cols], w.rest2[:, b_cols]), (xr[0:DR, a_cols], w.rest_lo[:, b_cols])]
    last = None
    for n, (x, y) in enumerate(pairs):
        lhs, rhs = (x, y) if moving_weights else (y, x)
        last = pe.matmul(out, lhs, rhs, start=(n == 0), stop=(n == len(pairs) - 1))
    return last


def embed_patches(nc, xT, w_proj, pos_rep, b_rep, cls_rep, pos0_rep, h0):
    ctx = ExitStack()
    with ctx:
        def sb(name, shape, dt=F32):
            return ctx.enter_context(nc.sbuf_tensor("em_" + name, shape, dt))

        def sem(name):
            return ctx.enter_context(nc.semaphore("em_" + name))

        ps = [ctx.enter_context(nc.psum_tensor(f"em_ps{n}", [128, 512], F32)) for n in range(2)]
        w = sb("w", [128, KD, D])
        wh, wl = sb("wh", [128, KD, D], F32R), sb("wl", [128, KD, D], F32R)
        x = sb("x", [128, 2, KD * EMB])
        xh, xl = sb("xh", [128, 2, KD * EMB], F32R), sb("xl", [128, 2, KD * EMB], F32R)
        pos, bias, posb = sb("pos", [EMB, D]), sb("bias", [EMB, D]), sb("posb", [EMB, D])
        cls, pos0, cls_row = sb("cls", [B, D]), sb("pos0", [B, D]), sb("cls_row", [B, D])
        out = sb("out", [EMB, 2, D])
        s_const, s_x = sem("const"), [sem("x0"), sem("x1")]
        s_wh, s_wl, s_cls, s_posb = sem("wh"), sem("wl"), sem("cls"), sem("posb")
        s_xh, s_xl, s_mm, s_out = sem("xh"), sem("xl"), sem("mm"), sem("out")
        s_store, s_cls_store = [sem("st0"), sem("st1")], sem("cls_st")
        half = B // 4
        block = ctx.enter_context(nc.Block())

        @block.sync
        def _(sp):
            sp.dma_start(w[:], w_proj.rearrange("(k p) n -> p k n", p=128)).then_inc(s_const, 16)
            for dst, src in ((pos, pos_rep), (bias, b_rep), (cls, cls_rep), (pos0, pos0_rep)):
                sp.dma_start(dst[:], src).then_inc(s_const, 16)
            for u in range(2):
                sp.dma_start(x[:, u, :], xT[u]).then_inc(s_x[u], 16)
            sp.wait_ge(s_cls, 1)
            sp.dma_start(h0[:, 0, :], cls_row[:]).then_inc(s_cls_store, 16)
            def tile(it, u, more):
                if more:
                    sp.wait_ge(s_xl, 2 * it + u + 1)
                    sp.dma_start(x[:, u, :], xT[bass.ds(2 * it + u + 2, 1)].rearrange("a p n -> (a p) n")
                                 ).then_inc(s_x[u], 16)
                sp.wait_ge(s_out, 2 * it + u + 1)
                for k in range(2):
                    sp.dma_start(h0[bass.ds(4 * it + 2 * u + k, 1), 1:NC, :].rearrange("b n d -> (b n) d"),
                                 out[k * NP:(k + 1) * NP, u, :]).then_inc(s_store[u], 16)
            with sp.Fori(0, half - 1) as it:
                for u in range(2):
                    tile(it, u, True)
            for u in range(2):
                tile(half - 1, u, False)
            for u in range(2):
                sp.wait_ge(s_store[u], 32 * half)
            sp.wait_ge(s_cls_store, 16)

        @block.scalar
        def _(act):
            act.wait_ge(s_const, 80)
            act.activation(wh[:], w[:], ACT.Copy).then_inc(s_wh, 1)
            def tile(i, it, u):
                act.wait_ge(s_x[u], 16 * it + 16)
                wait(act, s_mm, i - 1)
                act.activation(xh[:, u, :], x[:, u, :], ACT.Copy).then_inc(s_xh, 1)
            for u in range(2):
                tile(u, 0, u)
            with act.Fori(1, half) as it:
                for u in range(2):
                    tile(2 * it + u, it, u)

        @block.vector
        def _(dve):
            dve.wait_ge(s_const, 80)
            dve.tensor_tensor(cls_row[:], cls[:], pos0[:], ALU.add).then_inc(s_cls, 1)
            dve.tensor_tensor(posb[:], pos[:], bias[:], ALU.add).then_inc(s_posb, 1)
            dve.wait_ge(s_wh, 1)
            dve.tensor_tensor(wl[:], w[:], f(wh[:]), ALU.subtract).then_inc(s_wl, 1)
            dve.wait_ge(s_posb, 1)

            def low(i, u):
                dve.wait_ge(s_xh, i + 1)
                dve.tensor_tensor(xl[:, u, :], x[:, u, :], f(xh[:, u, :]), ALU.subtract).then_inc(s_xl, 1)

            def store(i, it, u):
                dve.wait_ge(s_mm, i + 1)
                wait(dve, s_store[u], 32 * it)
                dve.tensor_tensor(out[:, u, :], ps[u][0:EMB, 0:D], posb[:], ALU.add).then_inc(s_out, 1)
            low(0, 0)
            for i in range(1, 4):
                low(i, i % 2)
                store(i - 1, (i - 1) // 2, (i - 1) % 2)
            with dve.Fori(2, half) as it:
                for u in range(2):
                    low(2 * it + u, u)
                    store(2 * it + u - 1, it - 1 + u, 1 - u)
            store(2 * half - 1, half - 1, 1)

        @block.tensor
        def _(pe):
            pe.wait_ge(s_wl, 1)

            def tile(i, u):
                pe.wait_ge(s_xl, i + 1)
                wait(pe, s_out, i - 1)
                last = None
                for k in range(KD):
                    cols = slice(k * EMB, (k + 1) * EMB)
                    for n, (a, b) in enumerate(((xh, wh), (xl, wh), (xh, wl))):
                        last = pe.matmul(ps[u][0:EMB, 0:D], a[:, u, cols], b[:, k, :], start=(k + n == 0),
                                         stop=(k == KD - 1 and n == 2))
                last.then_inc(s_mm, 1)
            for u in range(2):
                tile(u, u)
            with pe.Fori(1, half) as it:
                for u in range(2):
                    tile(2 * it + u, u)


def attention(nc, txt, h0, h1, wqkv, bqkv, bv_rep, wl_rep, bl_rep, ww_rep, bw_rep, wp, bp_rep, ident_in, mask_in):
    ctx = ExitStack()
    with ctx:
        def sb(name, shape, dt=F32):
            return ctx.enter_context(nc.sbuf_tensor("at_" + name, shape, dt))

        def sem(name):
            return ctx.enter_context(nc.semaphore("at_" + name))

        bank = [ctx.enter_context(nc.psum_tensor(f"at_bank{n}", [128, 512], F32)) for n in range(8)]
        ps_s, ps_m, ps_mr, ps_q, ps_o = bank[0:2], bank[2:4], bank[4:6], bank[6], bank[7]

        NQK = 2 * D
        w_in, w_in_r = sb("w_in", [DM, NQK + 2 * D]), sb("w_in_r", [2 * DR, NQK + 2 * D])
        wqk, wv, wo = Split(sb, "wqk", NQK), Split(sb, "wv", D), Split(sb, "wo", D)
        bq, bk, bqr, bkr = sb("bq", [DM, 1]), sb("bk", [DM, 1]), sb("bqr", [DR, 1]), sb("bkr", [128, 1])
        bv, bp, bl = sb("bv", [128, D]), sb("bp", [128, D]), sb("bl", [HQ, 1])
        wl_in, wl_in_r = sb("wl_in", [DM, H]), sb("wl_in_r", [DR, H])
        wls, wls_r = sb("wls", [DM, H]), sb("wls_r", [DR, H])
        ww, mask, kron = sb("ww", [HQ, H]), sb("mask", [HQ, QS]), sb("kron", [HQ + 1, HQ])
        kron_h, kron_l = sb("kron_h", [HQ + 1, HQ], F32R), sb("kron_l", [HQ + 1, HQ], F32R)
        ident = sb("ident", [128, 128])

        tok = sb("tok", [128, 2, D])
        stats, moments = sb("stats", [128, 2, 6]), sb("moments", [128, 2, 2])
        var_eps, half_neg, rstd = sb("var_eps", [128, 2]), sb("half_neg", [128, 2]), sb("rstd", [128, 2])
        eps = sb("eps", [128, 2])
        xhat = sb("xhat", [128, 2, D])
        x = (sb("x_hi", [DM, SE], F32R), sb("x_lo", [DM, SE], F32R), sb("x_rest", [2 * DR, SE], F32R))
        q, q_r = sb("q", [DM, SQ]), sb("q_r", [DR, SQ])
        k_hi, k_lo = sb("k_hi", [DM, 2, SE], F32R), sb("k_lo", [DM, 2, SE], F32R)
        k_r2, k_rlo = sb("k_r2", [2 * DR, 2, SE], F32R), sb("k_rlo", [DR, 2, SE], F32R)
        qg_hi, qg_lo = sb("qg_hi", [DM, 2, TILES * HQ], F32R), sb("qg_lo", [DM, 2, TILES * HQ], F32R)
        qg_r = sb("qg_r", [2 * DR, 2, TILES * HQ], F32R)
        v = sb("v", [128, 2, 2, D])
        vz_hi, vz_lo = sb("vz_hi", [NT, VZ], F32R), sb("vz_lo", [NT, VZ], F32R)
        vz_r2, vz_rlo = sb("vz_r2", [128, VZ], F32R), sb("vz_rlo", [NC, VZ], F32R)
        neg_max, shift = sb("neg_max", [HQ, 2, GROUP]), sb("shift", [HQ, 2, GROUP])
        total, scale = sb("total", [HQ, 2, GROUP]), sb("scale", [HQ, 2, GROUP])
        ex = sb("ex", [HQ, 2, GROUP, S])
        p_hi, p_lo = sb("p_hi", [128, 2, GROUP, S], F32R), sb("p_lo", [128, 2, GROUP, S], F32R)
        a_hi, a_lo = sb("a_hi", [NT, 2, H * SQ], F32R), sb("a_lo", [NT, 2, H * SQ], F32R)
        a_r = sb("a_r", [128, 2, H * SQ], F32R)
        o = (sb("o_hi", [DM, SE], F32R), sb("o_lo", [DM, SE], F32R), sb("o_rest", [2 * DR, SE], F32R))
        res, resb, hout = sb("res", [128, 2, D]), sb("resb", [128, 2, D]), sb("hout", [128, 2, D])

        s_const, s_zero, s_whi, s_wlo, s_prep = (sem(n) for n in ("const", "zero", "whi", "wlo", "prep"))
        s_tok, s_res, s_store = sem("tok"), sem("res"), sem("store")
        s_stats, s_mom, s_veps, s_rstd, s_xhat = (sem(n) for n in ("stats", "mom", "veps", "rstd", "xhat"))
        s_t, s_xhi, s_xlo = sem("t"), sem("xhi"), sem("xlo")
        s_qk, s_kev, s_q, s_vmm, s_v, s_vz, s_vzc = (sem(n) for n in ("qk", "kev", "q", "vmm", "v", "vz", "vzc"))
        s_qgh, s_qgr, s_qgl = sem("qgh"), sem("qgr"), sem("qgl")
        s_s, s_max, s_shift, s_exp, s_scale, s_phi, s_plo = (
            sem(n) for n in ("s", "max", "shift", "exp", "scale", "phi", "plo"))
        s_m, s_ahi, s_alo, s_av, s_ohi, s_olo, s_pr, s_resb, s_h1 = (
            sem(n) for n in ("m", "ahi", "alo", "av", "ohi", "olo", "pr", "resb", "h1"))

        def has(i):
            return not isinstance(i, int) or 0 <= i < B

        def par(u):
            return u % 2

        def win(t, a, b):
            return t[a:b, VW - DH:].rearrange("p (g w) -> p g w", w=VW)[:, :, 0:DH]

        def heads(ap, g):
            return ap.rearrange("p (t g s) -> p t g s", g=H, s=QS)[:, :, g, :]

        def mixed(ap, j):
            ts = group_tiles(j)
            return ap.rearrange("p (g t s) -> p t g s", g=H, s=QS)[:, ts[0]:ts[-1] + 1, :, :]

        def mix_bank(t, j, rows):
            n = len(group_tiles(j))
            return t[0:rows, 0:n * HQ].rearrange("p (t g s) -> p t g s", g=H, s=QS)

        def steps(eng, step):
            for i in range(-2, 4):
                step(i, i % 2)
            with eng.Fori(2, (B - 2) // 2) as it:
                for u in range(2):
                    step(2 * it + u, u)
            for i in range(B - 2, B + 2):
                step(i, i % 2)

        block = ctx.enter_context(nc.Block())

        @block.sync
        def _(sp):
            with nc.allow_non_contiguous_dma("weights are loaded once"):
                for lo, n, at in ((0, DM, 0), (D, DM, DM), (DM, DR, 2 * DM), (D + DM, DR, 2 * DM + DR), (2 * D, D, NQK)):
                    sp.dma_start(w_in[:, at:at + n], wqkv[0:DM, lo:lo + n]).then_inc(s_const, 16)
                    for r in range(2):
                        sp.dma_start(w_in_r[r * DR:(r + 1) * DR, at:at + n], wqkv[DM:D, lo:lo + n]).then_inc(s_const, 16)
                sp.dma_start(w_in[:, NQK + D:], wp[0:DM, :]).then_inc(s_const, 16)
                for r in range(2):
                    sp.dma_start(w_in_r[r * DR:(r + 1) * DR, NQK + D:], wp[DM:D, :]).then_inc(s_const, 16)
                for dst, lo, n in ((bq[:], 0, DM), (bqr[:], DM, DR), (bk[:], D, DM), (bkr[DR:, :], D + DM, DR)):
                    sp.dma_start(dst, bqkv[lo:lo + n].rearrange("(n a) -> n a", a=1)).then_inc(s_const, 16)
                for dst, src in ((bv, bv_rep), (bp, bp_rep), (bl, bl_rep), (wl_in, wl_rep[0:DM, :]),
                                 (wl_in_r, wl_rep[DM:D, :]), (ww, ww_rep), (mask, mask_in), (ident, ident_in)):
                    sp.dma_start(dst[:], src).then_inc(s_const, 16)
                sp.dma_start(kron[HQ:HQ + 1, :], bw_rep).then_inc(s_const, 16)

            def step(i, u):
                if has(i + 2):
                    wait(sp, s_xhat, 2 * (i + 2))
                    sp.dma_start(tok[:, 0, :], txt[bass.ds(i + 2, 1)].rearrange("a t d -> (a t) d")).then_inc(s_tok, 16)
                    sp.dma_start(tok[0:NC, 1, :], h0[bass.ds(i + 2, 1)].rearrange("a t d -> (a t) d")
                                 ).then_inc(s_tok, 16)
                if has(i - 2):
                    wait(sp, s_resb, 2 * (i - 2))
                    sp.dma_start(res[:, 0, :], txt[bass.ds(i - 2, 1)].rearrange("a t d -> (a t) d")).then_inc(s_res, 16)
                    sp.dma_start(res[0:NC, 1, :], h0[bass.ds(i - 2, 1)].rearrange("a t d -> (a t) d")
                                 ).then_inc(s_res, 16)
                if has(i - 3):
                    out_image(i - 3)

            def out_image(i):
                sp.wait_ge(s_h1, 2 * i + 2)
                row = h1[bass.ds(i, 1)].rearrange("a t d -> (a t) d")
                sp.dma_start(row[NC:S, :], hout[:, 0, :]).then_inc(s_store, 16)
                sp.dma_start(row[0:NC, :], hout[0:NC, 1, :]).then_inc(s_store, 16)

            for i in range(-2, 3):
                step(i, 0)
            with sp.Fori(3, B - 2) as i:
                step(i, 0)
            for i in range(B - 2, B + 2):
                step(i, 0)
            out_image(B - 1)
            sp.wait_ge(s_store, 32 * B)

        @block.gpsimd
        def _(pool):
            zeroed = [x[0], x[1], x[2], k_hi, k_lo, k_r2, k_rlo, q, q_r, vz_hi, vz_lo, vz_r2, vz_rlo, a_r, o[0], o[1],
                      o[2]]
            for t in zeroed:
                pool.memset(t[:].bitcast(F32), 0.0).then_inc(s_zero, 1)
            pool.memset(moments[:], 1.0).then_inc(s_zero, 1)
            pool.memset(half_neg[:], -0.5).then_inc(s_zero, 1)
            pool.memset(eps[:], EPS).then_inc(s_zero, 1)
            assert len(zeroed) + 5 == N_ZERO
            pool.wait_ge(s_zero, N_ZERO)

            def step(i, u):
                pa = par(u)
                if has(i - 2):
                    pool.wait_ge(s_res, 32 * (i - 1))
                    wait(pool, s_h1, 2 * (i - 2))
                    pool.tensor_tensor(resb[:, 0, :], res[:, 0, :], bp[:], ALU.add).then_inc(s_resb, 1)
                if has(i - 1):
                    wait(pool, s_av, i - 1)
                    pool.wait_ge(s_v, 2 * i)
                if has(i - 2):
                    pool.tensor_tensor(resb[0:NC, 1, :], res[0:NC, 1, :], bp[0:NC, :], ALU.add).then_inc(s_resb, 1)
                if has(i - 1):
                    src = v[:, 1 - pa, 0, :].rearrange("p (g d) -> p g d", d=DH)
                    src_r = v[0:NC, 1 - pa, 1, :].rearrange("p (g d) -> p g d", d=DH)
                    pool.tensor_copy(win(vz_hi, 0, NT), src).then_inc(s_vz, 1)
                    pool.tensor_copy(win(vz_r2, 0, NC), src_r).then_inc(s_vz, 1)
                    pool.wait_ge(s_vz, 4 * (i - 1) + 1)
                    pool.tensor_tensor(win(vz_lo, 0, NT), src, f(win(vz_hi, 0, NT)), ALU.subtract).then_inc(s_vz, 1)
                if has(i + 1):
                    pool.wait_ge(s_q, 2 * (i + 2))
                    wait(pool, s_s, GROUPS * i)
                if has(i - 1):
                    pool.wait_ge(s_vz, 4 * (i - 1) + 2)
                    pool.tensor_tensor(win(vz_rlo, 0, NC), src_r, f(win(vz_r2, 0, NC)), ALU.subtract).then_inc(s_vz, 1)
                if has(i + 1):
                    for g in range(H):
                        pool.tensor_scalar(heads(qg_r[0:DR, 1 - pa, :], g), q_r[:, :].rearrange("p (t s) -> p t s", s=QS),
                                           wls_r[:, g:g + 1], None, ALU.mult).then_inc(s_qgr, 1)
                        if g == 5 and has(i + 2):
                            rstd_of(i + 2)
                elif has(i + 2):
                    rstd_of(i + 2)

            def rstd_of(n):
                pool.wait_ge(s_mom, 2 * (n + 1))
                wait(pool, s_xhat, 2 * n)
                pool.tensor_tensor(var_eps[:], moments[:, :, 1], eps[:], ALU.add).then_inc(s_veps, 1)
                pool.wait_ge(s_veps, n + 1)
                pool.tensor_tensor(rstd[:], var_eps[:], half_neg[:], ALU.pow).then_inc(s_rstd, 1)
            steps(pool, step)

        @block.scalar
        def _(act):
            act.wait_ge(s_const, 16 * N_LOADS)
            cuts = ((wqk, 0, NQK), (wv, NQK, NQK + D), (wo, NQK + D, NQK + 2 * D))
            for w, a, b in cuts:
                act.activation(w.hi[:], w_in[:, a:b], ACT.Copy).then_inc(s_whi, 1)
                act.activation(w.rest2[:], w_in_r[:, a:b], ACT.Copy).then_inc(s_whi, 1)
            act.wait_ge(s_prep, 2)
            act.activation(kron_h[:], kron[:], ACT.Copy).then_inc(s_whi, 1)
            act.wait_ge(s_zero, N_ZERO)

            def slot(i, u, j):
                pa = par(u)
                n, ja = (i, j - 2) if j >= 2 else (i - 1, j - 2 + GROUPS)
                if has(n):
                    pn = pa if j >= 2 else 1 - pa
                    act.wait_ge(s_m, GROUPS * n + ja + 1)
                    if ja == 0:
                        wait(act, s_av, n - 1)
                    act.activation(mixed(a_hi[:, pn, :], ja), mix_bank(ps_m[ja % 2], ja, NT), ACT.Copy).then_inc(s_ahi, 1)
                    act.activation(mixed(a_r[0:NC, pn, :], ja), mix_bank(ps_mr[ja % 2], ja, NC), ACT.Copy
                                   ).then_inc(s_ahi, 1)
                if j == 0 and has(i - 2):
                    act.wait_ge(s_av, i - 1)
                    wait(act, s_pr, i - 2)
                    act.activation(o[0][:, 0:S], ps_o[0:DM, 0:S], ACT.Copy).then_inc(s_ohi, 1)
                    act.activation(o[2][0:DR, 0:S], ps_o[0:DR, SE:SE + S], ACT.Copy).then_inc(s_ohi, 1)
                if j == 0 and has(i - 1):
                    wait(act, s_av, i - 1)
                    act.wait_ge(s_v, 2 * i)
                    act.activation(win(vz_r2, 64, 64 + NC), v[0:NC, 1 - pa, 1, :].rearrange("p (g d) -> p g d", d=DH),
                                   ACT.Copy).then_inc(s_vzc, 1)
                if j == 1 and has(i + 1):
                    act.wait_ge(s_kev, 5 * (i + 2))
                    wait(act, s_qgl, 2 * H * (i + 1))
                    wait(act, s_qgr, H * (i + 1))
                    act.activation(q[:, 0:S], ps_q[:, 0:S], ACT.Identity, bias=bq[:]).then_inc(s_q, 1)
                    act.activation(q_r[:, 0:S], ps_q[0:DR, 2 * SE:2 * SE + S], ACT.Identity, bias=bqr[:]
                                   ).then_inc(s_q, 1)
                if has(i):
                    b = j % 2
                    act.wait_ge(s_shift, GROUPS * i + j + 1)
                    wait(act, s_plo, GROUPS * i + j - 1)
                    for n, t in enumerate(group_tiles(j)):
                        last = act.activation(ex[:, b, n, :], ps_s[b][0:HQ, n * SE:n * SE + S], ACT.Exp,
                                              bias=shift[:, b, n:n + 1], accum_out=total[:, b, n:n + 1])
                    last.then_inc(s_exp, 1)
                    act.wait_ge(s_scale, GROUPS * i + j + 1)
                    wait(act, s_m, GROUPS * i + j - 1)
                    for n, t in enumerate(group_tiles(j)):
                        act.activation(p_hi[0:HQ, b, n, :], ex[:, b, n, :], ACT.Copy, scale=scale[:, b, n:n + 1]
                                       ).then_inc(s_phi, 1)
                if j == 5 and has(i + 2):
                    act.wait_ge(s_t, i + 3)
                    wait(act, s_vmm, i + 2)
                    act.activation(x[0][:, 0:S], ps_q[:, 0:S], ACT.Copy).then_inc(s_xhi, 1)
                    act.activation(x[2][0:DR, 0:S], ps_q[0:DR, SE:SE + S], ACT.Copy).then_inc(s_xhi, 1)

            def step(i, u):
                for j in range(GROUPS):
                    slot(i, u, j)
            steps(act, step)

        @block.vector
        def _(dve):
            dve.memset(f(p_lo[96:128, :, :, :]), 0.0).then_inc(s_zero, 1)
            dve.memset(f(p_hi[96:128, :, :, :]), 1.0).then_inc(s_zero, 1)
            dve.wait_ge(s_const, 16 * N_LOADS)
            dve.tensor_scalar(wls[:], wl_in[:], DH ** -0.5, None, ALU.mult).then_inc(s_prep, 1)
            for h in range(1):
                dve.tensor_tensor(kron[0:HQ, :].rearrange("p (g s) -> p g s", s=QS),
                                  ww[:].rearrange("p (g a) -> p g a", a=1).to_broadcast([HQ, H, QS]),
                                  mask[:].rearrange("p (a s) -> p a s", a=1).to_broadcast([HQ, H, QS]), ALU.mult
                                  ).then_inc(s_prep, 1)
            dve.tensor_scalar(wls_r[:], wl_in_r[:], DH ** -0.5, None, ALU.mult).then_inc(s_prep, 1)
            dve.wait_ge(s_whi, 7)
            cuts = ((wqk, 0, NQK), (wv, NQK, NQK + D), (wo, NQK + D, NQK + 2 * D))
            for w, a, b in cuts:
                dve.tensor_tensor(w.lo[:], w_in[:, a:b], f(w.hi[:]), ALU.subtract).then_inc(s_wlo, 1)
                dve.tensor_tensor(w.rest_lo[:], w_in_r[0:DR, a:b], f(w.rest2[0:DR, :]), ALU.subtract).then_inc(s_wlo, 1)
            dve.tensor_tensor(kron_l[:], kron[:], f(kron_h[:]), ALU.subtract).then_inc(s_wlo, 1)
            dve.wait_ge(s_zero, N_ZERO)
            dve.wait_ge(s_prep, 3)

            share = {1: range(0, 2), 2: range(2, 6), 3: range(6, 9), 4: range(9, 12)}

            def queries(i, pa, g_range, stats_of=None):
                qt = q[:, :].rearrange("p (t s) -> p t s", s=QS)
                qt_r = q_r[:, :].rearrange("p (t s) -> p t s", s=QS)
                for g in g_range:
                    dve.tensor_scalar(heads(qg_hi[:, pa, :], g), qt, wls[:, g:g + 1], None, ALU.mult).then_inc(s_qgh, 1)
                for g in g_range:
                    dve.wait_ge(s_qgh, H * i + g + 1)
                    dve.scalar_tensor_tensor(out=heads(qg_lo[:, pa, :], g), in0=qt, scalar=wls[:, g:g + 1],
                                             in1=f(heads(qg_hi[:, pa, :], g)), op0=ALU.mult, op1=ALU.subtract
                                             ).then_inc(s_qgl, 1)
                    dve.wait_ge(s_qgr, H * i + g + 1)
                    if stats_of is not None and g == g_range[-1]:
                        dve.wait_ge(s_stats, 2 * stats_of + 2)
                    dve.scalar_tensor_tensor(out=heads(qg_r[DR:2 * DR, pa, :], g), in0=qt_r, scalar=wls_r[:, g:g + 1],
                                             in1=f(heads(qg_r[0:DR, pa, :], g)), op0=ALU.mult, op1=ALU.subtract
                                             ).then_inc(s_qgl, 1)

            def slot(i, u, j):
                pa = par(u)
                b = j % 2
                if has(i):
                    nt = len(group_tiles(j))
                    dve.wait_ge(s_s, GROUPS * i + j + 1)
                    dve.tensor_reduce(out=neg_max[:, b, 0:nt], in_=ps_s[b][0:HQ, 0:nt * SE].rearrange(
                        "p (t k) -> p t k", k=SE)[:, :, 0:S], op=ALU.max, axis=AX_X, negate=True).then_inc(s_max, 1)
                    dve.wait_ge(s_max, GROUPS * i + j + 1)
                    dve.tensor_scalar(shift[:, b, 0:nt], neg_max[:, b, 0:nt], bl[:], bl[:], ALU.subtract, ALU.add
                                      ).then_inc(s_shift, 1)
                n, ja = (i, j - 2) if j >= 2 else (i - 1, j - 2 + GROUPS)
                if has(n):
                    pn = pa if j >= 2 else 1 - pa
                    dve.wait_ge(s_ahi, 2 * (GROUPS * n + ja) + 2)
                    dve.tensor_tensor(mixed(a_lo[:, pn, :], ja), mix_bank(ps_m[ja % 2], ja, NT),
                                      f(mixed(a_hi[:, pn, :], ja)), ALU.subtract).then_inc(s_alo, 1)
                    dve.tensor_tensor(mixed(a_r[64:64 + NC, pn, :], ja), mix_bank(ps_mr[ja % 2], ja, NC),
                                      f(mixed(a_r[0:NC, pn, :], ja)), ALU.subtract).then_inc(s_alo, 1)
                if j == 0 and has(i - 2):
                    dve.wait_ge(s_ohi, 2 * (i - 1))
                    dve.tensor_tensor(o[1][:, 0:S], ps_o[0:DM, 0:S], f(o[0][:, 0:S]), ALU.subtract).then_inc(s_olo, 1)
                    dve.tensor_tensor(o[2][DR:2 * DR, 0:S], ps_o[0:DR, SE:SE + S], f(o[2][0:DR, 0:S]), ALU.subtract
                                      ).then_inc(s_olo, 1)
                if j == 1 and has(i + 1):
                    pk = 1 - pa
                    km, kr = ps_q[:, SE:SE + S], ps_q[DR:2 * DR, 2 * SE:2 * SE + S]
                    dve.wait_ge(s_qk, i + 2)
                    wait(dve, s_s, GROUPS * i)
                    dve.tensor_scalar(k_r2[DR:, pk, 0:S], kr, bkr[DR:, :], None, ALU.add).then_inc(s_kev, 1)
                    dve.tensor_scalar(k_hi[:, pk, 0:S], km, bk[:], None, ALU.add).then_inc(s_kev, 1)
                    dve.wait_ge(s_kev, 5 * (i + 1) + 1)
                    dve.tensor_copy(k_r2[0:DR, pk, 0:S], f(k_r2[DR:, pk, 0:S])).then_inc(s_kev, 1)
                    dve.scalar_tensor_tensor(out=k_rlo[:, pk, 0:S], in0=kr, scalar=bkr[DR:, :], in1=f(k_r2[DR:, pk, 0:S]),
                                             op0=ALU.add, op1=ALU.subtract).then_inc(s_kev, 1)
                    dve.wait_ge(s_kev, 5 * (i + 1) + 2)
                    dve.scalar_tensor_tensor(out=k_lo[:, pk, 0:S], in0=km, scalar=bk[:], in1=f(k_hi[:, pk, 0:S]),
                                             op0=ALU.add, op1=ALU.subtract).then_inc(s_kev, 1)
                if j == 2 and has(i - 2):
                    dve.wait_ge(s_pr, i - 1)
                    dve.wait_ge(s_resb, 2 * (i - 1))
                    wait(dve, s_store, 32 * (i - 2))
                    dve.tensor_tensor(hout[:, 0, :], ps_o[:, 0:D], resb[:, 0, :], ALU.add).then_inc(s_h1, 1)
                    dve.tensor_tensor(hout[0:NC, 1, :], ps_o[0:NC, D:2 * D], resb[0:NC, 1, :], ALU.add).then_inc(s_h1, 1)
                if j == 3 and has(i + 1):
                    dve.wait_ge(s_vmm, i + 2)
                    wait(dve, s_vz, 4 * i)
                    wait(dve, s_vzc, i)
                    dve.tensor_tensor(v[:, 1 - pa, 0, :], ps_q[:, 0:D], bv[:], ALU.add).then_inc(s_v, 1)
                    dve.tensor_tensor(v[0:NC, 1 - pa, 1, :], ps_q[0:NC, D:2 * D], bv[0:NC, :], ALU.add).then_inc(s_v, 1)
                if j == 2 and has(i + 2):
                    dve.wait_ge(s_tok, 32 * (i + 3))
                    wait(dve, s_rstd, i + 2)
                    dve.bn_stats(stats[:, 0, :], tok[:, 0, :]).then_inc(s_stats, 1)
                    dve.bn_stats(stats[0:NC, 1, :], tok[0:NC, 1, :]).then_inc(s_stats, 1)
                if j in share and has(i + 1):
                    if j == 1:
                        dve.wait_ge(s_q, 2 * (i + 2))
                    queries(i + 1, 1 - pa, share[j], i + 2 if j == 2 and has(i + 2) else None)
                if j == 2 and has(i + 2):
                    if not has(i + 1):
                        dve.wait_ge(s_stats, 2 * (i + 2) + 2)
                    dve.bn_aggr(moments[:, 0, :], stats[:, 0, :]).then_inc(s_mom, 1)
                    dve.bn_aggr(moments[0:NC, 1, :], stats[0:NC, 1, :]).then_inc(s_mom, 1)
                if j == 4 and has(i + 2):
                    dve.wait_ge(s_rstd, i + 3)
                    wait(dve, s_t, i + 2)
                    for t, rows in ((0, NT), (1, NC)):
                        dve.tensor_scalar(xhat[0:rows, t, :], tok[0:rows, t, :], moments[0:rows, t, 0:1],
                                          rstd[0:rows, t:t + 1], ALU.subtract, ALU.mult).then_inc(s_xhat, 1)
                if has(i):
                    dve.wait_ge(s_exp, GROUPS * i + j + 1)
                    dve.reciprocal(scale[:, b, 0:nt], total[:, b, 0:nt]).then_inc(s_scale, 1)
                    wait(dve, s_m, GROUPS * i + j - 1)
                    for n, t in enumerate(group_tiles(j)):
                        dve.wait_ge(s_phi, TILES * i + t + 1)
                        last = dve.scalar_tensor_tensor(out=p_lo[0:HQ, b, n, :], in0=ex[:, b, n, :],
                                                        scalar=scale[:, b, n:n + 1], in1=f(p_hi[0:HQ, b, n, :]),
                                                        op0=ALU.mult, op1=ALU.subtract)
                    last.then_inc(s_plo, 1)
                if j == 5 and has(i + 2):
                    dve.wait_ge(s_xhi, 2 * (i + 3))
                    dve.tensor_tensor(x[1][:, 0:S], ps_q[:, 0:S], f(x[0][:, 0:S]), ALU.subtract).then_inc(s_xlo, 1)
                    dve.tensor_tensor(x[2][DR:, 0:S], ps_q[0:DR, SE:SE + S], f(x[2][0:DR, 0:S]), ALU.subtract
                                      ).then_inc(s_xlo, 1)

            def step(i, u):
                for j in range(GROUPS):
                    slot(i, u, j)
            steps(dve, step)

        @block.tensor
        def _(pe):
            pe.wait_ge(s_wlo, 7)
            pe.wait_ge(s_zero, N_ZERO)

            def logits(i, pa, j):
                if j == 0:
                    pe.wait_ge(s_qgl, 2 * H * (i + 1))
                    pe.wait_ge(s_q, 2 * (i + 1))
                wait(pe, s_exp, GROUPS * i + j - 1)
                for n, t in enumerate(group_tiles(j)):
                    c = slice(t * HQ, (t + 1) * HQ)
                    out = ps_s[j % 2][0:HQ, n * SE:(n + 1) * SE]
                    pe.matmul(out, qg_hi[:, pa, c], k_hi[:, pa, :], start=True, stop=False)
                    pe.matmul(out, qg_lo[:, pa, c], k_hi[:, pa, :], start=False, stop=False)
                    pe.matmul(out, qg_hi[:, pa, c], k_lo[:, pa, :], start=False, stop=False)
                    pe.matmul(out, qg_r[:, pa, c], k_r2[:, pa, :], start=False, stop=False)
                    last = pe.matmul(out, qg_r[0:DR, pa, c], k_rlo[:, pa, :], start=False, stop=True)
                last.then_inc(s_s, 1)

            def mix(i, j):
                b = j % 2
                pe.wait_ge(s_plo, GROUPS * i + j + 1)
                wait(pe, s_alo, 2 * (GROUPS * i + j - 1))
                for bank_, rows, cols in ((ps_m[b], NT, slice(0, NT)), (ps_mr[b], NC, slice(NT, S))):
                    for n, t in enumerate(group_tiles(j)):
                        out = bank_[0:rows, n * HQ:(n + 1) * HQ]
                        pe.matmul(out, p_hi[0:HQ + 1, b, n, cols], kron_h[:], start=True, stop=False)
                        pe.matmul(out, p_lo[0:HQ + 1, b, n, cols], kron_h[:], start=False, stop=False)
                        last = pe.matmul(out, p_hi[0:HQ + 1, b, n, cols], kron_l[:], start=False, stop=True)
                last.then_inc(s_m, 1)

            def values(i, pa, g_range):
                for g in g_range:
                    rows, gg, at = (DM, g, 0) if g < DM // DH else (DR, g - DM // DH, SE)
                    w = slice(g * VW + VW - DH * (gg + 1), g * VW + VW - DH * (gg + 1) + rows)
                    c = slice(g * SQ, g * SQ + SE)
                    out = ps_o[0:rows, at:at + SE]
                    pe.matmul(out, vz_hi[:, w], a_hi[:, pa, c], start=(gg == 0), stop=False)
                    pe.matmul(out, vz_lo[:, w], a_hi[:, pa, c], start=False, stop=False)
                    pe.matmul(out, vz_hi[:, w], a_lo[:, pa, c], start=False, stop=False)
                    pe.matmul(out, vz_r2[0:64 + NC, w], a_r[0:64 + NC, pa, c], start=False, stop=False)
                    last = pe.matmul(out, vz_rlo[:, w], a_r[0:NC, pa, c], start=False,
                                     stop=(g in (DM // DH - 1, H - 1)))
                return last

            def slot(i, u, j):
                pa = par(u)
                n, js, ps = (i, j + 1, pa) if j < GROUPS - 1 else (i + 1, 0, 1 - pa)
                if has(n):
                    logits(n, ps, js)
                n, jm = (i, j - 1) if j else (i - 1, GROUPS - 1)
                if has(n):
                    mix(n, jm)
                if j == 0 and has(i + 1):
                    pe.wait_ge(s_xlo, 2 * (i + 2))
                    for n in range(3):
                        last = product(pe, ps_q[:, n * SE:(n + 1) * SE], x, wqk, slice(0, SE),
                                       slice(n * 128, (n + 1) * 128), False)
                    last.then_inc(s_qk, 1)
                if j == 1 and has(i - 2):
                    pe.wait_ge(s_olo, 2 * (i - 1))
                    product(pe, ps_o[0:NT, 0:D], o, wo, slice(0, NT), slice(0, D), True)
                    product(pe, ps_o[0:NC, D:2 * D], o, wo, slice(NT, S), slice(0, D), True).then_inc(s_pr, 1)
                if j == 2 and has(i + 1):
                    pe.wait_ge(s_q, 2 * (i + 2))
                    product(pe, ps_q[0:NT, 0:D], x, wv, slice(0, NT), slice(0, D), True)
                    product(pe, ps_q[0:NC, D:2 * D], x, wv, slice(NT, S), slice(0, D), True).then_inc(s_vmm, 1)
                if j >= 3 and has(i - 1):
                    if j == 3:
                        pe.wait_ge(s_alo, 2 * GROUPS * i)
                        pe.wait_ge(s_vz, 4 * i)
                        pe.wait_ge(s_vzc, i)
                        wait(pe, s_h1, 2 * (i - 1))
                    last = values(i - 1, 1 - pa, range(4 * (j - 3), 4 * (j - 2)))
                    if j == 5:
                        last.then_inc(s_av, 1)
                if j == 4 and has(i + 2):
                    pe.wait_ge(s_xhat, 2 * (i + 3))
                    wait(pe, s_v, 2 * (i + 2))
                    for t, rows in ((0, NT), (1, NC)):
                        pe.transpose(ps_q[0:DM, t * NT:t * NT + rows], xhat[0:rows, t, 0:DM], ident[0:rows, 0:rows])
                        last = pe.transpose(ps_q[0:DR, SE + t * NT:SE + t * NT + rows], xhat[0:rows, t, DM:D],
                                            ident[0:rows, 0:rows])
                    last.then_inc(s_t, 1)

            def step(i, u):
                for j in range(GROUPS):
                    slot(i, u, j)
            steps(pe, step)


N_LOADS = 15 + 3 + 4 + 8 + 1
N_ZERO = 17 + 5


def experts(nc, h1, out, sg, su, sd, rg, ru, rd, router_rep, rbias_rep, ident_in):
    ctx = ExitStack()
    with ctx:
        def sb(name, shape, dt=F32):
            return ctx.enter_context(nc.sbuf_tensor("ex_" + name, shape, dt))

        def sem(name):
            return ctx.enter_context(nc.semaphore("ex_" + name))

        bank = [ctx.enter_context(nc.psum_tensor(f"ex_bank{n}", [128, 512], F32)) for n in range(8)]
        ps_g, ps_u, ps_d, ps_x, ps_xr = bank[0:2], bank[2:4], bank[4:6], bank[6], bank[7]
        NH = NF * 128
        gate, up = Split(sb, "gate", NH), Split(sb, "up", NH)
        down_h, down_l = sb("down_h", [128, NF, D], F32R), sb("down_l", [128, NF, D], F32R)
        stage, stage_r = sb("stage", [128, FT]), sb("stage_r", [128, FT])
        stage_d = sb("stage_d", [128, FT // 128, D])
        router, rbias, ident = sb("router", [TP, E, D]), sb("rbias", [TP, TT, E]), sb("ident", [128, 128])
        h = sb("h", [TP, 2, TT, D])
        stats, moments = sb("stats", [TP, TT, 6]), sb("moments", [TP, TT, 2])
        var_eps, half_neg, rstd = sb("var_eps", [TP, TT]), sb("half_neg", [TP, TT]), sb("rstd", [TP, TT])
        eps = sb("eps", [TP, TT])
        xhat, rprod = sb("xhat", [TP, TT, D]), sb("rprod", [TP, TT * E, D])
        rt = [sb(f"rt{n}", [TP, TT, E]) for n in range(6)]
        rs = [sb(f"rs{n}", [TP, TT]) for n in range(3)]
        cw = sb("cw", [TP, 2, TT, E])
        x = (sb("x_hi", [DM, CH], F32R), sb("x_lo", [DM, CH], F32R), sb("x_rest", [2 * DR, CH], F32R))
        act_g, hid = sb("act_g", [128, 2, CH]), sb("hid", [128, 2, CH])
        hid_hi, hid_lo = sb("hid_hi", [128, NF, CH], F32R), sb("hid_lo", [128, NF, CH], F32R)
        y = sb("y", [TP, 2, 4, D])

        s_w, s_wh, s_wl, s_const = sem("w"), sem("wh"), sem("wl"), sem("const")
        s_h, s_store = [sem("h0"), sem("h1")], [sem("store0"), sem("store1")]
        s_zero, s_st, s_mom, s_veps, s_rstd, s_xhat, s_t, s_xhi, s_xlo = (
            sem(n) for n in ("zero", "st", "mom", "veps", "rstd", "xhat", "t", "xhi", "xlo"))
        s_lg, s_tanh, s_r, s_cw = sem("lg"), sem("tanh"), sem("r"), sem("cw")
        s_gu, s_silu, s_hid, s_hh, s_hl, s_dn, s_y = (sem(n) for n in ("gu", "silu", "hid", "hh", "hl", "dn", "y"))

        def has(c):
            return not isinstance(c, int) or 0 <= c < CHUNKS

        def steps(eng, step):
            for c in range(-1, 1):
                step(c, c % 2, (c + 1) // 2)
            with eng.Fori(0, (CHUNKS - 2) // 2) as it:
                for u in range(2):
                    step(2 * it + u + 1, (u + 1) % 2, it + 1)
            for c in range(CHUNKS - 1, CHUNKS + 1):
                step(c, c % 2, (c + 1) // 2)

        def expert_weights(k):
            return (sg, su, sd) if k == 0 else (rg[k - 1], ru[k - 1], rd[k - 1])

        hv = h1.rearrange("b s d -> (b s) d").rearrange("(c t p) d -> c p t d", t=TT, p=TP)
        ov = out.rearrange("b s d -> (b s) d").rearrange("(c t p) d -> c p t d", t=TT, p=TP)
        block = ctx.enter_context(nc.Block())

        units = [(k, m) for k in range(4) for m in range(3)]

        def load(sp, c, u=0):
            sp.dma_start(h[:, u, :, :], hv[bass.ds(c, 1)].rearrange("a p t d -> (a p) t d")).then_inc(s_h[u], 16)

        @block.sync
        def _(sp):
            sp.dma_start(router[:], router_rep).then_inc(s_const, 16)
            sp.dma_start(rbias[:], rbias_rep).then_inc(s_const, 16)
            sp.dma_start(ident[:], ident_in).then_inc(s_const, 16)
            load(sp, 0)
            for n, (k, m) in enumerate(units):
                if n:
                    sp.wait_ge(s_wl, n)
                w = expert_weights(k)[m]
                if m < 2:
                    sp.dma_start(stage[:], w[0:DM, :]).then_inc(s_w, 16)
                    for r in range(2):
                        sp.dma_start(stage_r[r * DR:(r + 1) * DR, :], w[DM:D, :]).then_inc(s_w, 16)
                else:
                    sp.dma_start(stage_d[:], w.rearrange("(f p) d -> p f d", p=128)).then_inc(s_w, 48)

            def step(c, u, pairs):
                if has(c - 1):
                    for t in range(TT):
                        sp.wait_ge(s_y, TT * (c - 1) + t + 1)
                        sp.dma_start(ov[bass.ds(c - 1, 1), :, t, :].rearrange("a p d -> (a p) d"), y[:, t % 2, 3, :]
                                     ).then_inc(s_store[t % 2], 16)
                if has(c + 1) and not (isinstance(c, int) and c == -1):
                    load(sp, c + 1, 1 - u)
            steps(sp, step)
            for b in range(2):
                sp.wait_ge(s_store[b], 16 * CHUNKS * TT // 2)

        @block.gpsimd
        def _(pool):
            pool.memset(half_neg[:], -0.5).then_inc(s_zero, 1)
            pool.memset(eps[:], EPS).then_inc(s_zero, 1)
            pool.wait_ge(s_zero, 2)

            def step(c, u, pairs):
                if has(c + 1):
                    pool.wait_ge(s_mom, TT * (c + 2))
                    wait(pool, s_xhat, TT * (c + 1))
                    pool.tensor_tensor(var_eps[:], moments[:, :, 1], eps[:], ALU.add).then_inc(s_veps, 1)
                    pool.wait_ge(s_veps, c + 2)
                    pool.tensor_tensor(rstd[:], var_eps[:], half_neg[:], ALU.pow).then_inc(s_rstd, 1)
            steps(pool, step)

        @block.scalar
        def _(act):
            for n, (k, m) in enumerate(units):
                act.wait_ge(s_w, 48 * (n + 1))
                c = slice(k * FT, (k + 1) * FT)
                if m < 2:
                    w = (gate, up)[m]
                    act.activation(w.hi[:, c], stage[:], ACT.Copy)
                    act.activation(w.rest2[:, c], stage_r[:], ACT.Copy).then_inc(s_wh, 1)
                else:
                    act.activation(down_h[:, 3 * k:3 * k + 3, :], stage_d[:], ACT.Copy).then_inc(s_wh, 1)

            def step(c, u, pairs):
                for fi in range(NF):
                    if has(c):
                        n = NF * c + fi
                        b = fi % 2
                        act.wait_ge(s_gu, n + 1)
                        wait(act, s_hid, n - 1)
                        act.activation(act_g[:, b, :], ps_g[b][:, 0:CH], ACT.Silu).then_inc(s_silu, 1)
                        act.wait_ge(s_hid, n + 1)
                        wait(act, s_dn, TT * c) if fi == 0 else None
                        act.activation(hid_hi[:, fi, :], hid[:, b, :], ACT.Copy).then_inc(s_hh, 1)
                    if fi == 4 and has(c + 1):
                        act.wait_ge(s_lg, c + 2)
                        act.activation(rt[1][:], rt[0][:], ACT.Tanh, scale=0.5).then_inc(s_tanh, 1)
                if has(c + 1):
                    act.wait_ge(s_t, c + 2)
                    act.activation(x[0][:], ps_x[:, 0:CH], ACT.Copy).then_inc(s_xhi, 1)
                    act.activation(x[2][0:DR, :], ps_xr[0:DR, 0:CH], ACT.Copy).then_inc(s_xhi, 1)
            steps(act, step)

        @block.vector
        def _(dve):
            for n, (k, m) in enumerate(units):
                dve.wait_ge(s_wh, n + 1)
                c = slice(k * FT, (k + 1) * FT)
                if m < 2:
                    w = (gate, up)[m]
                    dve.tensor_tensor(w.lo[:, c], stage[:], f(w.hi[:, c]), ALU.subtract)
                    dve.tensor_tensor(w.rest_lo[:, c], stage_r[0:DR, :], f(w.rest2[0:DR, c]), ALU.subtract).then_inc(s_wl, 1)
                else:
                    dve.tensor_tensor(down_l[:, 3 * k:3 * k + 3, :], stage_d[:], f(down_h[:, 3 * k:3 * k + 3, :]),
                                      ALU.subtract).then_inc(s_wl, 1)
            dve.wait_ge(s_const, 48)

            def normalise(c, u, pairs):
                dve.wait_ge(s_h[u], 16 * pairs + 16)
                wait(dve, s_rstd, c)
                for t in range(TT):
                    dve.bn_stats(stats[:, t, :], h[:, u, t, :]).then_inc(s_st, 1)

            def aggregate():
                for t in range(TT):
                    dve.bn_aggr(moments[:, t, :], stats[:, t, :]).then_inc(s_mom, 1)

            def scale_tokens(c, u):
                dve.wait_ge(s_rstd, c + 1)
                wait(dve, s_t, c)
                for t in range(TT):
                    dve.tensor_scalar(xhat[:, t, :], h[:, u, t, :], moments[:, t, 0:1], rstd[:, t:t + 1],
                                      ALU.subtract, ALU.mult).then_inc(s_xhat, 1)

            def chain(op, n):
                op.then_inc(s_r, 1)
                dve.wait_ge(s_r, n)

            R = 12

            def route(c, u):
                r0 = R * c
                for t in range(TT):
                    dve.wait_ge(s_xhat, TT * c + t + 1)
                    for e in range(E):
                        last = dve.scalar_tensor_tensor(out=rprod[:, t * E + e, :], in0=xhat[:, t, :], scalar=1.0,
                                                        in1=router[:, e, :], op0=ALU.mult, op1=ALU.mult,
                                                        accum_out=rt[5][:, t, e:e + 1])
                chain(last, r0 + 1)
                dve.tensor_tensor(rt[0][:], rt[5][:], rbias[:], ALU.add).then_inc(s_lg, 1)
                dve.wait_ge(s_tanh, c + 1)
                chain(dve.tensor_scalar(rt[2][:], rt[1][:], 0.5, 0.5, ALU.mult, ALU.add), r0 + 2)
                p = [rt[2][:, :, e] for e in range(E)]
                keep = [rt[3][:, :, e] for e in range(E)]
                chain(dve.tensor_tensor(rs[0][:], p[1], p[2], ALU.min), r0 + 3)
                chain(dve.tensor_tensor(keep[0], p[0], rs[0][:], ALU.is_ge), r0 + 4)
                chain(dve.tensor_tensor(rs[1][:], p[0], p[1], ALU.min), r0 + 5)
                chain(dve.tensor_tensor(keep[2], p[2], rs[1][:], ALU.is_gt), r0 + 6)
                chain(dve.tensor_tensor(rs[2][:], keep[0], keep[2], ALU.add), r0 + 7)
                chain(dve.tensor_scalar(keep[1], rs[2][:], -1.0, 2.0, ALU.mult, ALU.add), r0 + 8)
                chain(dve.tensor_tensor(rt[4][:], rt[2][:], rt[3][:], ALU.mult), r0 + 9)
                chain(dve.tensor_reduce(out=rs[0][:], in_=rt[4][:], op=ALU.add, axis=AX_X), r0 + 10)
                chain(dve.reciprocal(rs[1][:], rs[0][:]), r0 + 11)
                chain(dve.tensor_tensor(cw[:, u, :, :], rt[4][:],
                                        rs[1][:].rearrange("p (t a) -> p t a", a=1).to_broadcast([TP, TT, E]),
                                        ALU.mult), r0 + 12)

            def combine(c, u, t):
                n = TT * c + t
                b = t % 2
                dve.wait_ge(s_dn, n + 1)
                wait(dve, s_store[b], 16 * (2 * c + t // 2))
                parts = [ps_d[0][0:TP, 0:D], ps_d[0][0:TP, D:2 * D], ps_d[1][0:TP, 0:D], ps_d[1][0:TP, D:2 * D]]
                dve.tensor_tensor(y[:, b, 0, :], parts[0], h[:, u, t, :], ALU.add).then_inc(s_cw, 1)
                for e in range(E):
                    dve.wait_ge(s_cw, 3 * n + e + 1)
                    last = dve.scalar_tensor_tensor(out=y[:, b, e + 1, :], in0=parts[e + 1], scalar=cw[:, u, t, e:e + 1],
                                                    in1=y[:, b, e, :], op0=ALU.mult, op1=ALU.add)
                    last.then_inc(s_cw if e < E - 1 else s_y, 1)

            def step(c, u, pairs):
                for fi in range(NF):
                    if has(c):
                        n = NF * c + fi
                        b = fi % 2
                        dve.wait_ge(s_silu, n + 1)
                        wait(dve, s_hl, n - 1)
                        wait(dve, s_hh, n - 1)
                        dve.tensor_tensor(hid[:, b, :], act_g[:, b, :], ps_u[b][:, 0:CH], ALU.mult).then_inc(s_hid, 1)
                        dve.wait_ge(s_hh, n + 1)
                        if fi == 0:
                            wait(dve, s_dn, TT * c)
                        if fi == 2 and has(c + 1):
                            dve.wait_ge(s_st, TT * (c + 2))
                        dve.tensor_tensor(hid_lo[:, fi, :], hid[:, b, :], f(hid_hi[:, fi, :]), ALU.subtract
                                          ).then_inc(s_hl, 1)
                    if fi == 1 and has(c + 1):
                        normalise(c + 1, 1 - u, pairs)
                    if fi == 2 and has(c + 1):
                        if not has(c):
                            dve.wait_ge(s_st, TT * (c + 2))
                        aggregate()
                    if fi == 4 and has(c + 1):
                        scale_tokens(c + 1, 1 - u)
                        route(c + 1, 1 - u)
                if has(c + 1):
                    dve.wait_ge(s_xhi, 2 * (c + 2))
                    dve.tensor_tensor(x[1][:], ps_x[:, 0:CH], f(x[0][:]), ALU.subtract).then_inc(s_xlo, 1)
                    dve.tensor_tensor(x[2][DR:, :], ps_xr[0:DR, 0:CH], f(x[2][0:DR, :]), ALU.subtract).then_inc(s_xlo, 1)
                if has(c):
                    for t in range(TT):
                        combine(c, u, t)
            steps(dve, step)

        @block.tensor
        def _(pe):
            pe.wait_ge(s_wl, len(units))
            pe.wait_ge(s_const, 48)

            def step(c, u, pairs):
                if has(c):
                    pe.wait_ge(s_xlo, 2 * (c + 1))
                for fi in range(NF):
                    if has(c):
                        n = NF * c + fi
                        b = fi % 2
                        cols = slice(fi * 128, (fi + 1) * 128)
                        wait(pe, s_hid, n - 1)
                        product(pe, ps_g[b][:, 0:CH], x, gate, slice(0, CH), cols, False)
                        product(pe, ps_u[b][:, 0:CH], x, up, slice(0, CH), cols, False).then_inc(s_gu, 1)
                if has(c + 1):
                    pe.wait_ge(s_xhat, TT * (c + 2))
                    wait(pe, s_xlo, 2 * (c + 1))
                    for t in range(TT):
                        pe.transpose(ps_x[:, t * TP:(t + 1) * TP], xhat[:, t, 0:DM], ident[0:TP, 0:TP])
                        last = pe.transpose(ps_xr[0:DR, t * TP:(t + 1) * TP], xhat[:, t, DM:D], ident[0:TP, 0:TP])
                    last.then_inc(s_t, 1)
                if has(c):
                    for t in range(TT):
                        n = TT * c + t
                        pe.wait_ge(s_hl, NF * (c + 1))
                        wait(pe, s_y, n)
                        cols = slice(t * TP, (t + 1) * TP)
                        for k in range(4):
                            o = ps_d[k // 2][0:TP, (k % 2) * D:(k % 2 + 1) * D]
                            for fi in range(3 * k, 3 * k + 3):
                                pe.matmul(o, hid_hi[:, fi, cols], down_h[:, fi, :], start=(fi == 3 * k), stop=False)
                                pe.matmul(o, hid_lo[:, fi, cols], down_h[:, fi, :], start=False, stop=False)
                                last = pe.matmul(o, hid_hi[:, fi, cols], down_l[:, fi, :], start=False,
                                                 stop=(fi == 3 * k + 2))
                        last.then_inc(s_dn, 1)
            steps(pe, step)


def build(nc, a, out):
    h0 = nc.dram_tensor("h0_scratch", [B, NC, D], F32, kind="Internal").ap()
    h1 = nc.dram_tensor("h1_scratch", [B, S, D], F32, kind="Internal").ap()
    embed_patches(nc, a["xT"], a["w_proj"], a["pos_rep"], a["b_rep"], a["cls_rep"], a["pos0_rep"], h0)
    attention(nc, a["txt"], h0, h1, a["wqkv"], a["bqkv"], a["bv_rep"], a["wl_rep"], a["bl_rep"], a["ww_rep"],
              a["bw_rep"], a["wp"], a["bp_rep"], a["ident"], a["mask"])
    experts(nc, h1, out, a["sg"], a["su"], a["sd"], a["rg"], a["ru"], a["rd"], a["router_rep"], a["rbias_rep"],
            a["ident"])


def layout(inputs):
    import numpy as np

    g = {k: np.asarray(v) for k, v in inputs.items()}
    P = 16
    n = 96 // P
    x = g["x"].reshape(B, n, P, n, P, 3).transpose(0, 1, 3, 2, 4, 5).reshape(B // 2, EMB, KD, 128)
    pos = g["L0_tok_pos_embedding"]
    bqkv = g["L0_attn_bqkv"]
    rows = np.arange(HQ)
    return {
        "xT": x.transpose(0, 3, 2, 1).reshape(B // 2, 128, KD * EMB),
        "w_proj": g["L0_tok_W_proj"],
        "pos_rep": np.concatenate([pos[1:], pos[1:]]),
        "b_rep": np.broadcast_to(g["L0_tok_b_proj"], (EMB, D)),
        "cls_rep": np.broadcast_to(g["L0_tok_cls_token"].reshape(1, D), (B, D)),
        "pos0_rep": np.broadcast_to(pos[0:1], (B, D)),
        "txt": g["txt"],
        "wqkv": g["L0_attn_Wqkv"],
        "bqkv": bqkv,
        "bv_rep": np.broadcast_to(bqkv[2 * D:], (128, D)),
        "wl_rep": np.repeat(g["L0_attn_Wl"], DH, axis=0),
        "bl_rep": np.repeat(g["L0_attn_bl"], QS).reshape(HQ, 1),
        "ww_rep": np.repeat(g["L0_attn_Ww"], QS, axis=0),
        "bw_rep": np.repeat(g["L0_attn_bw"], QS).reshape(1, HQ),
        "wp": g["L0_attn_Wproj"],
        "bp_rep": np.broadcast_to(g["L0_attn_bproj"], (128, D)),
        "ident": np.eye(128, dtype=np.float32),
        "mask": (rows[:, None] % QS == np.arange(QS)[None]).astype(np.float32),
        "sg": g["L0_ffn_shared_gate"], "su": g["L0_ffn_shared_up"], "sd": g["L0_ffn_shared_down"],
        "rg": g["L0_ffn_routed_gate"], "ru": g["L0_ffn_routed_up"], "rd": g["L0_ffn_routed_down"],
        "router_rep": np.broadcast_to(g["L0_ffn_router_w"].T, (TP, E, D)),
        "rbias_rep": np.broadcast_to(g["L0_ffn_routing_bias"], (TP, TT, E)),
    }


def kernel(**inputs):
    import numpy as np
    import concourse.bacc as bacc
    from concourse.bass_utils import run_bass_kernel_spmd

    nc = bacc.Bacc("TRN2", target_bir_lowering=False, num_devices=1)
    arrays, aps = {}, {}
    for name, a in layout(inputs).items():
        arrays["in_" + name] = np.ascontiguousarray(a)
        aps[name] = nc.dram_tensor("in_" + name, a.shape, mybir.dt.from_np(a.dtype), kind="ExternalInput").ap()
    out = nc.dram_tensor("out_0", [B, S, D], F32, kind="ExternalOutput").ap()
    build(nc, aps, out)
    r = run_bass_kernel_spmd(nc, [arrays], core_ids=[0])
    return r.results[0]["out_0"]
```

```python
import concourse.bass as bass
from concourse import mybir
from contextlib import ExitStack

F32 = mybir.dt.float32
F32R = mybir.dt.float32r
ACT = mybir.ActivationFunctionType
ALU = mybir.AluOpType
AX_X = mybir.AxisListType.X

B = 64
D = 192
NT = 128
NP = 36
NC = NP + 1
S = NT + NC
SE = S + 1
H = 12
DH = D // H
DM = 128
DR = D - DM
QS = 10
HQ = H * QS
TILES = -(-S // QS)
SQ = TILES * QS
GROUP = 3
GROUPS = -(-TILES // GROUP)
EPS = 1e-5
KD = 768 // 128
EMB = 2 * NP
NW = 16
VW = 128
VZ = H * VW + VW - DH

FT = 384
E = 3
NF = 4 * FT // 128
TP = 120
TT = 4
CH = TP * TT
CHUNKS = B * S // CH


def group_tiles(j):
    return range(j * GROUP, min(TILES, (j + 1) * GROUP))


def wait(eng, sem, value):
    if isinstance(value, int) and value <= 0:
        return
    eng.wait_ge(sem, value)


def f(ap):
    return ap.bitcast(F32)


class Split:

    def __init__(self, sb, name, n):
        self.hi = sb(name + "_hi", [DM, n], F32R)
        self.lo = sb(name + "_lo", [DM, n], F32R)
        self.rest2 = sb(name + "_rest2", [2 * DR, n], F32R)
        self.rest_lo = sb(name + "_rest_lo", [DR, n], F32R)


def product(pe, out, a, b, a_cols, b_cols, moving_weights):
    xh, xl, xr, w = a[0], a[1], a[2], b
    pairs = [(xh[:, a_cols], w.hi[:, b_cols]), (xl[:, a_cols], w.hi[:, b_cols]), (xh[:, a_cols], w.lo[:, b_cols]),
             (xr[:, a_cols], w.rest2[:, b_cols]), (xr[0:DR, a_cols], w.rest_lo[:, b_cols])]
    last = None
    for n, (x, y) in enumerate(pairs):
        lhs, rhs = (x, y) if moving_weights else (y, x)
        last = pe.matmul(out, lhs, rhs, start=(n == 0), stop=(n == len(pairs) - 1))
    return last


def embed_patches(nc, xT, w_proj, pos_rep, b_rep, cls_rep, pos0_rep, h0):
    ctx = ExitStack()
    with ctx:
        def sb(name, shape, dt=F32):
            return ctx.enter_context(nc.sbuf_tensor("em_" + name, shape, dt))

        def sem(name):
            return ctx.enter_context(nc.semaphore("em_" + name))

        ps = [ctx.enter_context(nc.psum_tensor(f"em_ps{n}", [128, 512], F32)) for n in range(2)]
        w = sb("w", [128, KD, D])
        wh, wl = sb("wh", [128, KD, D], F32R), sb("wl", [128, KD, D], F32R)
        x = sb("x", [128, 2, KD * EMB])
        xh, xl = sb("xh", [128, 2, KD * EMB], F32R), sb("xl", [128, 2, KD * EMB], F32R)
        pos, bias, posb = sb("pos", [EMB, D]), sb("bias", [EMB, D]), sb("posb", [EMB, D])
        cls, pos0, cls_row = sb("cls", [B, D]), sb("pos0", [B, D]), sb("cls_row", [B, D])
        out = sb("out", [EMB, 2, D])
        s_const, s_x = sem("const"), [sem("x0"), sem("x1")]
        s_wh, s_wl, s_cls, s_posb = sem("wh"), sem("wl"), sem("cls"), sem("posb")
        s_xh, s_xl, s_mm, s_out = sem("xh"), sem("xl"), sem("mm"), sem("out")
        s_store, s_cls_store = [sem("st0"), sem("st1")], sem("cls_st")
        half = B // 4
        block = ctx.enter_context(nc.Block())

        @block.sync
        def _(sp):
            sp.dma_start(w[:], w_proj.rearrange("(k p) n -> p k n", p=128)).then_inc(s_const, 16)
            for dst, src in ((pos, pos_rep), (bias, b_rep), (cls, cls_rep), (pos0, pos0_rep)):
                sp.dma_start(dst[:], src).then_inc(s_const, 16)
            for u in range(2):
                sp.dma_start(x[:, u, :], xT[u]).then_inc(s_x[u], 16)
            sp.wait_ge(s_cls, 1)
            sp.dma_start(h0[:, 0, :], cls_row[:]).then_inc(s_cls_store, 16)
            def tile(it, u, more):
                if more:
                    sp.wait_ge(s_xl, 2 * it + u + 1)
                    sp.dma_start(x[:, u, :], xT[bass.ds(2 * it + u + 2, 1)].rearrange("a p n -> (a p) n")
                                 ).then_inc(s_x[u], 16)
                sp.wait_ge(s_out, 2 * it + u + 1)
                for k in range(2):
                    sp.dma_start(h0[bass.ds(4 * it + 2 * u + k, 1), 1:NC, :].rearrange("b n d -> (b n) d"),
                                 out[k * NP:(k + 1) * NP, u, :]).then_inc(s_store[u], 16)
            with sp.Fori(0, half - 1) as it:
                for u in range(2):
                    tile(it, u, True)
            for u in range(2):
                tile(half - 1, u, False)
            for u in range(2):
                sp.wait_ge(s_store[u], 32 * half)
            sp.wait_ge(s_cls_store, 16)

        @block.scalar
        def _(act):
            act.wait_ge(s_const, 80)
            act.activation(wh[:], w[:], ACT.Copy).then_inc(s_wh, 1)
            def tile(i, it, u):
                act.wait_ge(s_x[u], 16 * it + 16)
                wait(act, s_mm, i - 1)
                act.activation(xh[:, u, :], x[:, u, :], ACT.Copy).then_inc(s_xh, 1)
            for u in range(2):
                tile(u, 0, u)
            with act.Fori(1, half) as it:
                for u in range(2):
                    tile(2 * it + u, it, u)

        @block.vector
        def _(dve):
            dve.wait_ge(s_const, 80)
            dve.tensor_tensor(cls_row[:], cls[:], pos0[:], ALU.add).then_inc(s_cls, 1)
            dve.tensor_tensor(posb[:], pos[:], bias[:], ALU.add).then_inc(s_posb, 1)
            dve.wait_ge(s_wh, 1)
            dve.tensor_tensor(wl[:], w[:], f(wh[:]), ALU.subtract).then_inc(s_wl, 1)
            dve.wait_ge(s_posb, 1)

            def low(i, u):
                dve.wait_ge(s_xh, i + 1)
                dve.tensor_tensor(xl[:, u, :], x[:, u, :], f(xh[:, u, :]), ALU.subtract).then_inc(s_xl, 1)

            def store(i, it, u):
                dve.wait_ge(s_mm, i + 1)
                wait(dve, s_store[u], 32 * it)
                dve.tensor_tensor(out[:, u, :], ps[u][0:EMB, 0:D], posb[:], ALU.add).then_inc(s_out, 1)
            low(0, 0)
            for i in range(1, 4):
                low(i, i % 2)
                store(i - 1, (i - 1) // 2, (i - 1) % 2)
            with dve.Fori(2, half) as it:
                for u in range(2):
                    low(2 * it + u, u)
                    store(2 * it + u - 1, it - 1 + u, 1 - u)
            store(2 * half - 1, half - 1, 1)

        @block.tensor
        def _(pe):
            pe.wait_ge(s_wl, 1)

            def tile(i, u):
                pe.wait_ge(s_xl, i + 1)
                wait(pe, s_out, i - 1)
                last = None
                for k in range(KD):
                    cols = slice(k * EMB, (k + 1) * EMB)
                    for n, (a, b) in enumerate(((xh, wh), (xl, wh), (xh, wl))):
                        last = pe.matmul(ps[u][0:EMB, 0:D], a[:, u, cols], b[:, k, :], start=(k + n == 0),
                                         stop=(k == KD - 1 and n == 2))
                last.then_inc(s_mm, 1)
            for u in range(2):
                tile(u, u)
            with pe.Fori(1, half) as it:
                for u in range(2):
                    tile(2 * it + u, u)


def attention(nc, txt, h0, h1, wqkv, bqkv, bv_rep, wl_rep, bl_rep, ww_rep, bw_rep, wp, bp_rep, ident_in, mask_in):
    ctx = ExitStack()
    with ctx:
        def sb(name, shape, dt=F32):
            return ctx.enter_context(nc.sbuf_tensor("at_" + name, shape, dt))

        def sem(name):
            return ctx.enter_context(nc.semaphore("at_" + name))

        bank = [ctx.enter_context(nc.psum_tensor(f"at_bank{n}", [128, 512], F32)) for n in range(8)]
        ps_s, ps_m, ps_mr, ps_q, ps_o = bank[0:2], bank[2:4], bank[4:6], bank[6], bank[7]

        NQK = 2 * D
        w_in, w_in_r = sb("w_in", [DM, NQK + 2 * D]), sb("w_in_r", [2 * DR, NQK + 2 * D])
        wqk, wv, wo = Split(sb, "wqk", NQK), Split(sb, "wv", D), Split(sb, "wo", D)
        bq, bk, bqr, bkr = sb("bq", [DM, 1]), sb("bk", [DM, 1]), sb("bqr", [DR, 1]), sb("bkr", [128, 1])
        bv, bp, bl = sb("bv", [128, D]), sb("bp", [128, D]), sb("bl", [HQ, 1])
        wl_in, wl_in_r = sb("wl_in", [DM, H]), sb("wl_in_r", [DR, H])
        wls, wls_r = sb("wls", [DM, H]), sb("wls_r", [DR, H])
        ww, mask, kron = sb("ww", [HQ, H]), sb("mask", [HQ, QS]), sb("kron", [HQ + 1, HQ])
        kron_h, kron_l = sb("kron_h", [HQ + 1, HQ], F32R), sb("kron_l", [HQ + 1, HQ], F32R)
        ident = sb("ident", [128, 128])

        tok = sb("tok", [128, 2, D])
        stats, moments = sb("stats", [128, 2, 6]), sb("moments", [128, 2, 2])
        var_eps, half_neg, rstd = sb("var_eps", [128, 2]), sb("half_neg", [128, 2]), sb("rstd", [128, 2])
        eps = sb("eps", [128, 2])
        centred, xhat = sb("centred", [128, 2, D]), sb("xhat", [128, 2, D])
        x = (sb("x_hi", [DM, SE], F32R), sb("x_lo", [DM, SE], F32R), sb("x_rest", [2 * DR, SE], F32R))
        q, q_r = sb("q", [DM, SQ]), sb("q_r", [DR, SQ])
        k_hi, k_lo = sb("k_hi", [DM, 2, SE], F32R), sb("k_lo", [DM, 2, SE], F32R)
        k_r2, k_rlo = sb("k_r2", [2 * DR, 2, SE], F32R), sb("k_rlo", [DR, 2, SE], F32R)
        qg_hi, qg_lo = sb("qg_hi", [DM, 2, H * SQ], F32R), sb("qg_lo", [DM, 2, H * SQ], F32R)
        qg_r = sb("qg_r", [2 * DR, 2, H * SQ], F32R)
        v = sb("v", [128, 2, 2, D])
        vz_hi, vz_lo = sb("vz_hi", [NT, VZ], F32R), sb("vz_lo", [NT, VZ], F32R)
        vz_r2, vz_rlo = sb("vz_r2", [128, VZ], F32R), sb("vz_rlo", [NC, VZ], F32R)
        neg_max, lifted, shift = (sb(n, [HQ, 2, GROUP]) for n in ("neg_max", "lifted", "shift"))
        total, scale = sb("total", [HQ, 2, GROUP]), sb("scale", [HQ, 2, GROUP])
        ex = sb("ex", [HQ, 2, GROUP, S])
        p_hi, p_lo = sb("p_hi", [128, 2, GROUP, S], F32R), sb("p_lo", [128, 2, GROUP, S], F32R)
        a_hi, a_lo = sb("a_hi", [NT, 2, H * SQ], F32R), sb("a_lo", [NT, 2, H * SQ], F32R)
        a_r = sb("a_r", [128, 2, H * SQ], F32R)
        o = (sb("o_hi", [DM, SE], F32R), sb("o_lo", [DM, SE], F32R), sb("o_rest", [2 * DR, SE], F32R))
        res, resb, hout = sb("res", [128, 2, D]), sb("resb", [128, 2, D]), sb("hout", [128, 2, D])

        s_const, s_zero, s_whi, s_wlo, s_prep = (sem(n) for n in ("const", "zero", "whi", "wlo", "prep"))
        s_tok, s_res, s_store = sem("tok"), sem("res"), sem("store")
        s_stats, s_mom, s_veps, s_rstd, s_xhat = (sem(n) for n in ("stats", "mom", "veps", "rstd", "xhat"))
        s_t, s_xhi, s_xlo = sem("t"), sem("xhi"), sem("xlo")
        s_qk, s_khi, s_klo, s_q, s_vmm, s_v, s_vz, s_vzc = (
            sem(n) for n in ("qk", "khi", "klo", "q", "vmm", "v", "vz", "vzc"))
        s_qgh, s_qgr, s_qgl = sem("qgh"), sem("qgr"), sem("qgl")
        s_xc = sem("xc")
        s_s, s_max, s_lift, s_shift, s_exp, s_scale, s_norm, s_phi, s_plo = (
            sem(n) for n in ("s", "max", "lift", "shift", "exp", "scale", "norm", "phi", "plo"))
        s_m, s_ahi, s_alo, s_av, s_ohi, s_olo, s_pr, s_resb, s_h1 = (
            sem(n) for n in ("m", "ahi", "alo", "av", "ohi", "olo", "pr", "resb", "h1"))

        def has(i):
            return not isinstance(i, int) or 0 <= i < B

        def par(u):
            return u % 2

        def win(t, a, b):
            return t[a:b, VW - DH:].rearrange("p (g w) -> p g w", w=VW)[:, :, 0:DH]

        def head(ap, g):
            return ap.rearrange("p (t g s) -> p t g s", g=H, s=QS)[:, :, g, :]

        def tiles(ap):
            return ap.rearrange("p (t s) -> p t s", s=QS)

        share = {0: (0, 1), 1: (2, 3), 2: (4, 5), 3: (6, 7, 8), 4: (9, 10, 11)}

        def ago(i, u, j, n):
            return (i, par(u), j - n) if j >= n else (i - 1, 1 - par(u), j - n + GROUPS)

        def mixed(ap, j):
            ts = group_tiles(j)
            return ap.rearrange("p (g t s) -> p t g s", g=H, s=QS)[:, ts[0]:ts[-1] + 1, :, :]

        def mix_bank(t, j, rows):
            n = len(group_tiles(j))
            return t[0:rows, 0:n * HQ].rearrange("p (t g s) -> p t g s", g=H, s=QS)

        def steps(eng, step):
            for i in range(-2, 4):
                step(i, i % 2)
            with eng.Fori(2, (B - 2) // 2) as it:
                for u in range(2):
                    step(2 * it + u, u)
            for i in range(B - 2, B + 2):
                step(i, i % 2)

        block = ctx.enter_context(nc.Block())

        @block.sync
        def _(sp):
            with nc.allow_non_contiguous_dma("weights are loaded once"):
                for lo, n, at in ((0, DM, 0), (D, DM, DM), (DM, DR, 2 * DM), (D + DM, DR, 2 * DM + DR), (2 * D, D, NQK)):
                    sp.dma_start(w_in[:, at:at + n], wqkv[0:DM, lo:lo + n]).then_inc(s_const, 16)
                    for r in range(2):
                        sp.dma_start(w_in_r[r * DR:(r + 1) * DR, at:at + n], wqkv[DM:D, lo:lo + n]).then_inc(s_const, 16)
                sp.dma_start(w_in[:, NQK + D:], wp[0:DM, :]).then_inc(s_const, 16)
                for r in range(2):
                    sp.dma_start(w_in_r[r * DR:(r + 1) * DR, NQK + D:], wp[DM:D, :]).then_inc(s_const, 16)
                for dst, lo, n in ((bq[:], 0, DM), (bqr[:], DM, DR), (bk[:], D, DM), (bkr[DR:, :], D + DM, DR)):
                    sp.dma_start(dst, bqkv[lo:lo + n].rearrange("(n a) -> n a", a=1)).then_inc(s_const, 16)
                for dst, src in ((bv, bv_rep), (bp, bp_rep), (bl, bl_rep), (wl_in, wl_rep[0:DM, :]),
                                 (wl_in_r, wl_rep[DM:D, :]), (ww, ww_rep), (mask, mask_in), (ident, ident_in)):
                    sp.dma_start(dst[:], src).then_inc(s_const, 16)
                sp.dma_start(kron[HQ:HQ + 1, :], bw_rep).then_inc(s_const, 16)

            def load_tokens(i):
                sp.dma_start(tok[:, 0, :], txt[bass.ds(i, 1)].rearrange("a t d -> (a t) d")).then_inc(s_tok, 16)
                sp.dma_start(tok[0:NC, 1, :], h0[bass.ds(i, 1)].rearrange("a t d -> (a t) d")).then_inc(s_tok, 16)

            def step(i, u):
                if has(i - 1):
                    wait(sp, s_resb, 2 * (i - 1))
                    sp.dma_start(res[:, 0, :], txt[bass.ds(i - 1, 1)].rearrange("a t d -> (a t) d")).then_inc(s_res, 16)
                    sp.dma_start(res[0:NC, 1, :], h0[bass.ds(i - 1, 1)].rearrange("a t d -> (a t) d")
                                 ).then_inc(s_res, 16)
                if has(i - 3):
                    out_image(i - 3)
                if has(i + 3):
                    sp.wait_ge(s_xhat, 2 * (i + 3))
                    load_tokens(i + 3)

            def out_image(i):
                sp.wait_ge(s_h1, 2 * i + 2)
                row = h1[bass.ds(i, 1)].rearrange("a t d -> (a t) d")
                sp.dma_start(row[NC:S, :], hout[:, 0, :]).then_inc(s_store, 16)
                sp.dma_start(row[0:NC, :], hout[0:NC, 1, :]).then_inc(s_store, 16)

            load_tokens(0)
            for i in range(-2, 4):
                step(i, 0)
            with sp.Fori(4, B - 3) as i:
                step(i, 0)
            for i in range(B - 3, B + 2):
                step(i, 0)
            out_image(B - 1)
            sp.wait_ge(s_store, 32 * B)

        @block.gpsimd
        def _(pool):
            zeroed = [x[0], x[1], x[2], k_hi, k_lo, k_r2, k_rlo, q, q_r, vz_hi, vz_lo, vz_r2, vz_rlo, a_r, o[0], o[1],
                      o[2]]
            for t in zeroed:
                pool.memset(t[:].bitcast(F32), 0.0).then_inc(s_zero, 1)
            pool.memset(moments[:], 1.0).then_inc(s_zero, 1)
            pool.memset(half_neg[:], -0.5).then_inc(s_zero, 1)
            pool.memset(eps[:], EPS).then_inc(s_zero, 1)
            assert len(zeroed) + 5 == N_ZERO
            pool.wait_ge(s_zero, N_ZERO)

            def rest_queries(i, pa, g_range):
                for g in g_range:
                    pool.tensor_tensor(head(qg_r[0:DR, pa, :], g), tiles(q_r[:]),
                                       wls_r[:, g:g + 1].rearrange("p (a b) -> p a b", b=1).to_broadcast([DR, TILES, QS]),
                                       ALU.mult).then_inc(s_qgr, 1)

            rest_share = {0: range(0, 3), 1: range(3, 5), 2: range(5, 7), 3: range(7, 10), 4: range(10, H)}

            def slot(i, u, j):
                pa = par(u)
                if j > 0 and j in rest_share and has(i + 1):
                    rest_queries(i + 1, 1 - pa, rest_share[j])
                if has(i):
                    b, nt = j % 2, len(group_tiles(j))
                    bias = bl[:].to_broadcast([HQ, nt])
                    pool.wait_ge(s_max, GROUPS * i + j + 1)
                    pool.tensor_tensor(lifted[:, b, 0:nt], neg_max[:, b, 0:nt], bias, ALU.subtract).then_inc(s_lift, 1)
                    pool.wait_ge(s_lift, GROUPS * i + j + 1)
                    pool.tensor_tensor(shift[:, b, 0:nt], lifted[:, b, 0:nt], bias, ALU.add).then_inc(s_shift, 1)
                n, _, jp = ago(i, u, j, 1)
                if has(n):
                    b, nt = jp % 2, len(group_tiles(jp))
                    pool.wait_ge(s_scale, GROUPS * n + jp + 1)
                    pool.tensor_tensor(ex[:, b, 0:nt, :], ex[:, b, 0:nt, :], scale[:, b, 0:nt].rearrange(
                        "p (t a) -> p t a", a=1).to_broadcast([HQ, nt, S]), ALU.mult).then_inc(s_norm, 1)
                if j == 1 and has(i - 1):
                    src = v[:, 1 - pa, 0, :].rearrange("p (g d) -> p g d", d=DH)
                    src_r = v[0:NC, 1 - pa, 1, :].rearrange("p (g d) -> p g d", d=DH)
                    pool.wait_ge(s_vzc, 3 * i)
                    pool.tensor_tensor(win(vz_lo, 0, NT), src, f(win(vz_hi, 0, NT)), ALU.subtract).then_inc(s_vz, 1)
                    pool.tensor_tensor(win(vz_rlo, 0, NC), src_r, f(win(vz_r2, 0, NC)), ALU.subtract).then_inc(s_vz, 1)
                if j == 2 and has(i + 2):
                    centre(i + 2)
                if j == 3 and has(i + 2):
                    normalise(i + 2)
                if j == 0 and has(i + 1):
                    pool.wait_ge(s_q, 2 * (i + 2))
                    wait(pool, s_s, GROUPS * i)
                    rest_queries(i + 1, 1 - pa, rest_share[j])
                if j == 5 and has(i - 1):
                    pool.wait_ge(s_res, 32 * i)
                    wait(pool, s_h1, 2 * (i - 1))
                    pool.tensor_tensor(resb[:, 0, :], res[:, 0, :], bp[:], ALU.add).then_inc(s_resb, 1)
                    pool.tensor_tensor(resb[0:NC, 1, :], res[0:NC, 1, :], bp[0:NC, :], ALU.add).then_inc(s_resb, 1)

            def step(i, u):
                for j in range(GROUPS):
                    slot(i, u, j)

            def centre(n):
                pool.wait_ge(s_mom, 2 * (n + 1))
                pool.tensor_tensor(var_eps[:], moments[:, :, 1], eps[:], ALU.add).then_inc(s_veps, 1)
                wait(pool, s_xhat, 2 * n)
                for t, rows in ((0, NT), (1, NC)):
                    pool.tensor_tensor(centred[0:rows, t, :], tok[0:rows, t, :],
                                       moments[0:rows, t, 0:1].to_broadcast([rows, D]), ALU.subtract).then_inc(s_xc, 1)
                pool.wait_ge(s_veps, n + 1)
                pool.tensor_tensor(rstd[:], var_eps[:], half_neg[:], ALU.pow).then_inc(s_rstd, 1)

            def normalise(n):
                pool.wait_ge(s_xc, 2 * (n + 1))
                pool.wait_ge(s_rstd, n + 1)
                wait(pool, s_t, n)
                for t, rows in ((0, NT), (1, NC)):
                    pool.tensor_tensor(xhat[0:rows, t, :], centred[0:rows, t, :],
                                       rstd[0:rows, t:t + 1].to_broadcast([rows, D]), ALU.mult).then_inc(s_xhat, 1)
            steps(pool, step)

        @block.scalar
        def _(act):
            act.wait_ge(s_const, 16 * N_LOADS)
            cuts = ((wqk, 0, NQK), (wv, NQK, NQK + D), (wo, NQK + D, NQK + 2 * D))
            for w, a, b in cuts:
                act.activation(w.hi[:], w_in[:, a:b], ACT.Copy).then_inc(s_whi, 1)
                act.activation(w.rest2[:], w_in_r[:, a:b], ACT.Copy).then_inc(s_whi, 1)
            act.wait_ge(s_prep, 2)
            act.activation(kron_h[:], kron[:], ACT.Copy).then_inc(s_whi, 1)
            act.wait_ge(s_zero, N_ZERO)

            def slot(i, u, j):
                pa = par(u)
                n, pn, ja = ago(i, u, j, 3)
                if has(n):
                    act.wait_ge(s_m, GROUPS * n + ja + 1)
                    if ja == 0:
                        wait(act, s_av, n - 1)
                    act.activation(mixed(a_hi[:, pn, :], ja), mix_bank(ps_m[ja % 2], ja, NT), ACT.Copy).then_inc(s_ahi, 1)
                    act.activation(mixed(a_r[0:NC, pn, :], ja), mix_bank(ps_mr[ja % 2], ja, NC), ACT.Copy
                                   ).then_inc(s_ahi, 1)
                if j == 1 and has(i - 2):
                    act.wait_ge(s_av, i - 1)
                    wait(act, s_pr, i - 2)
                    act.activation(o[0][:, 0:S], ps_o[0:DM, 0:S], ACT.Copy).then_inc(s_ohi, 1)
                    act.activation(o[2][0:DR, 0:S], ps_o[0:DR, SE:SE + S], ACT.Copy).then_inc(s_ohi, 1)
                if j == 1 and has(i - 1):
                    wait(act, s_av, i - 1)
                    act.wait_ge(s_v, 2 * i)
                    src_r = v[0:NC, 1 - pa, 1, :].rearrange("p (g d) -> p g d", d=DH)
                    act.activation(win(vz_hi, 0, NT), v[:, 1 - pa, 0, :].rearrange("p (g d) -> p g d", d=DH), ACT.Copy
                                   ).then_inc(s_vzc, 1)
                    act.activation(win(vz_r2, 0, NC), src_r, ACT.Copy).then_inc(s_vzc, 1)
                    act.activation(win(vz_r2, 64, 64 + NC), src_r, ACT.Copy).then_inc(s_vzc, 1)
                if j == 0 and has(i + 1):
                    pk = 1 - pa
                    km, kr = ps_q[:, SE:SE + S], ps_q[DR:2 * DR, 2 * SE:2 * SE + S]
                    act.wait_ge(s_qk, i + 2)
                    wait(act, s_qgl, 2 * H * (i + 1))
                    wait(act, s_qgr, H * (i + 1))
                    act.activation(q[:, 0:S], ps_q[:, 0:S], ACT.Identity, bias=bq[:]).then_inc(s_q, 1)
                    act.activation(q_r[:, 0:S], ps_q[0:DR, 2 * SE:2 * SE + S], ACT.Identity, bias=bqr[:]
                                   ).then_inc(s_q, 1)
                    wait(act, s_s, GROUPS * i)
                    act.activation(k_r2[DR:, pk, 0:S], kr, ACT.Identity, bias=bkr[DR:, :]).then_inc(s_khi, 1)
                    act.activation(k_hi[:, pk, 0:S], km, ACT.Identity, bias=bk[:]).then_inc(s_khi, 1)
                    act.activation(k_r2[0:DR, pk, 0:S], kr, ACT.Identity, bias=bkr[DR:, :]).then_inc(s_khi, 1)
                if j == 4 and has(i + 2):
                    act.wait_ge(s_t, i + 3)
                    wait(act, s_vmm, i + 2)
                    act.activation(x[0][:, 0:S], ps_q[:, 0:S], ACT.Copy).then_inc(s_xhi, 1)
                    act.activation(x[2][0:DR, 0:S], ps_q[0:DR, SE:SE + S], ACT.Copy).then_inc(s_xhi, 1)
                if j in share and has(i + 1):
                    if j == 0:
                        act.wait_ge(s_q, 2 * (i + 2))
                    for g in share[j]:
                        act.activation(head(qg_hi[:, 1 - pa, :], g), tiles(q[:]), ACT.Copy, scale=wls[:, g:g + 1]
                                       ).then_inc(s_qgh, 1)
                if has(i):
                    b = j % 2
                    act.wait_ge(s_shift, GROUPS * i + j + 1)
                    wait(act, s_plo, GROUPS * i + j - 1)
                    for k, t in enumerate(group_tiles(j)):
                        last = act.activation(ex[:, b, k, :], ps_s[b][0:HQ, k * SE:k * SE + S], ACT.Exp,
                                              bias=shift[:, b, k:k + 1], accum_out=total[:, b, k:k + 1])
                    last.then_inc(s_exp, 1)
                n, pn, jp = ago(i, u, j, 1)
                if has(n):
                    act.wait_ge(s_norm, GROUPS * n + jp + 1)
                    wait(act, s_m, GROUPS * n + jp - 1)
                    b, nt = jp % 2, len(group_tiles(jp))
                    act.activation(p_hi[0:HQ, b, 0:nt, :], ex[:, b, 0:nt, :], ACT.Copy).then_inc(s_phi, 1)

            def step(i, u):
                for j in range(GROUPS):
                    slot(i, u, j)
            steps(act, step)

        @block.vector
        def _(dve):
            dve.memset(f(p_lo[96:128, :, :, :]), 0.0).then_inc(s_zero, 1)
            dve.memset(f(p_hi[96:128, :, :, :]), 1.0).then_inc(s_zero, 1)
            dve.wait_ge(s_const, 16 * N_LOADS)
            dve.tensor_scalar(wls[:], wl_in[:], DH ** -0.5, None, ALU.mult).then_inc(s_prep, 1)
            dve.tensor_tensor(kron[0:HQ, :].rearrange("p (g s) -> p g s", s=QS),
                              ww[:].rearrange("p (g a) -> p g a", a=1).to_broadcast([HQ, H, QS]),
                              mask[:].rearrange("p (a s) -> p a s", a=1).to_broadcast([HQ, H, QS]), ALU.mult
                              ).then_inc(s_prep, 1)
            dve.tensor_scalar(wls_r[:], wl_in_r[:], DH ** -0.5, None, ALU.mult).then_inc(s_prep, 1)
            dve.wait_ge(s_whi, 7)
            cuts = ((wqk, 0, NQK), (wv, NQK, NQK + D), (wo, NQK + D, NQK + 2 * D))
            for w, a, b in cuts:
                dve.tensor_tensor(w.lo[:], w_in[:, a:b], f(w.hi[:]), ALU.subtract).then_inc(s_wlo, 1)
                dve.tensor_tensor(w.rest_lo[:], w_in_r[0:DR, a:b], f(w.rest2[0:DR, :]), ALU.subtract).then_inc(s_wlo, 1)
            dve.tensor_tensor(kron_l[:], kron[:], f(kron_h[:]), ALU.subtract).then_inc(s_wlo, 1)
            dve.wait_ge(s_zero, N_ZERO)
            dve.wait_ge(s_prep, 3)

            def slot(i, u, j):
                pa = par(u)
                if has(i):
                    b, nt = j % 2, len(group_tiles(j))
                    dve.wait_ge(s_s, GROUPS * i + j + 1)
                    dve.tensor_reduce(out=neg_max[:, b, 0:nt], in_=ps_s[b][0:HQ, 0:nt * SE].rearrange(
                        "p (t k) -> p t k", k=SE)[:, :, 0:S], op=ALU.max, axis=AX_X, negate=True).then_inc(s_max, 1)
                n, pn, jp = ago(i, u, j, 1)
                if has(n):
                    b, nt = jp % 2, len(group_tiles(jp))
                    dve.wait_ge(s_exp, GROUPS * n + jp + 1)
                    dve.reciprocal(scale[:, b, 0:nt], total[:, b, 0:nt]).then_inc(s_scale, 1)
                n, pn, ja = ago(i, u, j, 3)
                if has(n):
                    dve.wait_ge(s_ahi, 2 * (GROUPS * n + ja) + 2)
                    dve.tensor_tensor(mixed(a_lo[:, pn, :], ja), mix_bank(ps_m[ja % 2], ja, NT),
                                      f(mixed(a_hi[:, pn, :], ja)), ALU.subtract).then_inc(s_alo, 1)
                    dve.tensor_tensor(mixed(a_r[64:64 + NC, pn, :], ja), mix_bank(ps_mr[ja % 2], ja, NC),
                                      f(mixed(a_r[0:NC, pn, :], ja)), ALU.subtract).then_inc(s_alo, 1)
                if j == 0 and has(i + 1):
                    pk = 1 - pa
                    km, kr = ps_q[:, SE:SE + S], ps_q[DR:2 * DR, 2 * SE:2 * SE + S]
                    dve.wait_ge(s_khi, 3 * (i + 2))
                    dve.scalar_tensor_tensor(out=k_rlo[:, pk, 0:S], in0=kr, scalar=bkr[DR:, :], in1=f(k_r2[DR:, pk, 0:S]),
                                             op0=ALU.add, op1=ALU.subtract).then_inc(s_klo, 1)
                    dve.scalar_tensor_tensor(out=k_lo[:, pk, 0:S], in0=km, scalar=bk[:], in1=f(k_hi[:, pk, 0:S]),
                                             op0=ALU.add, op1=ALU.subtract).then_inc(s_klo, 1)
                if j == 1 and has(i - 2):
                    dve.wait_ge(s_ohi, 2 * (i - 1))
                    dve.tensor_tensor(o[1][:, 0:S], ps_o[0:DM, 0:S], f(o[0][:, 0:S]), ALU.subtract).then_inc(s_olo, 1)
                    dve.tensor_tensor(o[2][DR:2 * DR, 0:S], ps_o[0:DR, SE:SE + S], f(o[2][0:DR, 0:S]), ALU.subtract
                                      ).then_inc(s_olo, 1)
                if j == 2 and has(i + 1):
                    dve.wait_ge(s_vmm, i + 2)
                    wait(dve, s_vz, 2 * i)
                    dve.tensor_tensor(v[:, 1 - pa, 0, :], ps_q[:, 0:D], bv[:], ALU.add).then_inc(s_v, 1)
                    dve.tensor_tensor(v[0:NC, 1 - pa, 1, :], ps_q[0:NC, D:2 * D], bv[0:NC, :], ALU.add).then_inc(s_v, 1)
                if j == 3 and has(i - 2):
                    dve.wait_ge(s_pr, i - 1)
                    dve.wait_ge(s_resb, 2 * (i - 1))
                    wait(dve, s_store, 32 * (i - 2))
                    dve.tensor_tensor(hout[:, 0, :], ps_o[:, 0:D], resb[:, 0, :], ALU.add).then_inc(s_h1, 1)
                    dve.tensor_tensor(hout[0:NC, 1, :], ps_o[0:NC, D:2 * D], resb[0:NC, 1, :], ALU.add).then_inc(s_h1, 1)
                if j == 4 and has(i + 2):
                    dve.wait_ge(s_xhi, 2 * (i + 3))
                    dve.tensor_tensor(x[1][:, 0:S], ps_q[:, 0:S], f(x[0][:, 0:S]), ALU.subtract).then_inc(s_xlo, 1)
                    dve.tensor_tensor(x[2][DR:, 0:S], ps_q[0:DR, SE:SE + S], f(x[2][0:DR, 0:S]), ALU.subtract
                                      ).then_inc(s_xlo, 1)
                if j == 1 and has(i + 2):
                    dve.wait_ge(s_tok, 32 * (i + 3))
                    wait(dve, s_xhat, 2 * (i + 2))
                    dve.bn_stats(stats[:, 0, :], tok[:, 0, :]).then_inc(s_stats, 1)
                    dve.bn_stats(stats[0:NC, 1, :], tok[0:NC, 1, :]).then_inc(s_stats, 1)
                if j in share and has(i + 1):
                    for g in share[j]:
                        moments_next = j == 1 and g == share[j][0] and has(i + 2)
                        dve.wait_ge(s_qgh, H * (i + 1) + g + 1)
                        dve.scalar_tensor_tensor(out=head(qg_lo[:, 1 - pa, :], g), in0=tiles(q[:]), scalar=wls[:, g:g + 1],
                                                 in1=f(head(qg_hi[:, 1 - pa, :], g)), op0=ALU.mult, op1=ALU.subtract
                                                 ).then_inc(s_qgl, 1)
                        dve.wait_ge(s_qgr, H * (i + 1) + g + 1)
                        if moments_next:
                            dve.wait_ge(s_stats, 2 * (i + 3))
                        dve.scalar_tensor_tensor(out=head(qg_r[DR:2 * DR, 1 - pa, :], g), in0=tiles(q_r[:]),
                                                 scalar=wls_r[:, g:g + 1], in1=f(head(qg_r[0:DR, 1 - pa, :], g)),
                                                 op0=ALU.mult, op1=ALU.subtract).then_inc(s_qgl, 1)
                        if moments_next:
                            aggregate()
                elif j == 1 and has(i + 2):
                    dve.wait_ge(s_stats, 2 * (i + 3))
                    aggregate()
                n, pn, jp = ago(i, u, j, 1)
                if has(n):
                    b, nt = jp % 2, len(group_tiles(jp))
                    wait(dve, s_m, GROUPS * n + jp - 1)
                    dve.wait_ge(s_phi, GROUPS * n + jp + 1)
                    dve.tensor_tensor(p_lo[0:HQ, b, 0:nt, :], ex[:, b, 0:nt, :], f(p_hi[0:HQ, b, 0:nt, :]), ALU.subtract
                                      ).then_inc(s_plo, 1)

            def aggregate():
                dve.bn_aggr(moments[:, 0, :], stats[:, 0, :]).then_inc(s_mom, 1)
                dve.bn_aggr(moments[0:NC, 1, :], stats[0:NC, 1, :]).then_inc(s_mom, 1)

            def step(i, u):
                for j in range(GROUPS):
                    slot(i, u, j)
            steps(dve, step)

        @block.tensor
        def _(pe):
            pe.wait_ge(s_wlo, 7)
            pe.wait_ge(s_zero, N_ZERO)

            def logits(i, pa, j):
                if j == 0:
                    pe.wait_ge(s_qgl, 2 * H * (i + 1))
                    pe.wait_ge(s_klo, 2 * (i + 1))
                wait(pe, s_exp, GROUPS * i + j - 1)
                for n, t in enumerate(group_tiles(j)):
                    out = ps_s[j % 2][0:HQ, n * SE:(n + 1) * SE]
                    hi, lo, rest = (z[:, pa, t * HQ:(t + 1) * HQ] for z in (qg_hi, qg_lo, qg_r))
                    pe.matmul(out, hi, k_hi[:, pa, :], start=True, stop=False)
                    pe.matmul(out, lo, k_hi[:, pa, :], start=False, stop=False)
                    pe.matmul(out, hi, k_lo[:, pa, :], start=False, stop=False)
                    pe.matmul(out, rest, k_r2[:, pa, :], start=False, stop=False)
                    last = pe.matmul(out, rest[0:DR], k_rlo[:, pa, :], start=False, stop=True)
                last.then_inc(s_s, 1)

            def mix(i, j):
                b = j % 2
                pe.wait_ge(s_plo, GROUPS * i + j + 1)
                wait(pe, s_alo, 2 * (GROUPS * i + j - 1))
                for bank_, rows, cols in ((ps_m[b], NT, slice(0, NT)), (ps_mr[b], NC, slice(NT, S))):
                    for n, t in enumerate(group_tiles(j)):
                        out = bank_[0:rows, n * HQ:(n + 1) * HQ]
                        pe.matmul(out, p_hi[0:HQ + 1, b, n, cols], kron_h[:], start=True, stop=False)
                        pe.matmul(out, p_lo[0:HQ + 1, b, n, cols], kron_h[:], start=False, stop=False)
                        last = pe.matmul(out, p_hi[0:HQ + 1, b, n, cols], kron_l[:], start=False, stop=True)
                last.then_inc(s_m, 1)

            def values(i, pa, g_range):
                for g in g_range:
                    rows, gg, at = (DM, g, 0) if g < DM // DH else (DR, g - DM // DH, SE)
                    w = slice(g * VW + VW - DH * (gg + 1), g * VW + VW - DH * (gg + 1) + rows)
                    c = slice(g * SQ, g * SQ + SE)
                    out = ps_o[0:rows, at:at + SE]
                    pe.matmul(out, vz_hi[:, w], a_hi[:, pa, c], start=(gg == 0), stop=False)
                    pe.matmul(out, vz_lo[:, w], a_hi[:, pa, c], start=False, stop=False)
                    pe.matmul(out, vz_hi[:, w], a_lo[:, pa, c], start=False, stop=False)
                    pe.matmul(out, vz_r2[0:64 + NC, w], a_r[0:64 + NC, pa, c], start=False, stop=False)
                    last = pe.matmul(out, vz_rlo[:, w], a_r[0:NC, pa, c], start=False,
                                     stop=(g in (DM // DH - 1, H - 1)))
                return last

            def slot(i, u, j):
                pa = par(u)
                n, js, ps = (i, j + 1, pa) if j < GROUPS - 1 else (i + 1, 0, 1 - pa)
                if has(n):
                    logits(n, ps, js)
                n, _, jm = ago(i, u, j, 2)
                if has(n):
                    mix(n, jm)
                if j == 0 and has(i - 2):
                    values(i - 2, pa, range(9, H)).then_inc(s_av, 1)
                if j == 1 and has(i + 1):
                    pe.wait_ge(s_klo, 2 * (i + 2))
                    product(pe, ps_q[0:NT, 0:D], x, wv, slice(0, NT), slice(0, D), True)
                    product(pe, ps_q[0:NC, D:2 * D], x, wv, slice(NT, S), slice(0, D), True).then_inc(s_vmm, 1)
                if j == 2 and has(i - 2):
                    pe.wait_ge(s_olo, 2 * (i - 1))
                    product(pe, ps_o[0:NT, 0:D], o, wo, slice(0, NT), slice(0, D), True)
                    product(pe, ps_o[0:NC, D:2 * D], o, wo, slice(NT, S), slice(0, D), True).then_inc(s_pr, 1)
                if j == 3 and has(i - 1):
                    pe.wait_ge(s_alo, 2 * GROUPS * i)
                    pe.wait_ge(s_vz, 2 * i)
                    wait(pe, s_h1, 2 * (i - 1))
                if j >= 3 and has(i - 1):
                    values(i - 1, 1 - pa, {3: range(0, 3), 4: range(3, 7), 5: range(7, 9)}[j])
                if j == 3 and has(i + 2):
                    pe.wait_ge(s_xhat, 2 * (i + 3))
                    wait(pe, s_v, 2 * (i + 2))
                    for t, rows in ((0, NT), (1, NC)):
                        pe.transpose(ps_q[0:DM, t * NT:t * NT + rows], xhat[0:rows, t, 0:DM], ident[0:rows, 0:rows])
                        last = pe.transpose(ps_q[0:DR, SE + t * NT:SE + t * NT + rows], xhat[0:rows, t, DM:D],
                                            ident[0:rows, 0:rows])
                    last.then_inc(s_t, 1)
                if j == 5 and has(i + 2):
                    pe.wait_ge(s_xlo, 2 * (i + 3))
                    for n in range(3):
                        last = product(pe, ps_q[:, n * SE:(n + 1) * SE], x, wqk, slice(0, SE),
                                       slice(n * 128, (n + 1) * 128), False)
                    last.then_inc(s_qk, 1)

            def warm_up(i):
                pe.wait_ge(s_exp, GROUPS * i)
                for n in range(16):
                    pe.matmul(ps_s[1][:, 0:NQK], wqk.hi[:, 0:128], wqk.hi[:], start=True, stop=True)

            def step(i, u):
                if isinstance(i, int) and i == 1:
                    warm_up(i)
                for j in range(GROUPS):
                    slot(i, u, j)
            steps(pe, step)


N_LOADS = 15 + 3 + 4 + 8 + 1
N_ZERO = 17 + 5


def experts(nc, h1, out, sg, su, sd, rg, ru, rd, router_rep, rbias_rep, ident_in):
    ctx = ExitStack()
    with ctx:
        def sb(name, shape, dt=F32):
            return ctx.enter_context(nc.sbuf_tensor("ex_" + name, shape, dt))

        def sem(name):
            return ctx.enter_context(nc.semaphore("ex_" + name))

        bank = [ctx.enter_context(nc.psum_tensor(f"ex_bank{n}", [128, 512], F32)) for n in range(8)]
        ps_g, ps_u, ps_d, ps_x, ps_xr = bank[0:2], bank[2:4], bank[4:6], bank[6], bank[7]
        NH = NF * 128
        gate, up = Split(sb, "gate", NH), Split(sb, "up", NH)
        down_h, down_l = sb("down_h", [128, NF, D], F32R), sb("down_l", [128, NF, D], F32R)
        stage, stage_r = sb("stage", [128, FT]), sb("stage_r", [128, FT])
        stage_d = sb("stage_d", [128, FT // 128, D])
        router, rbias, ident = sb("router", [TP, E, D]), sb("rbias", [TP, TT, E]), sb("ident", [128, 128])
        h = sb("h", [TP, 2, TT, D])
        stats, moments = sb("stats", [TP, TT, 6]), sb("moments", [TP, TT, 2])
        var_eps, half_neg, rstd = sb("var_eps", [TP, TT]), sb("half_neg", [TP, TT]), sb("rstd", [TP, TT])
        eps = sb("eps", [TP, TT])
        xhat, rprod = sb("xhat", [TP, TT, D]), sb("rprod", [TP, TT * E, D])
        rt = [sb(f"rt{n}", [TP, TT, E]) for n in range(6)]
        rs = [sb(f"rs{n}", [TP, TT]) for n in range(3)]
        cw = sb("cw", [TP, 2, TT, E])
        x = (sb("x_hi", [DM, CH], F32R), sb("x_lo", [DM, CH], F32R), sb("x_rest", [2 * DR, CH], F32R))
        act_g, hid = sb("act_g", [128, 2, CH]), sb("hid", [128, 2, CH])
        hid_hi, hid_lo = sb("hid_hi", [128, NF, CH], F32R), sb("hid_lo", [128, NF, CH], F32R)
        y = sb("y", [TP, 2, 4, D])

        s_w, s_wh, s_wl, s_const = sem("w"), sem("wh"), sem("wl"), sem("const")
        s_h, s_store = [sem("h0"), sem("h1")], [sem("store0"), sem("store1")]
        s_zero, s_st, s_mom, s_veps, s_rstd, s_xhat, s_t, s_xhi, s_xlo = (
            sem(n) for n in ("zero", "st", "mom", "veps", "rstd", "xhat", "t", "xhi", "xlo"))
        s_lg, s_tanh, s_r, s_cw = sem("lg"), sem("tanh"), sem("r"), sem("cw")
        s_gu, s_silu, s_hid, s_hh, s_hl, s_dn, s_y = (sem(n) for n in ("gu", "silu", "hid", "hh", "hl", "dn", "y"))

        def has(c):
            return not isinstance(c, int) or 0 <= c < CHUNKS

        def steps(eng, step):
            for c in range(-1, 1):
                step(c, c % 2, (c + 1) // 2)
            with eng.Fori(0, (CHUNKS - 2) // 2) as it:
                for u in range(2):
                    step(2 * it + u + 1, (u + 1) % 2, it + 1)
            for c in range(CHUNKS - 1, CHUNKS + 1):
                step(c, c % 2, (c + 1) // 2)

        def expert_weights(k):
            return (sg, su, sd) if k == 0 else (rg[k - 1], ru[k - 1], rd[k - 1])

        hv = h1.rearrange("b s d -> (b s) d").rearrange("(c t p) d -> c p t d", t=TT, p=TP)
        ov = out.rearrange("b s d -> (b s) d").rearrange("(c t p) d -> c p t d", t=TT, p=TP)
        block = ctx.enter_context(nc.Block())

        units = [(k, m) for k in range(4) for m in range(3)]

        def load(sp, c, u=0):
            sp.dma_start(h[:, u, :, :], hv[bass.ds(c, 1)].rearrange("a p t d -> (a p) t d")).then_inc(s_h[u], 16)

        @block.sync
        def _(sp):
            sp.dma_start(router[:], router_rep).then_inc(s_const, 16)
            sp.dma_start(rbias[:], rbias_rep).then_inc(s_const, 16)
            sp.dma_start(ident[:], ident_in).then_inc(s_const, 16)
            load(sp, 0)
            for n, (k, m) in enumerate(units):
                if n:
                    sp.wait_ge(s_wl, n)
                w = expert_weights(k)[m]
                if m < 2:
                    sp.dma_start(stage[:], w[0:DM, :]).then_inc(s_w, 16)
                    for r in range(2):
                        sp.dma_start(stage_r[r * DR:(r + 1) * DR, :], w[DM:D, :]).then_inc(s_w, 16)
                else:
                    sp.dma_start(stage_d[:], w.rearrange("(f p) d -> p f d", p=128)).then_inc(s_w, 48)

            def step(c, u, pairs):
                if has(c - 1):
                    for t in range(TT):
                        sp.wait_ge(s_y, TT * (c - 1) + t + 1)
                        sp.dma_start(ov[bass.ds(c - 1, 1), :, t, :].rearrange("a p d -> (a p) d"), y[:, t % 2, 3, :]
                                     ).then_inc(s_store[t % 2], 16)
                if has(c + 1) and not (isinstance(c, int) and c == -1):
                    load(sp, c + 1, 1 - u)
            steps(sp, step)
            for b in range(2):
                sp.wait_ge(s_store[b], 16 * CHUNKS * TT // 2)

        @block.gpsimd
        def _(pool):
            pool.memset(half_neg[:], -0.5).then_inc(s_zero, 1)
            pool.memset(eps[:], EPS).then_inc(s_zero, 1)
            pool.wait_ge(s_zero, 2)

            def step(c, u, pairs):
                if has(c + 1):
                    pool.wait_ge(s_mom, TT * (c + 2))
                    wait(pool, s_xhat, TT * (c + 1))
                    pool.tensor_tensor(var_eps[:], moments[:, :, 1], eps[:], ALU.add).then_inc(s_veps, 1)
                    pool.wait_ge(s_veps, c + 2)
                    pool.tensor_tensor(rstd[:], var_eps[:], half_neg[:], ALU.pow).then_inc(s_rstd, 1)
            steps(pool, step)

        @block.scalar
        def _(act):
            for n, (k, m) in enumerate(units):
                act.wait_ge(s_w, 48 * (n + 1))
                c = slice(k * FT, (k + 1) * FT)
                if m < 2:
                    w = (gate, up)[m]
                    act.activation(w.hi[:, c], stage[:], ACT.Copy)
                    act.activation(w.rest2[:, c], stage_r[:], ACT.Copy).then_inc(s_wh, 1)
                else:
                    act.activation(down_h[:, 3 * k:3 * k + 3, :], stage_d[:], ACT.Copy).then_inc(s_wh, 1)

            def step(c, u, pairs):
                for fi in range(NF):
                    if has(c):
                        n = NF * c + fi
                        b = fi % 2
                        act.wait_ge(s_gu, n + 1)
                        wait(act, s_hid, n - 1)
                        act.activation(act_g[:, b, :], ps_g[b][:, 0:CH], ACT.Silu).then_inc(s_silu, 1)
                        act.wait_ge(s_hid, n + 1)
                        wait(act, s_dn, TT * c) if fi == 0 else None
                        act.activation(hid_hi[:, fi, :], hid[:, b, :], ACT.Copy).then_inc(s_hh, 1)
                    if fi == 4 and has(c + 1):
                        act.wait_ge(s_lg, c + 2)
                        act.activation(rt[1][:], rt[0][:], ACT.Tanh, scale=0.5).then_inc(s_tanh, 1)
                if has(c + 1):
                    act.wait_ge(s_t, c + 2)
                    act.activation(x[0][:], ps_x[:, 0:CH], ACT.Copy).then_inc(s_xhi, 1)
                    act.activation(x[2][0:DR, :], ps_xr[0:DR, 0:CH], ACT.Copy).then_inc(s_xhi, 1)
            steps(act, step)

        @block.vector
        def _(dve):
            for n, (k, m) in enumerate(units):
                dve.wait_ge(s_wh, n + 1)
                c = slice(k * FT, (k + 1) * FT)
                if m < 2:
                    w = (gate, up)[m]
                    dve.tensor_tensor(w.lo[:, c], stage[:], f(w.hi[:, c]), ALU.subtract)
                    dve.tensor_tensor(w.rest_lo[:, c], stage_r[0:DR, :], f(w.rest2[0:DR, c]), ALU.subtract).then_inc(s_wl, 1)
                else:
                    dve.tensor_tensor(down_l[:, 3 * k:3 * k + 3, :], stage_d[:], f(down_h[:, 3 * k:3 * k + 3, :]),
                                      ALU.subtract).then_inc(s_wl, 1)
            dve.wait_ge(s_const, 48)

            def normalise(c, u, pairs):
                dve.wait_ge(s_h[u], 16 * pairs + 16)
                wait(dve, s_rstd, c)
                for t in range(TT):
                    dve.bn_stats(stats[:, t, :], h[:, u, t, :]).then_inc(s_st, 1)

            def aggregate():
                for t in range(TT):
                    dve.bn_aggr(moments[:, t, :], stats[:, t, :]).then_inc(s_mom, 1)

            def scale_tokens(c, u):
                dve.wait_ge(s_rstd, c + 1)
                wait(dve, s_t, c)
                for t in range(TT):
                    dve.tensor_scalar(xhat[:, t, :], h[:, u, t, :], moments[:, t, 0:1], rstd[:, t:t + 1],
                                      ALU.subtract, ALU.mult).then_inc(s_xhat, 1)

            def chain(op, n):
                op.then_inc(s_r, 1)
                dve.wait_ge(s_r, n)

            R = 12

            def route(c, u):
                r0 = R * c
                for t in range(TT):
                    dve.wait_ge(s_xhat, TT * c + t + 1)
                    for e in range(E):
                        last = dve.scalar_tensor_tensor(out=rprod[:, t * E + e, :], in0=xhat[:, t, :], scalar=1.0,
                                                        in1=router[:, e, :], op0=ALU.mult, op1=ALU.mult,
                                                        accum_out=rt[5][:, t, e:e + 1])
                chain(last, r0 + 1)
                dve.tensor_tensor(rt[0][:], rt[5][:], rbias[:], ALU.add).then_inc(s_lg, 1)
                dve.wait_ge(s_tanh, c + 1)
                chain(dve.tensor_scalar(rt[2][:], rt[1][:], 0.5, 0.5, ALU.mult, ALU.add), r0 + 2)
                p = [rt[2][:, :, e] for e in range(E)]
                keep = [rt[3][:, :, e] for e in range(E)]
                chain(dve.tensor_tensor(rs[0][:], p[1], p[2], ALU.min), r0 + 3)
                chain(dve.tensor_tensor(keep[0], p[0], rs[0][:], ALU.is_ge), r0 + 4)
                chain(dve.tensor_tensor(rs[1][:], p[0], p[1], ALU.min), r0 + 5)
                chain(dve.tensor_tensor(keep[2], p[2], rs[1][:], ALU.is_gt), r0 + 6)
                chain(dve.tensor_tensor(rs[2][:], keep[0], keep[2], ALU.add), r0 + 7)
                chain(dve.tensor_scalar(keep[1], rs[2][:], -1.0, 2.0, ALU.mult, ALU.add), r0 + 8)
                chain(dve.tensor_tensor(rt[4][:], rt[2][:], rt[3][:], ALU.mult), r0 + 9)
                chain(dve.tensor_reduce(out=rs[0][:], in_=rt[4][:], op=ALU.add, axis=AX_X), r0 + 10)
                chain(dve.reciprocal(rs[1][:], rs[0][:]), r0 + 11)
                chain(dve.tensor_tensor(cw[:, u, :, :], rt[4][:],
                                        rs[1][:].rearrange("p (t a) -> p t a", a=1).to_broadcast([TP, TT, E]),
                                        ALU.mult), r0 + 12)

            def combine(c, u, t):
                n = TT * c + t
                b = t % 2
                dve.wait_ge(s_dn, n + 1)
                wait(dve, s_store[b], 16 * (2 * c + t // 2))
                parts = [ps_d[0][0:TP, 0:D], ps_d[0][0:TP, D:2 * D], ps_d[1][0:TP, 0:D], ps_d[1][0:TP, D:2 * D]]
                dve.tensor_tensor(y[:, b, 0, :], parts[0], h[:, u, t, :], ALU.add).then_inc(s_cw, 1)
                for e in range(E):
                    dve.wait_ge(s_cw, 3 * n + e + 1)
                    last = dve.scalar_tensor_tensor(out=y[:, b, e + 1, :], in0=parts[e + 1], scalar=cw[:, u, t, e:e + 1],
                                                    in1=y[:, b, e, :], op0=ALU.mult, op1=ALU.add)
                    last.then_inc(s_cw if e < E - 1 else s_y, 1)

            def step(c, u, pairs):
                for fi in range(NF):
                    if has(c):
                        n = NF * c + fi
                        b = fi % 2
                        dve.wait_ge(s_silu, n + 1)
                        wait(dve, s_hl, n - 1)
                        wait(dve, s_hh, n - 1)
                        dve.tensor_tensor(hid[:, b, :], act_g[:, b, :], ps_u[b][:, 0:CH], ALU.mult).then_inc(s_hid, 1)
                        dve.wait_ge(s_hh, n + 1)
                        if fi == 0:
                            wait(dve, s_dn, TT * c)
                        if fi == 2 and has(c + 1):
                            dve.wait_ge(s_st, TT * (c + 2))
                        dve.tensor_tensor(hid_lo[:, fi, :], hid[:, b, :], f(hid_hi[:, fi, :]), ALU.subtract
                                          ).then_inc(s_hl, 1)
                    if fi == 1 and has(c + 1):
                        normalise(c + 1, 1 - u, pairs)
                    if fi == 2 and has(c + 1):
                        if not has(c):
                            dve.wait_ge(s_st, TT * (c + 2))
                        aggregate()
                    if fi == 4 and has(c + 1):
                        scale_tokens(c + 1, 1 - u)
                        route(c + 1, 1 - u)
                if has(c + 1):
                    dve.wait_ge(s_xhi, 2 * (c + 2))
                    dve.tensor_tensor(x[1][:], ps_x[:, 0:CH], f(x[0][:]), ALU.subtract).then_inc(s_xlo, 1)
                    dve.tensor_tensor(x[2][DR:, :], ps_xr[0:DR, 0:CH], f(x[2][0:DR, :]), ALU.subtract).then_inc(s_xlo, 1)
                if has(c):
                    for t in range(TT):
                        combine(c, u, t)
            steps(dve, step)

        @block.tensor
        def _(pe):
            pe.wait_ge(s_wl, len(units))
            pe.wait_ge(s_const, 48)

            def step(c, u, pairs):
                if has(c):
                    pe.wait_ge(s_xlo, 2 * (c + 1))
                for fi in range(NF):
                    if has(c):
                        n = NF * c + fi
                        b = fi % 2
                        cols = slice(fi * 128, (fi + 1) * 128)
                        wait(pe, s_hid, n - 1)
                        product(pe, ps_g[b][:, 0:CH], x, gate, slice(0, CH), cols, False)
                        product(pe, ps_u[b][:, 0:CH], x, up, slice(0, CH), cols, False).then_inc(s_gu, 1)
                if has(c + 1):
                    pe.wait_ge(s_xhat, TT * (c + 2))
                    wait(pe, s_xlo, 2 * (c + 1))
                    for t in range(TT):
                        pe.transpose(ps_x[:, t * TP:(t + 1) * TP], xhat[:, t, 0:DM], ident[0:TP, 0:TP])
                        last = pe.transpose(ps_xr[0:DR, t * TP:(t + 1) * TP], xhat[:, t, DM:D], ident[0:TP, 0:TP])
                    last.then_inc(s_t, 1)
                if has(c):
                    for t in range(TT):
                        n = TT * c + t
                        pe.wait_ge(s_hl, NF * (c + 1))
                        wait(pe, s_y, n)
                        cols = slice(t * TP, (t + 1) * TP)
                        for k in range(4):
                            o = ps_d[k // 2][0:TP, (k % 2) * D:(k % 2 + 1) * D]
                            for fi in range(3 * k, 3 * k + 3):
                                pe.matmul(o, hid_hi[:, fi, cols], down_h[:, fi, :], start=(fi == 3 * k), stop=False)
                                pe.matmul(o, hid_lo[:, fi, cols], down_h[:, fi, :], start=False, stop=False)
                                last = pe.matmul(o, hid_hi[:, fi, cols], down_l[:, fi, :], start=False,
                                                 stop=(fi == 3 * k + 2))
                        last.then_inc(s_dn, 1)
            steps(pe, step)


def build(nc, a, out):
    h0 = nc.dram_tensor("h0_scratch", [B, NC, D], F32, kind="Internal").ap()
    h1 = nc.dram_tensor("h1_scratch", [B, S, D], F32, kind="Internal").ap()
    embed_patches(nc, a["xT"], a["w_proj"], a["pos_rep"], a["b_rep"], a["cls_rep"], a["pos0_rep"], h0)
    attention(nc, a["txt"], h0, h1, a["wqkv"], a["bqkv"], a["bv_rep"], a["wl_rep"], a["bl_rep"], a["ww_rep"],
              a["bw_rep"], a["wp"], a["bp_rep"], a["ident"], a["mask"])
    experts(nc, h1, out, a["sg"], a["su"], a["sd"], a["rg"], a["ru"], a["rd"], a["router_rep"], a["rbias_rep"],
            a["ident"])


def layout(inputs):
    import numpy as np

    g = {k: np.asarray(v) for k, v in inputs.items()}
    P = 16
    n = 96 // P
    x = g["x"].reshape(B, n, P, n, P, 3).transpose(0, 1, 3, 2, 4, 5).reshape(B // 2, EMB, KD, 128)
    pos = g["L0_tok_pos_embedding"]
    bqkv = g["L0_attn_bqkv"]
    rows = np.arange(HQ)
    return {
        "xT": x.transpose(0, 3, 2, 1).reshape(B // 2, 128, KD * EMB),
        "w_proj": g["L0_tok_W_proj"],
        "pos_rep": np.concatenate([pos[1:], pos[1:]]),
        "b_rep": np.broadcast_to(g["L0_tok_b_proj"], (EMB, D)),
        "cls_rep": np.broadcast_to(g["L0_tok_cls_token"].reshape(1, D), (B, D)),
        "pos0_rep": np.broadcast_to(pos[0:1], (B, D)),
        "txt": g["txt"],
        "wqkv": g["L0_attn_Wqkv"],
        "bqkv": bqkv,
        "bv_rep": np.broadcast_to(bqkv[2 * D:], (128, D)),
        "wl_rep": np.repeat(g["L0_attn_Wl"], DH, axis=0),
        "bl_rep": np.repeat(g["L0_attn_bl"], QS).reshape(HQ, 1),
        "ww_rep": np.repeat(g["L0_attn_Ww"], QS, axis=0),
        "bw_rep": np.repeat(g["L0_attn_bw"], QS).reshape(1, HQ),
        "wp": g["L0_attn_Wproj"],
        "bp_rep": np.broadcast_to(g["L0_attn_bproj"], (128, D)),
        "ident": np.eye(128, dtype=np.float32),
        "mask": (rows[:, None] % QS == np.arange(QS)[None]).astype(np.float32),
        "sg": g["L0_ffn_shared_gate"], "su": g["L0_ffn_shared_up"], "sd": g["L0_ffn_shared_down"],
        "rg": g["L0_ffn_routed_gate"], "ru": g["L0_ffn_routed_up"], "rd": g["L0_ffn_routed_down"],
        "router_rep": np.broadcast_to(g["L0_ffn_router_w"].T, (TP, E, D)),
        "rbias_rep": np.broadcast_to(g["L0_ffn_routing_bias"], (TP, TT, E)),
    }


def kernel(**inputs):
    import numpy as np
    import concourse.bacc as bacc
    from concourse.bass_utils import run_bass_kernel_spmd

    nc = bacc.Bacc("TRN2", target_bir_lowering=False, num_devices=1)
    arrays, aps = {}, {}
    for name, a in layout(inputs).items():
        arrays["in_" + name] = np.ascontiguousarray(a)
        aps[name] = nc.dram_tensor("in_" + name, a.shape, mybir.dt.from_np(a.dtype), kind="ExternalInput").ap()
    out = nc.dram_tensor("out_0", [B, S, D], F32, kind="ExternalOutput").ap()
    build(nc, aps, out)
    r = run_bass_kernel_spmd(nc, [arrays], core_ids=[0])
    return r.results[0]["out_0"]
```

```python
import concourse.bass as bass
from concourse import mybir
from contextlib import ExitStack

F32 = mybir.dt.float32
F32R = mybir.dt.float32r
ACT = mybir.ActivationFunctionType
ALU = mybir.AluOpType
AX_X = mybir.AxisListType.X

B = 64
D = 192
NT = 128
NP = 36
NC = NP + 1
S = NT + NC
SE = S + 1
H = 12
DH = D // H
DM = 128
DR = D - DM
QS = 10
HQ = H * QS
TILES = -(-S // QS)
SQ = TILES * QS
GROUP = 3
GROUPS = -(-TILES // GROUP)
EPS = 1e-5
KD = 768 // 128
EMB = 2 * NP
RING = 4
NQK = 2 * D
HB = DR // DH
VW = DR
VZ = H * VW + VW - DH

FT = 384
E = 3
TP = 120
TT = 4
CH = TP * TT
CHUNKS = B * S // CH
NF = 4 * FT // 128
NH = NF * 128


def group_tiles(j):
    return range(j * GROUP, min(TILES, (j + 1) * GROUP))


def wait(eng, sem, value):
    if isinstance(value, int) and value <= 0:
        return
    eng.wait_ge(sem, value)


def f(ap):
    return ap.bitcast(F32)


class Split:

    def __init__(self, sb, name, n):
        self.hi = sb(name + "_hi", [DM, n], F32R)
        self.lo = sb(name + "_lo", [DM, n], F32R)
        self.rest2 = sb(name + "_rest2", [2 * DR, n], F32R)
        self.rest_lo = sb(name + "_rest_lo", [DR, n], F32R)


def product(pe, out, a, b, a_cols, b_cols, moving_weights):
    xh, xl, xr, w = a[0], a[1], a[2], b
    pairs = [(xh[:, a_cols], w.hi[:, b_cols]), (xl[:, a_cols], w.hi[:, b_cols]), (xh[:, a_cols], w.lo[:, b_cols]),
             (xr[:, a_cols], w.rest2[:, b_cols]), (xr[0:DR, a_cols], w.rest_lo[:, b_cols])]
    last = None
    for n, (x, y) in enumerate(pairs):
        lhs, rhs = (x, y) if moving_weights else (y, x)
        last = pe.matmul(out, lhs, rhs, start=(n == 0), stop=(n == len(pairs) - 1))
    return last


class Constants:

    def __init__(self, nc, ctx, a):
        def sb(name, shape):
            return ctx.enter_context(nc.sbuf_tensor("co_" + name, shape, F32))

        self.w_in, self.w_in_r = sb("w_in", [DM, NQK + 2 * D]), sb("w_in_r", [2 * DR, NQK + 2 * D])
        self.bq, self.bk, self.bqr, self.bkr = (
            sb("bq", [DM, 1]), sb("bk", [DM, 1]), sb("bqr", [DR, 1]), sb("bkr", [128, 1]))
        self.bv, self.bp, self.bl = sb("bv", [128, D]), sb("bp", [128, D]), sb("bl", [HQ, 1])
        self.wl_in, self.wl_in_r = sb("wl_in", [DM, H]), sb("wl_in_r", [DR, H])
        self.ww, self.mask, self.kron = sb("ww", [HQ, H]), sb("mask", [HQ, QS]), sb("kron", [HQ + 1, HQ])
        self.ident = sb("ident", [128, 128])
        wqkv, bqkv, wp = a["wqkv"], a["bqkv"], a["wp"]
        self.copies = []
        for lo, n, at in ((0, DM, 0), (D, DM, DM), (DM, DR, 2 * DM), (D + DM, DR, 2 * DM + DR), (2 * D, D, NQK)):
            self.copies.append((self.w_in[:, at:at + n], wqkv[0:DM, lo:lo + n]))
            for r in range(2):
                self.copies.append((self.w_in_r[r * DR:(r + 1) * DR, at:at + n], wqkv[DM:D, lo:lo + n]))
        self.copies.append((self.w_in[:, NQK + D:], wp[0:DM, :]))
        for r in range(2):
            self.copies.append((self.w_in_r[r * DR:(r + 1) * DR, NQK + D:], wp[DM:D, :]))
        for dst, lo, n in ((self.bq[:], 0, DM), (self.bqr[:], DM, DR), (self.bk[:], D, DM), (self.bkr[DR:, :], D + DM, DR)):
            self.copies.append((dst, bqkv[lo:lo + n].rearrange("(n a) -> n a", a=1)))
        for dst, src in ((self.bv, a["bv_rep"]), (self.bp, a["bp_rep"]), (self.bl, a["bl_rep"]),
                         (self.wl_in, a["wl_rep"][0:DM, :]), (self.wl_in_r, a["wl_rep"][DM:D, :]),
                         (self.ww, a["ww_rep"]), (self.mask, a["mask"]), (self.ident, a["ident"])):
            self.copies.append((dst[:], src))
        self.copies.append((self.kron[HQ:HQ + 1, :], a["bw_rep"]))


def embed_patches(nc, xT, w_proj, pos_rep, b_rep, cls_rep, pos0_rep, h0, const):
    ctx = ExitStack()
    with ctx:
        def sb(name, shape, dt=F32):
            return ctx.enter_context(nc.sbuf_tensor("em_" + name, shape, dt))

        def sem(name):
            return ctx.enter_context(nc.semaphore("em_" + name))

        ps = [ctx.enter_context(nc.psum_tensor(f"em_ps{n}", [128, 512], F32)) for n in range(2)]
        w = sb("w", [128, KD, D])
        wh, wl = sb("wh", [128, KD, D], F32R), sb("wl", [128, KD, D], F32R)
        x = sb("x", [128, RING, KD * EMB])
        xh, xl = sb("xh", [128, 2, KD * EMB], F32R), sb("xl", [128, 2, KD * EMB], F32R)
        pos, bias, posb = sb("pos", [EMB, D]), sb("bias", [EMB, D]), sb("posb", [EMB, D])
        cls, pos0, cls_row = sb("cls", [B, D]), sb("pos0", [B, D]), sb("cls_row", [B, D])
        out = sb("out", [EMB, 2, D])
        s_w, s_const, s_x = sem("w"), sem("const"), [sem(f"x{n}") for n in range(RING)]
        s_attn = sem("attn_const")
        s_wh, s_wl, s_cls, s_posb = sem("wh"), sem("wl"), sem("cls"), sem("posb")
        s_xh, s_xl, s_mm, s_out = sem("xh"), sem("xl"), sem("mm"), sem("out")
        s_store, s_cls_store = [sem("st0"), sem("st1")], sem("cls_st")
        tiles = B // 2
        rounds = tiles // RING
        block = ctx.enter_context(nc.Block())

        @block.sync
        def _(sp):
            sp.dma_start(w[:], w_proj.rearrange("(k p) n -> p k n", p=128)).then_inc(s_w, 16)
            for u in range(RING):
                sp.dma_start(x[:, u, :], xT[u]).then_inc(s_x[u], 16)
            for dst, src in ((pos, pos_rep), (bias, b_rep), (cls, cls_rep), (pos0, pos0_rep)):
                sp.dma_start(dst[:], src).then_inc(s_const, 16)

            def tile(it, u, more):
                if more:
                    sp.wait_ge(s_xl, RING * it + u + 1)
                    sp.dma_start(x[:, u, :], xT[bass.ds(RING * (it + 1) + u, 1)].rearrange("a p n -> (a p) n")
                                 ).then_inc(s_x[u], 16)
                sp.wait_ge(s_out, RING * it + u + 1)
                for k in range(2):
                    sp.dma_start(h0[bass.ds(2 * RING * it + 2 * u + k, 1), 1:NC, :].rearrange("b n d -> (b n) d"),
                                 out[k * NP:(k + 1) * NP, u % 2, :]).then_inc(s_store[u % 2], 16)
            with sp.Fori(0, rounds - 1) as it:
                for u in range(RING):
                    tile(it, u, True)
            for u in range(RING):
                tile(rounds - 1, u, False)
            sp.wait_ge(s_cls, 1)
            sp.dma_start(h0[:, 0, :], cls_row[:]).then_inc(s_cls_store, 16)
            for u in range(2):
                sp.wait_ge(s_store[u], 16 * tiles)
            sp.wait_ge(s_cls_store, 16)

        @block.gpsimd
        def _(pool):
            with nc.allow_non_contiguous_dma("weights are loaded once"):
                for dst, src in const.copies:
                    pool.dma_start(dst, src).then_inc(s_attn, 16)
            pool.wait_ge(s_attn, 16 * len(const.copies))

        @block.scalar
        def _(act):
            act.wait_ge(s_w, 16)
            act.activation(wh[:], w[:], ACT.Copy).then_inc(s_wh, 1)

            def tile(i, it, u):
                act.wait_ge(s_x[u], 16 * it + 16)
                wait(act, s_mm, i - 1)
                act.activation(xh[:, u % 2, :], x[:, u, :], ACT.Copy).then_inc(s_xh, 1)
            for u in range(RING):
                tile(u, 0, u)
            with act.Fori(1, rounds) as it:
                for u in range(RING):
                    tile(RING * it + u, it, u)

        @block.vector
        def _(dve):
            dve.wait_ge(s_wh, 1)
            dve.tensor_tensor(wl[:], w[:], f(wh[:]), ALU.subtract).then_inc(s_wl, 1)

            def low(i, u):
                dve.wait_ge(s_xh, i + 1)
                dve.tensor_tensor(xl[:, u % 2, :], x[:, u, :], f(xh[:, u % 2, :]), ALU.subtract).then_inc(s_xl, 1)

            def store(i, u, pairs):
                dve.wait_ge(s_mm, i + 1)
                wait(dve, s_store[u % 2], 32 * pairs)
                dve.tensor_tensor(out[:, u % 2, :], ps[u % 2][0:EMB, 0:D], posb[:], ALU.add).then_inc(s_out, 1)
            low(0, 0)
            dve.wait_ge(s_const, 64)
            dve.tensor_tensor(posb[:], pos[:], bias[:], ALU.add).then_inc(s_posb, 1)
            dve.tensor_tensor(cls_row[:], cls[:], pos0[:], ALU.add).then_inc(s_cls, 1)
            dve.wait_ge(s_posb, 1)
            for i in range(1, RING):
                low(i, i)
                store(i - 1, i - 1, (i - 1) // 2)
            with dve.Fori(1, rounds) as it:
                for u in range(RING):
                    low(RING * it + u, u)
                    store(RING * it + u - 1, (u - 1) % RING, RING // 2 * it + (u - 1) // 2)
            store(tiles - 1, RING - 1, tiles // 2 - 1)

        @block.tensor
        def _(pe):
            pe.wait_ge(s_wl, 1)

            def tile(i, u):
                pe.wait_ge(s_xl, i + 1)
                wait(pe, s_out, i - 1)
                last = None
                for k in range(KD):
                    cols = slice(k * EMB, (k + 1) * EMB)
                    for n, (a, b) in enumerate(((xh, wh), (xl, wh), (xh, wl))):
                        last = pe.matmul(ps[u][0:EMB, 0:D], a[:, u, cols], b[:, k, :], start=(k + n == 0),
                                         stop=(k == KD - 1 and n == 2))
                last.then_inc(s_mm, 1)
            for u in range(2):
                tile(u, u)
            with pe.Fori(1, tiles // 2) as it:
                for u in range(2):
                    tile(2 * it + u, u)


def attention(nc, txt, h0, h1, const, experts_raw):
    ctx = ExitStack()
    with ctx:
        def sb(name, shape, dt=F32):
            return ctx.enter_context(nc.sbuf_tensor("at_" + name, shape, dt))

        def sem(name):
            return ctx.enter_context(nc.semaphore("at_" + name))

        bank = [ctx.enter_context(nc.psum_tensor(f"at_bank{n}", [128, 512], F32)) for n in range(8)]
        ps_s, ps_m, ps_mr, ps_q, ps_o = bank[0:2], bank[2:4], bank[4:6], bank[6], bank[7]

        c = const
        w_in, w_in_r, bq, bk, bqr, bkr, bv, bp, bl = c.w_in, c.w_in_r, c.bq, c.bk, c.bqr, c.bkr, c.bv, c.bp, c.bl
        wl_in, wl_in_r, ww, mask, kron, ident = c.wl_in, c.wl_in_r, c.ww, c.mask, c.kron, c.ident
        wqk, wv, wo = Split(sb, "wqk", NQK), Split(sb, "wv", D), Split(sb, "wo", D)
        wls, wls_r = sb("wls", [DM, H]), sb("wls_r", [DR, H])
        kron_h, kron_l = sb("kron_h", [HQ + 1, HQ], F32R), sb("kron_l", [HQ + 1, HQ], F32R)

        tok = sb("tok", [128, 2, D])
        stats, moments = sb("stats", [128, 2, 6]), sb("moments", [128, 2, 2])
        var_eps, half_neg, rstd = sb("var_eps", [128, 2]), sb("half_neg", [128, 2]), sb("rstd", [128, 2])
        eps = sb("eps", [128, 2])
        centred, xhat = sb("centred", [128, 2, D]), sb("xhat", [128, 2, D])
        x = (sb("x_hi", [DM, SE], F32R), sb("x_lo", [DM, SE], F32R), sb("x_rest", [2 * DR, SE], F32R))
        q, q_r = sb("q", [DM, SQ]), sb("q_r", [DR, SQ])
        k_hi, k_lo = sb("k_hi", [DM, 2, SE], F32R), sb("k_lo", [DM, 2, SE], F32R)
        k_r2, k_rlo = sb("k_r2", [2 * DR, 2, SE], F32R), sb("k_rlo", [DR, 2, SE], F32R)
        qg_hi, qg_lo = sb("qg_hi", [DM, 2, H * SQ], F32R), sb("qg_lo", [DM, 2, H * SQ], F32R)
        qg_r = sb("qg_r", [2 * DR, 2, H * SQ], F32R)
        v = sb("v", [128, 2, 2, D])
        vz_hi, vz_lo = sb("vz_hi", [NT, VZ], F32R), sb("vz_lo", [NT, VZ], F32R)
        vz_r2, vz_rlo = sb("vz_r2", [128, VZ], F32R), sb("vz_rlo", [NC, VZ], F32R)
        neg_max, lifted, shift = (sb(n, [HQ, 2, GROUP]) for n in ("neg_max", "lifted", "shift"))
        total, scale = sb("total", [HQ, 2, GROUP]), sb("scale", [HQ, 2, GROUP])
        ex = sb("ex", [HQ, 2, GROUP, S])
        p_hi, p_lo = sb("p_hi", [128, 2, GROUP, S], F32R), sb("p_lo", [128, 2, GROUP, S], F32R)
        a_hi, a_lo = sb("a_hi", [NT, 2, H * SQ], F32R), sb("a_lo", [NT, 2, H * SQ], F32R)
        a_r = sb("a_r", [128, 2, H * SQ], F32R)
        o = (sb("o_hi", [DM, SE], F32R), sb("o_lo", [DM, SE], F32R), sb("o_rest", [2 * DR, SE], F32R))
        res, resb, hout = sb("res", [128, 2, D]), sb("resb", [128, 2, D]), sb("hout", [128, 2, D])

        experts_raw.place(nc, ctx)
        s_experts = sem("experts")
        s_zero, s_whi, s_wlo, s_prep = (sem(n) for n in ("zero", "whi", "wlo", "prep"))
        s_tok, s_res, s_store = sem("tok"), sem("res"), sem("store")
        s_stats, s_mom, s_veps, s_rstd, s_xhat = (sem(n) for n in ("stats", "mom", "veps", "rstd", "xhat"))
        s_t, s_xhi, s_xlo = sem("t"), sem("xhi"), sem("xlo")
        s_qk, s_khi, s_klo, s_q, s_vmm, s_v, s_vz, s_vzc = (
            sem(n) for n in ("qk", "khi", "klo", "q", "vmm", "v", "vz", "vzc"))
        s_qgh, s_qgr, s_qgl = sem("qgh"), sem("qgr"), sem("qgl")
        s_xc = sem("xc")
        s_s, s_max, s_lift, s_shift, s_exp, s_scale, s_norm, s_phi, s_plo = (
            sem(n) for n in ("s", "max", "lift", "shift", "exp", "scale", "norm", "phi", "plo"))
        s_m, s_ahi, s_alo, s_av, s_ohi, s_olo, s_pr, s_resb, s_h1 = (
            sem(n) for n in ("m", "ahi", "alo", "av", "ohi", "olo", "pr", "resb", "h1"))

        def has(i):
            return not isinstance(i, int) or 0 <= i < B

        def par(u):
            return u % 2

        def win(t, a, b):
            return t[a:b, VW - DH:].rearrange("p (g w) -> p g w", w=VW)[:, :, 0:DH]

        def head(ap, g):
            return ap.rearrange("p (t g s) -> p t g s", g=H, s=QS)[:, :, g, :]

        def tiles(ap):
            return ap.rearrange("p (t s) -> p t s", s=QS)

        share = {0: (0, 1, 2), 1: (3, 4), 2: (5, 6), 3: (7, 8), 4: (9, 10, 11)}

        def ago(i, u, j, n):
            return (i, par(u), j - n) if j >= n else (i - 1, 1 - par(u), j - n + GROUPS)

        def mixed(ap, j):
            ts = group_tiles(j)
            return ap.rearrange("p (g t s) -> p t g s", g=H, s=QS)[:, ts[0]:ts[-1] + 1, :, :]

        def mix_bank(t, j, rows):
            n = len(group_tiles(j))
            return t[0:rows, 0:n * HQ].rearrange("p (t g s) -> p t g s", g=H, s=QS)

        def steps(eng, step):
            for i in range(-3, 4):
                step(i, i % 2)
            with eng.Fori(2, (B - 4) // 2) as it:
                for u in range(2):
                    step(2 * it + u, u)
            for i in range(B - 4, B + 2):
                step(i, i % 2)

        block = ctx.enter_context(nc.Block())

        @block.sync
        def _(sp):
            def load_tokens(i):
                sp.dma_start(tok[:, 0, :], txt[bass.ds(i, 1)].rearrange("a t d -> (a t) d")).then_inc(s_tok, 16)
                sp.dma_start(tok[0:NC, 1, :], h0[bass.ds(i, 1)].rearrange("a t d -> (a t) d")).then_inc(s_tok, 16)

            def step(i, u):
                if has(i - 1):
                    wait(sp, s_resb, 2 * (i - 1))
                    sp.dma_start(res[:, 0, :], txt[bass.ds(i - 1, 1)].rearrange("a t d -> (a t) d")).then_inc(s_res, 16)
                    sp.dma_start(res[0:NC, 1, :], h0[bass.ds(i - 1, 1)].rearrange("a t d -> (a t) d")
                                 ).then_inc(s_res, 16)
                if has(i - 3):
                    out_image(i - 3)
                if has(i + 3):
                    sp.wait_ge(s_xhat, 2 * (i + 3))
                    load_tokens(i + 3)

            def out_image(i):
                sp.wait_ge(s_h1, 2 * i + 2)
                row = h1[bass.ds(i, 1)].rearrange("a t d -> (a t) d")
                sp.dma_start(row[NC:S, :], hout[:, 0, :]).then_inc(s_store, 16)
                sp.dma_start(row[0:NC, :], hout[0:NC, 1, :]).then_inc(s_store, 16)

            load_tokens(0)
            for i in range(-2, 4):
                step(i, 0)
            for dst, src in experts_raw.copies:
                sp.dma_start(dst, src).then_inc(s_experts, 16)
            with sp.Fori(4, B - 3) as i:
                step(i, 0)
            for i in range(B - 3, B + 2):
                step(i, 0)
            out_image(B - 1)
            sp.wait_ge(s_store, 32 * B)
            sp.wait_ge(s_experts, 16 * len(experts_raw.copies))

        @block.gpsimd
        def _(pool):
            zeroed = [x[0], x[1], x[2], k_hi, k_lo, k_r2, k_rlo, q, q_r, o[0], o[1], o[2]]
            for t in zeroed:
                pool.memset(t[:].bitcast(F32), 0.0).then_inc(s_zero, 1)
            pool.memset(moments[:], 1.0).then_inc(s_zero, 1)
            pool.memset(half_neg[:], -0.5).then_inc(s_zero, 1)
            pool.memset(eps[:], EPS).then_inc(s_zero, 1)
            assert len(zeroed) + 3 + 7 == N_ZERO
            pool.wait_ge(s_zero, N_ZERO)

            def rest_queries(i, pa, g_range):
                for g in g_range:
                    pool.tensor_tensor(head(qg_r[0:DR, pa, :], g), tiles(q_r[:]),
                                       wls_r[:, g:g + 1].rearrange("p (a b) -> p a b", b=1).to_broadcast([DR, TILES, QS]),
                                       ALU.mult).then_inc(s_qgr, 1)

            def shifts(i, j):
                b, nt = j % 2, len(group_tiles(j))
                bias = bl[:].to_broadcast([HQ, nt])
                pool.wait_ge(s_max, GROUPS * i + j + 1)
                pool.tensor_tensor(lifted[:, b, 0:nt], neg_max[:, b, 0:nt], bias, ALU.subtract).then_inc(s_lift, 1)
                pool.wait_ge(s_lift, GROUPS * i + j + 1)
                pool.tensor_tensor(shift[:, b, 0:nt], lifted[:, b, 0:nt], bias, ALU.add).then_inc(s_shift, 1)

            def normalised(n, jp):
                b, nt = jp % 2, len(group_tiles(jp))
                pool.wait_ge(s_scale, GROUPS * n + jp + 1)
                pool.tensor_tensor(ex[:, b, 0:nt, :], ex[:, b, 0:nt, :], scale[:, b, 0:nt].rearrange(
                    "p (t a) -> p t a", a=1).to_broadcast([HQ, nt, S]), ALU.mult).then_inc(s_norm, 1)

            def slot(i, u, j):
                pa = par(u)
                if j in share and has(i + 1):
                    if j == 0:
                        pool.wait_ge(s_q, 2 * (i + 2))
                        wait(pool, s_s, GROUPS * i)
                    rest_queries(i + 1, 1 - pa, share[j])
                n, _, jp = ago(i, u, j, 1)
                if j == 5 and has(n):
                    normalised(n, jp)
                if has(i):
                    shifts(i, j)
                if j < 5 and has(n):
                    normalised(n, jp)
                if j == 1 and has(i - 1):
                    src = v[:, 1 - pa, 0, :].rearrange("p (g d) -> p g d", d=DH)
                    src_r = v[0:NC, 1 - pa, 1, :].rearrange("p (g d) -> p g d", d=DH)
                    pool.wait_ge(s_vzc, 3 * i)
                    pool.tensor_tensor(win(vz_lo, 0, NT), src, f(win(vz_hi, 0, NT)), ALU.subtract).then_inc(s_vz, 1)
                    pool.tensor_tensor(win(vz_rlo, 0, NC), src_r, f(win(vz_r2, 0, NC)), ALU.subtract).then_inc(s_vz, 1)
                if j == 2 and has(i + 2):
                    centre(i + 2)
                if j == 3 and has(i + 2):
                    normalise(i + 2)
                if j == 5 and has(i - 1):
                    pool.wait_ge(s_res, 32 * i)
                    wait(pool, s_h1, 2 * (i - 1))
                    pool.tensor_tensor(resb[:, 0, :], res[:, 0, :], bp[:], ALU.add).then_inc(s_resb, 1)
                    pool.tensor_tensor(resb[0:NC, 1, :], res[0:NC, 1, :], bp[0:NC, :], ALU.add).then_inc(s_resb, 1)

            def step(i, u):
                for j in range(GROUPS):
                    slot(i, u, j)

            def centre(n):
                pool.wait_ge(s_mom, 2 * (n + 1))
                pool.tensor_tensor(var_eps[:], moments[:, :, 1], eps[:], ALU.add).then_inc(s_veps, 1)
                wait(pool, s_xhat, 2 * n)
                for t, rows in ((0, NT), (1, NC)):
                    pool.tensor_tensor(centred[0:rows, t, :], tok[0:rows, t, :],
                                       moments[0:rows, t, 0:1].to_broadcast([rows, D]), ALU.subtract).then_inc(s_xc, 1)
                pool.wait_ge(s_veps, n + 1)
                pool.tensor_tensor(rstd[:], var_eps[:], half_neg[:], ALU.pow).then_inc(s_rstd, 1)

            def normalise(n):
                pool.wait_ge(s_xc, 2 * (n + 1))
                pool.wait_ge(s_rstd, n + 1)
                wait(pool, s_t, n)
                for t, rows in ((0, NT), (1, NC)):
                    pool.tensor_tensor(xhat[0:rows, t, :], centred[0:rows, t, :],
                                       rstd[0:rows, t:t + 1].to_broadcast([rows, D]), ALU.mult).then_inc(s_xhat, 1)
            steps(pool, step)

        @block.scalar
        def _(act):
            cuts = ((wqk, 0, NQK), (wv, NQK, NQK + D), (wo, NQK + D, NQK + 2 * D))
            for w, a, b in cuts:
                act.activation(w.hi[:], w_in[:, a:b], ACT.Copy).then_inc(s_whi, 1)
                act.activation(w.rest2[:], w_in_r[:, a:b], ACT.Copy).then_inc(s_whi, 1)
            act.wait_ge(s_prep, 2)
            act.activation(kron_h[:], kron[:], ACT.Copy).then_inc(s_whi, 1)
            act.wait_ge(s_zero, N_ZERO)

            def exponentials(i, j):
                b = j % 2
                act.wait_ge(s_shift, GROUPS * i + j + 1)
                wait(act, s_plo, GROUPS * i + j - 1)
                for k, t in enumerate(group_tiles(j)):
                    last = act.activation(ex[:, b, k, :], ps_s[b][0:HQ, k * SE:k * SE + S], ACT.Exp,
                                      bias=shift[:, b, k:k + 1], accum_out=total[:, b, k:k + 1])
                last.then_inc(s_exp, 1)

            def probabilities_hi(n, jp):
                act.wait_ge(s_norm, GROUPS * n + jp + 1)
                wait(act, s_m, GROUPS * n + jp - 1)
                b, nt = jp % 2, len(group_tiles(jp))
                act.activation(p_hi[0:HQ, b, 0:nt, :], ex[:, b, 0:nt, :], ACT.Copy).then_inc(s_phi, 1)

            def slot(i, u, j):
                pa = par(u)
                n, pn, ja = ago(i, u, j, 3)
                if has(n):
                    act.wait_ge(s_m, GROUPS * n + ja + 1)
                    if ja == 0:
                        wait(act, s_av, n - 1)
                    act.activation(mixed(a_hi[:, pn, :], ja), mix_bank(ps_m[ja % 2], ja, NT), ACT.Copy).then_inc(s_ahi, 1)
                    act.activation(mixed(a_r[0:NC, pn, :], ja), mix_bank(ps_mr[ja % 2], ja, NC), ACT.Copy
                                   ).then_inc(s_ahi, 1)
                if j == 1 and has(i - 2):
                    act.wait_ge(s_av, i - 1)
                    wait(act, s_pr, i - 2)
                    for k, dst in enumerate((o[0][0:DR, 0:S], o[0][DR:DM, 0:S], o[2][0:DR, 0:S])):
                        act.activation(dst, ps_o[0:DR, k * SE:k * SE + S], ACT.Copy).then_inc(s_ohi, 1)
                if j == 1 and has(i - 1):
                    wait(act, s_av, i - 1)
                    act.wait_ge(s_v, 2 * i)
                    src_r = v[0:NC, 1 - pa, 1, :].rearrange("p (g d) -> p g d", d=DH)
                    act.activation(win(vz_hi, 0, NT), v[:, 1 - pa, 0, :].rearrange("p (g d) -> p g d", d=DH), ACT.Copy
                                   ).then_inc(s_vzc, 1)
                    act.activation(win(vz_r2, 0, NC), src_r, ACT.Copy).then_inc(s_vzc, 1)
                    act.activation(win(vz_r2, 64, 64 + NC), src_r, ACT.Copy).then_inc(s_vzc, 1)
                if j == 4 and has(i + 2):
                    act.wait_ge(s_t, i + 3)
                    wait(act, s_vmm, i + 2)
                    act.activation(x[0][:, 0:S], ps_q[:, 0:S], ACT.Copy).then_inc(s_xhi, 1)
                    act.activation(x[2][0:DR, 0:S], ps_q[0:DR, SE:SE + S], ACT.Copy).then_inc(s_xhi, 1)
                if j in share and has(i + 1):
                    if j == 0:
                        act.wait_ge(s_q, 2 * (i + 2))
                    for g in share[j]:
                        act.activation(head(qg_hi[:, 1 - pa, :], g), tiles(q[:]), ACT.Copy, scale=wls[:, g:g + 1]
                                       ).then_inc(s_qgh, 1)
                n, _, jp = ago(i, u, j, 1)
                if j == 5 and has(n):
                    probabilities_hi(n, jp)
                if has(i):
                    exponentials(i, j)
                if j < 5 and has(n):
                    probabilities_hi(n, jp)
                if j == 5 and has(i + 2):
                    km, kr = ps_q[:, SE:SE + S], ps_q[DR:2 * DR, 2 * SE:2 * SE + S]
                    act.wait_ge(s_qk, i + 3)
                    wait(act, s_qgl, 2 * H * (i + 2))
                    wait(act, s_qgr, H * (i + 2))
                    act.activation(q[:, 0:S], ps_q[:, 0:S], ACT.Identity, bias=bq[:]).then_inc(s_q, 1)
                    act.activation(q_r[:, 0:S], ps_q[0:DR, 2 * SE:2 * SE + S], ACT.Identity, bias=bqr[:]
                                   ).then_inc(s_q, 1)
                    wait(act, s_s, GROUPS * (i + 1))
                    act.activation(k_r2[DR:, pa, 0:S], kr, ACT.Identity, bias=bkr[DR:, :]).then_inc(s_khi, 1)
                    act.activation(k_hi[:, pa, 0:S], km, ACT.Identity, bias=bk[:]).then_inc(s_khi, 1)
                    act.activation(k_r2[0:DR, pa, 0:S], kr, ACT.Identity, bias=bkr[DR:, :]).then_inc(s_khi, 1)

            def step(i, u):
                for j in range(GROUPS):
                    slot(i, u, j)
            steps(act, step)

        @block.vector
        def _(dve):
            dve.memset(f(p_lo[96:128, :, :, :]), 0.0).then_inc(s_zero, 1)
            dve.memset(f(p_hi[96:128, :, :, :]), 1.0).then_inc(s_zero, 1)
            for t in (vz_hi, vz_lo, vz_r2, vz_rlo, a_r):
                dve.memset(f(t[:]), 0.0).then_inc(s_zero, 1)
            dve.tensor_scalar(wls[:], wl_in[:], DH ** -0.5, None, ALU.mult).then_inc(s_prep, 1)
            dve.tensor_tensor(kron[0:HQ, :].rearrange("p (g s) -> p g s", s=QS),
                              ww[:].rearrange("p (g a) -> p g a", a=1).to_broadcast([HQ, H, QS]),
                              mask[:].rearrange("p (a s) -> p a s", a=1).to_broadcast([HQ, H, QS]), ALU.mult
                              ).then_inc(s_prep, 1)
            dve.tensor_scalar(wls_r[:], wl_in_r[:], DH ** -0.5, None, ALU.mult).then_inc(s_prep, 1)
            dve.wait_ge(s_whi, 7)
            cuts = ((wqk, 0, NQK), (wv, NQK, NQK + D), (wo, NQK + D, NQK + 2 * D))
            for w, a, b in cuts:
                dve.tensor_tensor(w.lo[:], w_in[:, a:b], f(w.hi[:]), ALU.subtract).then_inc(s_wlo, 1)
                dve.tensor_tensor(w.rest_lo[:], w_in_r[0:DR, a:b], f(w.rest2[0:DR, :]), ALU.subtract).then_inc(s_wlo, 1)
            dve.tensor_tensor(kron_l[:], kron[:], f(kron_h[:]), ALU.subtract).then_inc(s_wlo, 1)
            dve.wait_ge(s_zero, N_ZERO)
            dve.wait_ge(s_prep, 3)

            def maxima(i, j):
                b, nt = j % 2, len(group_tiles(j))
                dve.wait_ge(s_s, GROUPS * i + j + 1)
                dve.tensor_reduce(out=neg_max[:, b, 0:nt], in_=ps_s[b][0:HQ, 0:nt * SE].rearrange(
                    "p (t k) -> p t k", k=SE)[:, :, 0:S], op=ALU.max, axis=AX_X, negate=True).then_inc(s_max, 1)

            def reciprocals(n, jp):
                b, nt = jp % 2, len(group_tiles(jp))
                dve.wait_ge(s_exp, GROUPS * n + jp + 1)
                dve.reciprocal(scale[:, b, 0:nt], total[:, b, 0:nt]).then_inc(s_scale, 1)

            def slot(i, u, j):
                pa = par(u)
                n, _, jp = ago(i, u, j, 1)
                if j == 5 and has(n):
                    reciprocals(n, jp)
                if has(i):
                    maxima(i, j)
                if j < 5 and has(n):
                    reciprocals(n, jp)
                n, pn, ja = ago(i, u, j, 3)
                if has(n):
                    dve.wait_ge(s_ahi, 2 * (GROUPS * n + ja) + 2)
                    dve.tensor_tensor(mixed(a_lo[:, pn, :], ja), mix_bank(ps_m[ja % 2], ja, NT),
                                      f(mixed(a_hi[:, pn, :], ja)), ALU.subtract).then_inc(s_alo, 1)
                    dve.tensor_tensor(mixed(a_r[64:64 + NC, pn, :], ja), mix_bank(ps_mr[ja % 2], ja, NC),
                                      f(mixed(a_r[0:NC, pn, :], ja)), ALU.subtract).then_inc(s_alo, 1)
                if j == 0 and has(i + 1):
                    pk = 1 - pa
                    km, kr = ps_q[:, SE:SE + S], ps_q[DR:2 * DR, 2 * SE:2 * SE + S]
                    dve.wait_ge(s_khi, 3 * (i + 2))
                    dve.scalar_tensor_tensor(out=k_rlo[:, pk, 0:S], in0=kr, scalar=bkr[DR:, :], in1=f(k_r2[DR:, pk, 0:S]),
                                             op0=ALU.add, op1=ALU.subtract).then_inc(s_klo, 1)
                    dve.scalar_tensor_tensor(out=k_lo[:, pk, 0:S], in0=km, scalar=bk[:], in1=f(k_hi[:, pk, 0:S]),
                                             op0=ALU.add, op1=ALU.subtract).then_inc(s_klo, 1)
                if j == 1 and has(i - 2):
                    dve.wait_ge(s_ohi, 3 * (i - 1))
                    for k, (dst, hi) in enumerate(((o[1][0:DR, 0:S], o[0][0:DR, 0:S]), (o[1][DR:DM, 0:S], o[0][DR:DM, 0:S]),
                                                   (o[2][DR:2 * DR, 0:S], o[2][0:DR, 0:S]))):
                        dve.tensor_tensor(dst, ps_o[0:DR, k * SE:k * SE + S], f(hi), ALU.subtract).then_inc(s_olo, 1)
                if j == 2 and has(i + 1):
                    dve.wait_ge(s_vmm, i + 2)
                    wait(dve, s_vz, 2 * i)
                    dve.tensor_tensor(v[:, 1 - pa, 0, :], ps_q[:, 0:D], bv[:], ALU.add).then_inc(s_v, 1)
                    dve.tensor_tensor(v[0:NC, 1 - pa, 1, :], ps_q[0:NC, D:2 * D], bv[0:NC, :], ALU.add).then_inc(s_v, 1)
                if j == 3 and has(i - 2):
                    dve.wait_ge(s_pr, i - 1)
                    dve.wait_ge(s_resb, 2 * (i - 1))
                    wait(dve, s_store, 32 * (i - 2))
                    dve.tensor_tensor(hout[:, 0, :], ps_o[:, 0:D], resb[:, 0, :], ALU.add).then_inc(s_h1, 1)
                    dve.tensor_tensor(hout[0:NC, 1, :], ps_o[0:NC, D:2 * D], resb[0:NC, 1, :], ALU.add).then_inc(s_h1, 1)
                if j == 4 and has(i + 2):
                    dve.wait_ge(s_xhi, 2 * (i + 3))
                    dve.tensor_tensor(x[1][:, 0:S], ps_q[:, 0:S], f(x[0][:, 0:S]), ALU.subtract).then_inc(s_xlo, 1)
                    dve.tensor_tensor(x[2][DR:, 0:S], ps_q[0:DR, SE:SE + S], f(x[2][0:DR, 0:S]), ALU.subtract
                                      ).then_inc(s_xlo, 1)
                if j in share and has(i + 1):
                    for g in share[j]:
                        dve.wait_ge(s_qgh, H * (i + 1) + g + 1)
                        dve.scalar_tensor_tensor(out=head(qg_lo[:, 1 - pa, :], g), in0=tiles(q[:]), scalar=wls[:, g:g + 1],
                                                 in1=f(head(qg_hi[:, 1 - pa, :], g)), op0=ALU.mult, op1=ALU.subtract
                                                 ).then_inc(s_qgl, 1)
                        dve.wait_ge(s_qgr, H * (i + 1) + g + 1)
                        dve.scalar_tensor_tensor(out=head(qg_r[DR:2 * DR, 1 - pa, :], g), in0=tiles(q_r[:]),
                                                 scalar=wls_r[:, g:g + 1], in1=f(head(qg_r[0:DR, 1 - pa, :], g)),
                                                 op0=ALU.mult, op1=ALU.subtract).then_inc(s_qgl, 1)
                if j == 5 and has(i + 3):
                    wait(dve, s_xhat, 2 * (i + 3))
                    dve.wait_ge(s_tok, 32 * (i + 4))
                    dve.bn_stats(stats[:, 0, :], tok[:, 0, :]).then_inc(s_stats, 1)
                    dve.bn_stats(stats[0:NC, 1, :], tok[0:NC, 1, :]).then_inc(s_stats, 1)
                    dve.wait_ge(s_stats, 2 * (i + 4))
                n, pn, jp = ago(i, u, j, 1)
                if has(n):
                    b, nt = jp % 2, len(group_tiles(jp))
                    wait(dve, s_m, GROUPS * n + jp - 1)
                    dve.wait_ge(s_phi, GROUPS * n + jp + 1)
                    dve.tensor_tensor(p_lo[0:HQ, b, 0:nt, :], ex[:, b, 0:nt, :], f(p_hi[0:HQ, b, 0:nt, :]), ALU.subtract
                                      ).then_inc(s_plo, 1)
                if j == 5 and has(i + 3):
                    aggregate()

            def aggregate():
                dve.bn_aggr(moments[:, 0, :], stats[:, 0, :]).then_inc(s_mom, 1)
                dve.bn_aggr(moments[0:NC, 1, :], stats[0:NC, 1, :]).then_inc(s_mom, 1)

            def step(i, u):
                for j in range(GROUPS):
                    slot(i, u, j)
            steps(dve, step)

        @block.tensor
        def _(pe):
            pe.wait_ge(s_wlo, 7)
            pe.wait_ge(s_zero, N_ZERO)

            def logits(i, pa, j):
                if j == 0:
                    pe.wait_ge(s_qgl, 2 * H * (i + 1))
                    pe.wait_ge(s_klo, 2 * (i + 1))
                wait(pe, s_exp, GROUPS * i + j - 1)
                for n, t in enumerate(group_tiles(j)):
                    out = ps_s[j % 2][0:HQ, n * SE:(n + 1) * SE]
                    hi, lo, rest = (z[:, pa, t * HQ:(t + 1) * HQ] for z in (qg_hi, qg_lo, qg_r))
                    pe.matmul(out, hi, k_hi[:, pa, :], start=True, stop=False)
                    pe.matmul(out, lo, k_hi[:, pa, :], start=False, stop=False)
                    pe.matmul(out, hi, k_lo[:, pa, :], start=False, stop=False)
                    pe.matmul(out, rest, k_r2[:, pa, :], start=False, stop=False)
                    last = pe.matmul(out, rest[0:DR], k_rlo[:, pa, :], start=False, stop=True)
                last.then_inc(s_s, 1)

            def mix(i, j):
                b = j % 2
                pe.wait_ge(s_plo, GROUPS * i + j + 1)
                wait(pe, s_alo, 2 * (GROUPS * i + j - 1))
                for bank_, rows, cols in ((ps_m[b], NT, slice(0, NT)), (ps_mr[b], NC, slice(NT, S))):
                    for n, t in enumerate(group_tiles(j)):
                        out = bank_[0:rows, n * HQ:(n + 1) * HQ]
                        pe.matmul(out, p_hi[0:HQ + 1, b, n, cols], kron_h[:], start=True, stop=False)
                        pe.matmul(out, p_lo[0:HQ + 1, b, n, cols], kron_h[:], start=False, stop=False)
                        last = pe.matmul(out, p_hi[0:HQ + 1, b, n, cols], kron_l[:], start=False, stop=True)
                last.then_inc(s_m, 1)

            def values(i, pa, g_range):
                for g in g_range:
                    gg, at = g % HB, g // HB * SE
                    w = slice(g * VW + VW - DH * (gg + 1), g * VW + VW - DH * (gg + 1) + DR)
                    c = slice(g * SQ, g * SQ + SE)
                    out = ps_o[0:DR, at:at + SE]
                    pe.matmul(out, vz_hi[:, w], a_hi[:, pa, c], start=(gg == 0), stop=False)
                    pe.matmul(out, vz_lo[:, w], a_hi[:, pa, c], start=False, stop=False)
                    pe.matmul(out, vz_hi[:, w], a_lo[:, pa, c], start=False, stop=False)
                    pe.matmul(out, vz_r2[0:64 + NC, w], a_r[0:64 + NC, pa, c], start=False, stop=False)
                    last = pe.matmul(out, vz_rlo[:, w], a_r[0:NC, pa, c], start=False,
                                     stop=(gg == HB - 1))
                return last

            def slot(i, u, j):
                pa = par(u)
                n, js, ps = (i, j + 1, pa) if j < GROUPS - 1 else (i + 1, 0, 1 - pa)
                if has(n):
                    logits(n, ps, js)
                if j == 5 and has(i + 2):
                    pe.wait_ge(s_xlo, 2 * (i + 3))
                    for m in range(3):
                        last = product(pe, ps_q[:, m * SE:(m + 1) * SE], x, wqk, slice(0, SE),
                                       slice(m * 128, (m + 1) * 128), False)
                    last.then_inc(s_qk, 1)
                n, _, jm = ago(i, u, j, 2)
                if has(n):
                    mix(n, jm)
                if j == 0 and has(i - 2):
                    values(i - 2, pa, range(9, H)).then_inc(s_av, 1)
                if j == 1 and has(i + 1):
                    pe.wait_ge(s_klo, 2 * (i + 2))
                    product(pe, ps_q[0:NT, 0:D], x, wv, slice(0, NT), slice(0, D), True)
                    product(pe, ps_q[0:NC, D:2 * D], x, wv, slice(NT, S), slice(0, D), True).then_inc(s_vmm, 1)
                if j == 2 and has(i - 2):
                    pe.wait_ge(s_olo, 3 * (i - 1))
                    product(pe, ps_o[0:NT, 0:D], o, wo, slice(0, NT), slice(0, D), True)
                    product(pe, ps_o[0:NC, D:2 * D], o, wo, slice(NT, S), slice(0, D), True).then_inc(s_pr, 1)
                if j == 3 and has(i - 1):
                    pe.wait_ge(s_alo, 2 * GROUPS * i)
                    pe.wait_ge(s_vz, 2 * i)
                    wait(pe, s_h1, 2 * (i - 1))
                if j in (3, 4) and has(i - 1):
                    values(i - 1, 1 - pa, range(0, 3) if j == 3 else range(3, 9))
                if j == 3 and has(i + 2):
                    pe.wait_ge(s_xhat, 2 * (i + 3))
                    wait(pe, s_v, 2 * (i + 2))
                    for t, rows in ((0, NT), (1, NC)):
                        pe.transpose(ps_q[0:DM, t * NT:t * NT + rows], xhat[0:rows, t, 0:DM], ident[0:rows, 0:rows])
                        last = pe.transpose(ps_q[0:DR, SE + t * NT:SE + t * NT + rows], xhat[0:rows, t, DM:D],
                                            ident[0:rows, 0:rows])
                    last.then_inc(s_t, 1)

            def warm_up(i):
                wait(pe, s_exp, GROUPS * i)
                for n in range(16):
                    pe.matmul(ps_s[1][:, 0:NQK], wqk.hi[:, 0:128], wqk.hi[:], start=True, stop=True)

            def step(i, u):
                if isinstance(i, int) and i in (0, 1):
                    warm_up(i)
                for j in range(GROUPS):
                    slot(i, u, j)
            steps(pe, step)


N_ZERO = 17 + 5


class ExpertWeights:

    def __init__(self, a):
        self.weights = [(a["sg"], a["su"], a["sd"])] + [(a["rg"][e], a["ru"][e], a["rd"][e]) for e in range(E)]

    def place(self, nc, ctx):
        t = ctx.enter_context(nc.sbuf_tensor("experts_raw", [128, 4 * NH + NF * D], F32))
        self.main = [t[:, m * NH:(m + 1) * NH] for m in range(2)]
        self.rest = [t[:, (2 + m) * NH:(3 + m) * NH] for m in range(2)]
        self.down = t[:, 4 * NH:4 * NH + NF * D].rearrange("p (n d) -> p n d", d=D)
        self.copies = []
        for k in range(E + 1):
            c = slice(k * FT, (k + 1) * FT)
            for m in range(2):
                w = self.weights[k][m]
                self.copies.append((self.main[m][:, c], w[0:DM, :]))
                for r in range(2):
                    self.copies.append((self.rest[m][r * DR:(r + 1) * DR, c], w[DM:D, :]))
            self.copies.append((self.down[:, 3 * k:3 * k + 3, :], self.weights[k][2].rearrange("(f p) d -> p f d", p=128)))


def experts(nc, h1, out, raw, router_rep, rbias_rep, ident_in):
    ctx = ExitStack()
    with ctx:
        def sb(name, shape, dt=F32):
            return ctx.enter_context(nc.sbuf_tensor("ex_" + name, shape, dt))

        def sem(name):
            return ctx.enter_context(nc.semaphore("ex_" + name))

        bank = [ctx.enter_context(nc.psum_tensor(f"ex_bank{n}", [128, 512], F32)) for n in range(8)]
        ps_g, ps_u, ps_d, ps_x, ps_xr = bank[0:2], bank[2:4], bank[4:6], bank[6], bank[7]
        gate, up = Split(sb, "gate", NH), Split(sb, "up", NH)
        down_h, down_l = sb("down_h", [128, NF, D], F32R), sb("down_l", [128, NF, D], F32R)
        router, rbias, ident = sb("router", [TP, E, D]), sb("rbias", [TP, TT, E]), sb("ident", [128, 128])
        h, hres = sb("h", [TP, TT, D]), sb("hres", [TP, TT, D])
        stats, moments = sb("stats", [TP, TT, 6]), sb("moments", [TP, TT, 2])
        var_eps, half_neg, rstd = sb("var_eps", [TP, TT]), sb("half_neg", [TP, TT]), sb("rstd", [TP, TT])
        eps = sb("eps", [TP, TT])
        xhat, rprod = sb("xhat", [TP, TT, D]), sb("rprod", [TP, 2 * E, D])
        rt = [sb(f"rt{n}", [TP, TT, E]) for n in range(6)]
        rs = [sb(f"rs{n}", [TP, TT]) for n in range(3)]
        cw = sb("cw", [TP, 2, TT, E])
        x = (sb("x_hi", [DM, CH], F32R), sb("x_lo", [DM, CH], F32R), sb("x_rest", [2 * DR, CH], F32R))
        act_g, hid = sb("act_g", [128, 2, CH]), sb("hid", [128, 2, CH])
        hid_hi, hid_lo = sb("hid_hi", [128, 2, NF, CH], F32R), sb("hid_lo", [128, 2, NF, CH], F32R)
        y = sb("y", [TP, 2, 2, D])

        s_wh, s_wl, s_const = sem("wh"), sem("wl"), sem("const")
        s_h, s_hres, s_store = sem("h"), sem("hres"), [sem("store0"), sem("store1")]
        s_zero, s_st, s_mom, s_veps, s_rstd, s_xhat, s_t, s_xhi, s_xlo = (
            sem(n) for n in ("zero", "st", "mom", "veps", "rstd", "xhat", "t", "xhi", "xlo"))
        s_rp, s_lg, s_tanh, s_r, s_cw = sem("rp"), sem("lg"), sem("tanh"), sem("r"), sem("cw")
        s_gu, s_silu, s_hid, s_hh, s_hl, s_dn, s_y = (sem(n) for n in ("gu", "silu", "hid", "hh", "hl", "dn", "y"))

        def has(c):
            return not isinstance(c, int) or 0 <= c < CHUNKS

        def steps(eng, step):
            for c in range(3):
                step(c, c % 2)
            with eng.Fori(1, CHUNKS // 2 - 2) as it:
                for u in range(2):
                    step(2 * it + u + 1, 1 - u)
            for c in range(CHUNKS - 3, CHUNKS + 2):
                step(c, c % 2)

        def hidden_ago(c, u, fi):
            return (c, u, fi - 1) if fi else (c - 1, 1 - u, NF - 1)

        hv = h1.rearrange("b s d -> (b s) d").rearrange("(c t p) d -> c p t d", t=TT, p=TP)
        ov = out.rearrange("b s d -> (b s) d").rearrange("(c t p) d -> c p t d", t=TT, p=TP)
        block = ctx.enter_context(nc.Block())

        units = [(k, m) for k in range(E + 1) for m in range(3)]

        @block.sync
        def _(sp):
            def load(c):
                sp.dma_start(h[:], hv[bass.ds(c, 1)].rearrange("a p t d -> (a p) t d")).then_inc(s_h, 16)

            load(0)
            sp.dma_start(ident[:], ident_in).then_inc(s_const, 16)
            sp.dma_start(router[:], router_rep).then_inc(s_const, 16)
            sp.dma_start(rbias[:], rbias_rep).then_inc(s_const, 16)
            def store(c, t):
                sp.wait_ge(s_y, TT * c + t + 1)
                sp.dma_start(ov[bass.ds(c, 1), :, t, :].rearrange("a p d -> (a p) d"), y[:, t % 2, 1, :]
                             ).then_inc(s_store[t % 2], 16)

            def step(c, u):
                if has(c - 2):
                    store(c - 2, TT - 1)
                if has(c - 1):
                    sp.dma_start(hres[:], hv[bass.ds(c - 1, 1)].rearrange("a p t d -> (a p) t d")).then_inc(s_hres, 16)
                    store(c - 1, 0)
                if has(c + 2):
                    sp.wait_ge(s_xhat, TT * (c + 2))
                    load(c + 2)
                if has(c - 1):
                    for t in range(1, TT - 1):
                        store(c - 1, t)
            step(-1, 1)
            steps(sp, step)
            for b in range(2):
                sp.wait_ge(s_store[b], 16 * CHUNKS * TT // 2)

        @block.gpsimd
        def _(pool):
            pool.memset(half_neg[:], -0.5).then_inc(s_zero, 1)
            pool.memset(eps[:], EPS).then_inc(s_zero, 1)
            pool.wait_ge(s_zero, 2)

            def step(c, u):
                if has(c + 1):
                    pool.wait_ge(s_mom, TT * (c + 2))
                    wait(pool, s_xhat, TT * (c + 1))
                    pool.tensor_tensor(var_eps[:], moments[:, :, 1], eps[:], ALU.add).then_inc(s_veps, 1)
                    pool.wait_ge(s_veps, c + 2)
                    pool.tensor_tensor(rstd[:], var_eps[:], half_neg[:], ALU.pow).then_inc(s_rstd, 1)
            step(-1, 1)
            steps(pool, step)

        @block.scalar
        def _(act):
            for k, m in units:
                c = slice(k * FT, (k + 1) * FT)
                if m < 2:
                    w = (gate, up)[m]
                    act.activation(w.hi[:, c], raw.main[m][:, c], ACT.Copy)
                    act.activation(w.rest2[:, c], raw.rest[m][:, c], ACT.Copy).then_inc(s_wh, 1)
                else:
                    act.activation(down_h[:, 3 * k:3 * k + 3, :], raw.down[:, 3 * k:3 * k + 3, :], ACT.Copy
                                   ).then_inc(s_wh, 1)

            def tokens_hi(c):
                act.wait_ge(s_t, c + 1)
                act.activation(x[0][:], ps_x[:, 0:CH], ACT.Copy).then_inc(s_xhi, 1)
                act.activation(x[2][0:DR, :], ps_xr[0:DR, 0:CH], ACT.Copy).then_inc(s_xhi, 1)

            def probabilities(c):
                act.wait_ge(s_lg, c + 1)
                act.activation(rt[1][:], rt[0][:], ACT.Tanh, scale=0.5).then_inc(s_tanh, 1)

            def step(c, u):
                for fi in range(NF):
                    n = NF * c + fi
                    if has(c):
                        b = fi % 2
                        act.wait_ge(s_gu, n + 1)
                        wait(act, s_hid, n - 1)
                        act.activation(act_g[:, b, :], ps_g[b][:, 0:CH], ACT.Silu).then_inc(s_silu, 1)
                    cl, ul, fl = hidden_ago(c, u, fi)
                    if has(cl):
                        act.wait_ge(s_hid, n)
                        if fl == 0:
                            wait(act, s_dn, TT * (c - 1))
                        act.activation(hid_hi[:, ul, fl, :], hid[:, fl % 2, :], ACT.Copy).then_inc(s_hh, 1)
                    if fi == 10 and has(c + 1):
                        probabilities(c + 1)
                if has(c + 1):
                    tokens_hi(c + 1)
            tokens_hi(0)
            probabilities(0)
            act.wait_ge(s_wl, len(units))
            steps(act, step)

        @block.vector
        def _(dve):
            def weights_lo(n):
                k, m = units[n]
                dve.wait_ge(s_wh, n + 1)
                c = slice(k * FT, (k + 1) * FT)
                if m < 2:
                    w = (gate, up)[m]
                    dve.tensor_tensor(w.lo[:, c], raw.main[m][:, c], f(w.hi[:, c]), ALU.subtract)
                    dve.tensor_tensor(w.rest_lo[:, c], raw.rest[m][0:DR, c], f(w.rest2[0:DR, c]), ALU.subtract
                                      ).then_inc(s_wl, 1)
                else:
                    dve.tensor_tensor(down_l[:, 3 * k:3 * k + 3, :], raw.down[:, 3 * k:3 * k + 3, :],
                                      f(down_h[:, 3 * k:3 * k + 3, :]), ALU.subtract).then_inc(s_wl, 1)

            def statistics(c):
                dve.wait_ge(s_h, 16 * (c + 1))
                wait(dve, s_rstd, c)
                for t in range(TT):
                    dve.bn_stats(stats[:, t, :], h[:, t, :]).then_inc(s_st, 1)

            def aggregate():
                for t in range(TT):
                    dve.bn_aggr(moments[:, t, :], stats[:, t, :]).then_inc(s_mom, 1)

            def normalise(c):
                dve.wait_ge(s_rstd, c + 1)
                wait(dve, s_t, c)
                for t in range(TT):
                    dve.tensor_scalar(xhat[:, t, :], h[:, t, :], moments[:, t, 0:1], rstd[:, t:t + 1],
                                      ALU.subtract, ALU.mult).then_inc(s_xhat, 1)

            def tokens_lo(c):
                dve.wait_ge(s_xhi, 2 * (c + 1))
                dve.tensor_tensor(x[1][:], ps_x[:, 0:CH], f(x[0][:]), ALU.subtract).then_inc(s_xlo, 1)
                dve.tensor_tensor(x[2][DR:, :], ps_xr[0:DR, 0:CH], f(x[2][0:DR, :]), ALU.subtract).then_inc(s_xlo, 1)

            def router_products(c, t):
                dve.wait_ge(s_xhat, TT * c + t + 1)
                wait(dve, s_rp, TT * c + t - 1)
                for e in range(E):
                    last = dve.scalar_tensor_tensor(out=rprod[:, (t % 2) * E + e, :], in0=xhat[:, t, :], scalar=1.0,
                                                    in1=router[:, e, :], op0=ALU.mult, op1=ALU.mult,
                                                    accum_out=rt[5][:, t, e:e + 1])
                last.then_inc(s_rp, 1)

            def router_logits(c):
                dve.wait_ge(s_rp, TT * (c + 1))
                dve.tensor_tensor(rt[0][:], rt[5][:], rbias[:], ALU.add).then_inc(s_lg, 1)

            def chain(op, n):
                op.then_inc(s_r, 1)
                dve.wait_ge(s_r, n)

            R = 11

            def route(c, u):
                r0 = R * c - 1
                dve.wait_ge(s_tanh, c + 1)
                chain(dve.tensor_scalar(rt[2][:], rt[1][:], 0.5, 0.5, ALU.mult, ALU.add), r0 + 2)
                p = [rt[2][:, :, e] for e in range(E)]
                keep = [rt[3][:, :, e] for e in range(E)]
                chain(dve.tensor_tensor(rs[0][:], p[1], p[2], ALU.min), r0 + 3)
                chain(dve.tensor_tensor(keep[0], p[0], rs[0][:], ALU.is_ge), r0 + 4)
                chain(dve.tensor_tensor(rs[1][:], p[0], p[1], ALU.min), r0 + 5)
                chain(dve.tensor_tensor(keep[2], p[2], rs[1][:], ALU.is_gt), r0 + 6)
                chain(dve.tensor_tensor(rs[2][:], keep[0], keep[2], ALU.add), r0 + 7)
                chain(dve.tensor_scalar(keep[1], rs[2][:], -1.0, 2.0, ALU.mult, ALU.add), r0 + 8)
                chain(dve.tensor_tensor(rt[4][:], rt[2][:], rt[3][:], ALU.mult), r0 + 9)
                chain(dve.tensor_reduce(out=rs[0][:], in_=rt[4][:], op=ALU.add, axis=AX_X), r0 + 10)
                chain(dve.reciprocal(rs[1][:], rs[0][:]), r0 + 11)
                chain(dve.tensor_tensor(cw[:, u, :, :], rt[4][:],
                                        rs[1][:].rearrange("p (t a) -> p t a", a=1).to_broadcast([TP, TT, E]),
                                        ALU.mult), r0 + 12)

            def combine(c, u, t):
                n = TT * c + t
                b = t % 2
                dve.wait_ge(s_dn, n + 1)
                dve.wait_ge(s_hres, 16 * (c + 1))
                wait(dve, s_store[b], 16 * (2 * c + t // 2))
                parts = [ps_d[k // 2][0:TP, (k % 2) * D:(k % 2 + 1) * D] for k in range(E + 1)]
                dve.tensor_tensor(y[:, b, 0, :], parts[0], hres[:, t, :], ALU.add).then_inc(s_cw, 1)
                for e in range(E):
                    dve.wait_ge(s_cw, 3 * n + e + 1)
                    last = dve.scalar_tensor_tensor(out=y[:, b, (e + 1) % 2, :], in0=parts[e + 1],
                                                    scalar=cw[:, u, t, e:e + 1], in1=y[:, b, e % 2, :],
                                                    op0=ALU.mult, op1=ALU.add)
                    last.then_inc(s_cw if e < E - 1 else s_y, 1)

            def step(c, u):
                for fi in range(NF):
                    n = NF * c + fi
                    if has(c):
                        b = fi % 2
                        dve.wait_ge(s_silu, n + 1)
                        wait(dve, s_hh, n - 1)
                        wait(dve, s_hl, n - 1)
                        dve.tensor_tensor(hid[:, b, :], act_g[:, b, :], ps_u[b][:, 0:CH], ALU.mult).then_inc(s_hid, 1)
                    if fi == 2 and has(c + 1):
                        dve.wait_ge(s_st, TT * (c + 2))
                    cl, ul, fl = hidden_ago(c, u, fi)
                    if has(cl):
                        dve.wait_ge(s_hh, n)
                        if fl == 0:
                            wait(dve, s_dn, TT * (c - 1))
                        dve.tensor_tensor(hid_lo[:, ul, fl, :], hid[:, fl % 2, :], f(hid_hi[:, ul, fl, :]), ALU.subtract
                                          ).then_inc(s_hl, 1)
                    if fi == 0 and has(c - 2):
                        combine(c - 2, u, TT - 1)
                    if fi in (3, 6, 9) and has(c - 1):
                        combine(c - 1, 1 - u, fi // 3 - 1)
                    if fi == 2:
                        if has(c + 1):
                            aggregate()
                        if has(c):
                            route(c, u)
                    if has(c + 1):
                        if fi == 1:
                            statistics(c + 1)
                        if fi == 4:
                            normalise(c + 1)
                        if fi == 5:
                            router_products(c + 1, 0)
                            router_products(c + 1, 1)
                        if fi == 7:
                            router_products(c + 1, 2)
                        if fi == 8:
                            router_products(c + 1, 3)
                            router_logits(c + 1)
                if has(c + 1):
                    tokens_lo(c + 1)
            for n in range(7):
                weights_lo(n)
            statistics(0)
            dve.wait_ge(s_st, TT)
            aggregate()
            normalise(0)
            for n in range(7, len(units)):
                weights_lo(n)
            tokens_lo(0)
            dve.wait_ge(s_const, 48)
            for t in range(TT):
                router_products(0, t)
            router_logits(0)
            steps(dve, step)

        @block.tensor
        def _(pe):
            pe.wait_ge(s_const, 48)

            def turn(c):
                pe.wait_ge(s_xhat, TT * (c + 1))
                wait(pe, s_xlo, 2 * c)
                for t in range(TT):
                    pe.transpose(ps_x[:, t * TP:(t + 1) * TP], xhat[:, t, 0:DM], ident[0:TP, 0:TP])
                    last = pe.transpose(ps_xr[0:DR, t * TP:(t + 1) * TP], xhat[:, t, DM:D], ident[0:TP, 0:TP])
                last.then_inc(s_t, 1)

            def down(c, u, t):
                pe.wait_ge(s_hl, NF * (c + 1))
                wait(pe, s_y, TT * c + t)
                cols = slice(t * TP, (t + 1) * TP)
                for k in range(E + 1):
                    o = ps_d[k // 2][0:TP, (k % 2) * D:(k % 2 + 1) * D]
                    for fi in range(3 * k, 3 * k + 3):
                        pe.matmul(o, hid_hi[:, u, fi, cols], down_h[:, fi, :], start=(fi == 3 * k), stop=False)
                        pe.matmul(o, hid_lo[:, u, fi, cols], down_h[:, fi, :], start=False, stop=False)
                        last = pe.matmul(o, hid_hi[:, u, fi, cols], down_l[:, fi, :], start=False,
                                         stop=(fi == 3 * k + 2))
                last.then_inc(s_dn, 1)

            def step(c, u):
                for fi in range(NF):
                    if has(c):
                        n = NF * c + fi
                        b = fi % 2
                        if fi == 0:
                            pe.wait_ge(s_xlo, 2 * (c + 1))
                        cols = slice(fi * 128, (fi + 1) * 128)
                        wait(pe, s_hid, n - 1)
                        product(pe, ps_g[b][:, 0:CH], x, gate, slice(0, CH), cols, False)
                        product(pe, ps_u[b][:, 0:CH], x, up, slice(0, CH), cols, False).then_inc(s_gu, 1)
                    if fi == NF - 1 and has(c + 1):
                        turn(c + 1)
                    if fi % 3 == 2 and has(c - 1):
                        down(c - 1, 1 - u, fi // 3)
            turn(0)
            pe.wait_ge(s_wl, len(units))
            steps(pe, step)


def build(nc, a, out):
    h0 = nc.dram_tensor("h0_scratch", [B, NC, D], F32, kind="Internal").ap()
    h1 = nc.dram_tensor("h1_scratch", [B, S, D], F32, kind="Internal").ap()
    raw = ExpertWeights(a)
    with ExitStack() as ctx:
        const = Constants(nc, ctx, a)
        embed_patches(nc, a["xT"], a["w_proj"], a["pos_rep"], a["b_rep"], a["cls_rep"], a["pos0_rep"], h0, const)
        attention(nc, a["txt"], h0, h1, const, raw)
    experts(nc, h1, out, raw, a["router_rep"], a["rbias_rep"], a["ident"])


def layout(inputs):
    import numpy as np

    g = {k: np.asarray(v) for k, v in inputs.items()}
    P = 16
    n = 96 // P
    x = g["x"].reshape(B, n, P, n, P, 3).transpose(0, 1, 3, 2, 4, 5).reshape(B // 2, EMB, KD, 128)
    pos = g["L0_tok_pos_embedding"]
    bqkv = g["L0_attn_bqkv"]
    rows = np.arange(HQ)
    return {
        "xT": x.transpose(0, 3, 2, 1).reshape(B // 2, 128, KD * EMB),
        "w_proj": g["L0_tok_W_proj"],
        "pos_rep": np.concatenate([pos[1:], pos[1:]]),
        "b_rep": np.broadcast_to(g["L0_tok_b_proj"], (EMB, D)),
        "cls_rep": np.broadcast_to(g["L0_tok_cls_token"].reshape(1, D), (B, D)),
        "pos0_rep": np.broadcast_to(pos[0:1], (B, D)),
        "txt": g["txt"],
        "wqkv": g["L0_attn_Wqkv"],
        "bqkv": bqkv,
        "bv_rep": np.broadcast_to(bqkv[2 * D:], (128, D)),
        "wl_rep": np.repeat(g["L0_attn_Wl"], DH, axis=0),
        "bl_rep": np.repeat(g["L0_attn_bl"], QS).reshape(HQ, 1),
        "ww_rep": np.repeat(g["L0_attn_Ww"], QS, axis=0),
        "bw_rep": np.repeat(g["L0_attn_bw"], QS).reshape(1, HQ),
        "wp": g["L0_attn_Wproj"],
        "bp_rep": np.broadcast_to(g["L0_attn_bproj"], (128, D)),
        "ident": np.eye(128, dtype=np.float32),
        "mask": (rows[:, None] % QS == np.arange(QS)[None]).astype(np.float32),
        "sg": g["L0_ffn_shared_gate"], "su": g["L0_ffn_shared_up"], "sd": g["L0_ffn_shared_down"],
        "rg": g["L0_ffn_routed_gate"], "ru": g["L0_ffn_routed_up"], "rd": g["L0_ffn_routed_down"],
        "router_rep": np.broadcast_to(g["L0_ffn_router_w"].T, (TP, E, D)),
        "rbias_rep": np.broadcast_to(g["L0_ffn_routing_bias"], (TP, TT, E)),
    }


def kernel(**inputs):
    import numpy as np
    import concourse.bacc as bacc
    from concourse.bass_utils import run_bass_kernel_spmd

    nc = bacc.Bacc("TRN2", target_bir_lowering=False, num_devices=1)
    arrays, aps = {}, {}
    for name, a in layout(inputs).items():
        arrays["in_" + name] = np.ascontiguousarray(a)
        aps[name] = nc.dram_tensor("in_" + name, a.shape, mybir.dt.from_np(a.dtype), kind="ExternalInput").ap()
    out = nc.dram_tensor("out_0", [B, S, D], F32, kind="ExternalOutput").ap()
    build(nc, aps, out)
    r = run_bass_kernel_spmd(nc, [arrays], core_ids=[0])
    return r.results[0]["out_0"]
```
